# Optimizing a Trainium2 kernel written in Bass

```python
import numpy as np
import jax
import jax.numpy as jnp

def _softmax(x, axis=-1):
    return jax.nn.softmax(x, axis=axis)

def _gelu(x):
    return jax.nn.gelu(x, approximate=True)

def _silu(x):
    return jax.nn.silu(x)

def _sigmoid(x):
    return jax.nn.sigmoid(x)

def _layernorm(x, axis=-1, eps=1e-05):
    m = jnp.mean(x, axis=axis, keepdims=True)
    v = jnp.var(x, axis=axis, keepdims=True)
    return (x - m) / jnp.sqrt(v + eps)

def _scatter_add(tgt, idx, src, axis=0):
    return tgt.at[idx].add(src)

def _segment_sum(src, seg, n):
    return jax.ops.segment_sum(src, seg, n)
kernel_name = 'mk_decoder_postln_d1_seqx_r4_b8bfa3'

def setup_inputs(seed: int=0):
    np.random.seed(seed)
    _w = jnp.asarray

    def _rec_inputs():
        import jax
        import jax.numpy as jnp
        _rk = jax.random.key(seed)
        x = 7.22e-05 + 1 * jax.random.normal(jax.random.fold_in(_rk, 1), (4, 512, 256), jnp.float32)
        _lenS = 512 - jax.random.randint(jax.random.fold_in(_rk, 7), (4,), 0, max(1, 512 // 4) + 1, jnp.int32)
        _lenS2 = 512 - jax.random.randint(jax.random.fold_in(_rk, 8), (4,), 0, max(1, 512 // 4) + 1, jnp.int32)
        _ctx_1024P = jax.random.normal(jax.random.fold_in(_rk, 11), (4, 16, 256), jnp.float32)
        _ctx_1024c = jax.random.dirichlet(jax.random.fold_in(_rk, 511), 0.3 * jnp.ones((16,), jnp.float32), (4, 512))
        _ctx_1024t = jnp.einsum('bsk,bkd->bsd', _ctx_1024c, _ctx_1024P)
        _ctx_1024t = _ctx_1024t * jax.lax.rsqrt(jnp.mean(jnp.square(_ctx_1024t)) + 1e-12) * 0.953939
        ctx_1024 = -0.000514642 + 1.00011 * (_ctx_1024t + 0.3 * jax.random.normal(jax.random.fold_in(_rk, 611), (4, 512, 256), jnp.float32))
        return (x, ctx_1024)
    x, ctx_1024 = _rec_inputs()

    def _L0_attn_setup():
        import jax, jax.numpy as jnp
        import numpy as np
        D_MODEL = 256
        NUM_HEADS = 16
        HEAD_DIM = D_MODEL // NUM_HEADS
        key = jax.random.key(seed)
        ks = jax.random.split(key, 5)
        B, S = (1, 1024)
        scale = 0.02
        return {'x': jax.random.normal(ks[0], (B, S, D_MODEL), dtype=jnp.float32), 'w_q': jax.random.normal(ks[1], (D_MODEL, D_MODEL), dtype=jnp.float32) * scale, 'w_k': jax.random.normal(ks[2], (D_MODEL, D_MODEL), dtype=jnp.float32) * scale, 'w_v': jax.random.normal(ks[3], (D_MODEL, D_MODEL), dtype=jnp.float32) * scale, 'w_o': jax.random.normal(ks[4], (D_MODEL, D_MODEL), dtype=jnp.float32) * scale}
    _L0_attn_all = _L0_attn_setup()
    _L0_attn_in = {k: v for k, v in _L0_attn_all.items() if k in ('w_q', 'w_k', 'w_v', 'w_o')}
    del _L0_attn_all

    def _L0_xattn_setup():
        import jax, jax.numpy as jnp
        import numpy as np
        B, L_ENC, L_DEC, D = (16, 128, 128, 256)
        key = jax.random.key(seed)
        k1, k2, k3, k4, k5, k6 = jax.random.split(key, 6)
        encoder_hc = jax.random.normal(k1, (B, L_ENC, D), dtype=jnp.float32)
        decoder_hq = jax.random.normal(k2, (B, L_DEC, D), dtype=jnp.float32)
        w_sim = jax.random.normal(k3, (3 * D,), dtype=jnp.float32) * 0.02
        b_sim = jax.random.normal(k4, (1,), dtype=jnp.float32) * 0.02
        W_qv = jax.random.normal(k5, (4 * D, D), dtype=jnp.float32) * 0.02
        b_qv = jax.random.normal(k6, (D,), dtype=jnp.float32) * 0.02
        return {'encoder_hc': encoder_hc, 'decoder_hq': decoder_hq, 'w_sim': w_sim, 'b_sim': b_sim, 'W_qv': W_qv, 'b_qv': b_qv}
    _L0_xattn_all = _L0_xattn_setup()
    _L0_xattn_in = {k: v for k, v in _L0_xattn_all.items() if k in ('w_sim', 'b_sim', 'W_qv', 'b_qv')}
    del _L0_xattn_all

    def _L0_ffn_setup():
        import jax, jax.numpy as jnp
        import numpy as np
        NUM_EXPERTS = 160
        TOP_K = 8
        ROUTED_SCALE = 2.5
        HIDDEN = 256
        INTER = 128
        key = jax.random.key(seed)
        ks = jax.random.split(key, 7)
        B, S = (1, 512)
        return {'hidden_states': jax.random.normal(ks[0], (B, S, HIDDEN), dtype=jnp.float32), 'router_w': jax.random.normal(ks[1], (NUM_EXPERTS, HIDDEN), dtype=jnp.float32) * 0.02, 'expert_bias': jnp.zeros((NUM_EXPERTS,), dtype=jnp.float32), 'w_gate': jax.random.normal(ks[2], (NUM_EXPERTS, INTER, HIDDEN), dtype=jnp.float32) * 0.02, 'w_down': jax.random.normal(ks[3], (NUM_EXPERTS, HIDDEN, INTER), dtype=jnp.float32) * 0.02, 'w_gate_shared': jax.random.normal(ks[4], (INTER, HIDDEN), dtype=jnp.float32) * 0.02, 'w_down_shared': jax.random.normal(ks[5], (HIDDEN, INTER), dtype=jnp.float32) * 0.02}
    _L0_ffn_all = _L0_ffn_setup()
    _L0_ffn_in = {k: v for k, v in _L0_ffn_all.items() if k in ('router_w', 'expert_bias', 'w_gate', 'w_down', 'w_gate_shared', 'w_down_shared')}
    del _L0_ffn_all
    return {'x': x, 'ctx_1024': ctx_1024, 'L0_attn_w_q': _L0_attn_in['w_q'], 'L0_attn_w_k': _L0_attn_in['w_k'], 'L0_attn_w_v': _L0_attn_in['w_v'], 'L0_attn_w_o': _L0_attn_in['w_o'], 'L0_xattn_w_sim': _L0_xattn_in['w_sim'], 'L0_xattn_b_sim': _L0_xattn_in['b_sim'], 'L0_xattn_W_qv': _L0_xattn_in['W_qv'], 'L0_xattn_b_qv': _L0_xattn_in['b_qv'], 'L0_ffn_router_w': _L0_ffn_in['router_w'], 'L0_ffn_expert_bias': _L0_ffn_in['expert_bias'], 'L0_ffn_w_gate': _L0_ffn_in['w_gate'], 'L0_ffn_w_down': _L0_ffn_in['w_down'], 'L0_ffn_w_gate_shared': _L0_ffn_in['w_gate_shared'], 'L0_ffn_w_down_shared': _L0_ffn_in['w_down_shared']}

def reference(x, ctx_1024, L0_attn_w_q, L0_attn_w_k, L0_attn_w_v, L0_attn_w_o, L0_xattn_w_sim, L0_xattn_b_sim, L0_xattn_W_qv, L0_xattn_b_qv, L0_ffn_router_w, L0_ffn_expert_bias, L0_ffn_w_gate, L0_ffn_w_down, L0_ffn_w_gate_shared, L0_ffn_w_down_shared):
    import jax
    import jax.numpy as jnp

    def _L0_attn_ref(x, w_q, w_k, w_v, w_o):
        import jax, jax.numpy as jnp
        import numpy as np
        D_MODEL = 256
        NUM_HEADS = 16
        HEAD_DIM = D_MODEL // NUM_HEADS
        B, S, _ = x.shape
        q = x @ w_q.T
        k = x @ w_k.T
        v = x @ w_v.T
        q = q.reshape(B, S, NUM_HEADS, HEAD_DIM)
        k = k.reshape(B, S, NUM_HEADS, HEAD_DIM)
        v = v.reshape(B, S, NUM_HEADS, HEAD_DIM)
        scale = HEAD_DIM ** (-0.5)
        scores = jnp.einsum('bqhd,bkhd->bhqk', q, k) * scale
        weights = jax.nn.softmax(scores, axis=-1)
        out = jnp.einsum('bhqk,bkhd->bqhd', weights, v)
        concat = out.reshape(B, S, D_MODEL)
        return concat @ w_o.T

    def _L0_xattn_ref(encoder_hc, decoder_hq, w_sim, b_sim, W_qv, b_qv):
        import jax, jax.numpy as jnp
        import numpy as np
        B, L_ENC, L_DEC, D = (16, 128, 128, 256)
        d = encoder_hc.shape[-1]
        w1, w2, w3 = (w_sim[:d], w_sim[d:2 * d], w_sim[2 * d:])
        Sim = (encoder_hc @ w1)[:, :, None] + (decoder_hq @ w2)[:, None, :] + jnp.einsum('bid,bjd->bij', encoder_hc * w3, decoder_hq) + b_sim[0]
        A = jax.nn.softmax(Sim, axis=2)
        hq_hat = jnp.einsum('bij,bjd->bid', A, decoder_hq)
        Batt = jax.nn.softmax(jnp.max(Sim, axis=2), axis=1)
        hc_bar = jnp.einsum('bi,bid->bd', Batt, encoder_hc)[:, None, :]
        hc_hat = jnp.broadcast_to(hc_bar, encoder_hc.shape)
        feats = jnp.concatenate([encoder_hc, hq_hat, encoder_hc * hq_hat, encoder_hc * hc_hat], axis=-1)
        hcq = feats @ W_qv + b_qv
        return hcq

    def _L0_ffn_ref(hidden_states, router_w, expert_bias, w_gate, w_down, w_gate_shared, w_down_shared):
        import jax, jax.numpy as jnp
        import numpy as np
        NUM_EXPERTS = 160
        TOP_K = 8
        ROUTED_SCALE = 2.5
        HIDDEN = 256
        INTER = 128
        B, S, H = hidden_states.shape
        x = hidden_states.reshape(-1, H)
        T = x.shape[0]
        logits = x @ router_w.T + expert_bias[None, :]
        probs = jax.nn.sigmoid(logits)
        top_w, top_idx = jax.lax.top_k(probs, TOP_K)
        top_w = top_w / (jnp.sum(top_w, axis=-1, keepdims=True) + 1e-09)
        top_w = top_w * ROUTED_SCALE
        combine = jnp.zeros((T, NUM_EXPERTS), dtype=x.dtype)
        combine = combine.at[jnp.arange(T)[:, None], top_idx].set(top_w)
        h1 = jax.nn.silu(jnp.einsum('th,eih->eti', x, w_gate))
        h1w = h1 * combine.T[:, :, None]
        routed = jnp.einsum('eti,ehi->th', h1w, w_down)
        shared = jax.nn.silu(x @ w_gate_shared.T) @ w_down_shared.T
        return (routed + shared).reshape(B, S, H)
    x = _layernorm(x + _L0_attn_ref(x, L0_attn_w_q, L0_attn_w_k, L0_attn_w_v, L0_attn_w_o), axis=-1)
    x = _layernorm(x + _L0_xattn_ref(x, ctx_1024, L0_xattn_w_sim, L0_xattn_b_sim, L0_xattn_W_qv, L0_xattn_b_qv), axis=-1)
    x = _layernorm(x + _L0_ffn_ref(x, L0_ffn_router_w, L0_ffn_expert_bias, L0_ffn_w_gate, L0_ffn_w_down, L0_ffn_w_gate_shared, L0_ffn_w_down_shared), axis=-1)
    return x

_drawn_inputs = setup_inputs


def setup_inputs(seed=0):
    import zlib

    import numpy as np

    out = dict(_drawn_inputs(seed))
    spreads = {'L0_ffn_expert_bias': (0.0, 0.335)}
    factors = {'L0_attn_w_q': 8.0,
     'L0_attn_w_k': 8.0,
     'L0_attn_w_v': 8.0,
     'L0_attn_w_o': 8.0,
     'L0_xattn_b_qv': 2.835}
    for name, (base, spread) in spreads.items():
        noise = np.random.default_rng([zlib.crc32(name.encode()), seed]).standard_normal(out[name].shape)
        drawn = base * np.exp(spread * noise) if base else spread * noise
        out[name] = jnp.asarray(drawn.astype(out[name].dtype))
    for name, factor in factors.items():
        out[name] = (out[name] * factor).astype(out[name].dtype)
    return out
```

```python
from contextlib import ExitStack

import concourse.bass as bass
from concourse import mybir

F32 = mybir.dt.float32
F32R = mybir.dt.float32r
BF16 = mybir.dt.bfloat16
I32 = mybir.dt.int32
U32 = mybir.dt.uint32
ALU = mybir.AluOpType
ACT = mybir.ActivationFunctionType
AX = mybir.AxisListType.X

P = 128
B, S, D = 4, 512, 256
DC = D // P
TT = S // P
HEADS, DH = 16, 16
HG = 4
NG = HEADS // HG
STEPS = B * NG
EXPERTS, TOP_K, INTER = 160, 8, 128
SLOTS = TOP_K + 1
TOKENS = B * S
TILES = TOKENS // P
ROUTED_SCALE = 2.5
PAGES = (TOKENS * TOP_K + EXPERTS * (P - 1)) // P
POOL_PAGES = -(-PAGES // 4) * 4
STEPS_E = POOL_PAGES + TILES
W_COL, DST_COL = D, D + 1
ROW = D + 4
FILL_PAGES = 6
FILLS = POOL_PAGES // FILL_PAGES
NOWHERE = 1 << 20
FAR = float(1 << 17)
LN_EPS = 1e-5


def repeated(ap, at, count):
    shape = list(ap.shape)
    return ap.unsqueeze(at).broadcast_to(shape[:at] + [count] + shape[at:])


def project(nc, xt, wq, wk, wv, fill, qd, kd, vd):
    with ExitStack() as ctx:
        sb = lambda n, s, d=F32: ctx.enter_context(nc.sbuf_tensor(n, s, d))
        sem = lambda n: ctx.enter_context(nc.semaphore(n))
        xT = sb("p_xT", [P, B, DC, S])
        Wq, Wk, Wv = sb("p_wq", [P, DC, D]), sb("p_wk", [P, DC, D]), sb("p_wv", [P, DC, D])
        hi, lo = sb("p_hi", [P, 2, 4, S], F32R), sb("p_lo", [P, 2, 4, S], F32R)
        V = sb("p_v", [P, 2, TT, HEADS, 2 * DH])
        ps = ctx.enter_context(nc.psum_tensor("p_ps", [P, 8, S], F32))
        x_in = [sem(f"p_x_in{b}") for b in range(B)]
        w_in, v_ones, fill_zero = sem("p_w_in"), sem("p_v_ones"), sem("p_fill_zero")
        qk_made, v_made = sem("p_qk_made"), sem("p_v_made")
        hi_done, lo_done, v_done = sem("p_hi_done"), sem("p_lo_done"), sem("p_v_done")
        stored = [sem(f"p_stored{u}") for u in range(2)]
        STORES = 8 + 1
        block = ctx.enter_context(nc.Block())

        @block.sync
        def _(sp):
            sp.dma_start(Wq[:], wq).then_inc(w_in, 16)
            sp.dma_start(xT[:, 0], xt[0]).then_inc(x_in[0], 16)
            sp.dma_start(Wk[:], wk).then_inc(w_in, 16)
            sp.dma_start(Wv[:], wv).then_inc(w_in, 16)
            for b in range(1, B):
                sp.dma_start(xT[:, b], xt[b]).then_inc(x_in[b], 16)
            for b in range(B):
                u = b % 2
                sp.wait_ge(lo_done, 4 * (b + 1))
                for part, src in enumerate((hi, lo)):
                    for half in range(2):
                        for w, dst in enumerate((qd, kd)):
                            to = dst[:, part].rearrange("(b j g) e h q -> b g (e h) j q", b=B, g=2)[b, half]
                            rows = slice(P // 2 * half, P // 2 * (half + 1))
                            sp.dma_start(to, src[rows, u, 2 * w:2 * w + 2].bitcast(F32)).then_inc(stored[u], 16)
                sp.wait_ge(v_done, TT * (b + 1))
                sp.dma_start(vd.rearrange("(b g) p t e -> b p t g e", b=B)[b],
                             V[:, u].rearrange("p t (g h) e -> p t g (h e)", g=NG)).then_inc(stored[u], 16)
            for u in range(2):
                sp.wait_ge(stored[u], 16 * STORES * (B // 2))

        @block.gpsimd
        def _(pool_eng):
            nc.gpsimd.memset(V[:], 1.0).then_inc(v_ones, 1)
            nc.gpsimd.memset(fill[:], 0.0).then_inc(fill_zero, 1)
            pool_eng.wait_ge(fill_zero, 1)
            nc.gpsimd.memset(fill[:, DST_COL:DST_COL + 1].bitcast(I32), NOWHERE).then_inc(fill_zero, 1)
            pool_eng.wait_ge(fill_zero, 2)

        @block.tensor
        def _(pe):
            for b in range(B):
                pe.wait_ge(x_in[b], 16)
                if b == 0:
                    pe.wait_ge(w_in, 48)
                for n, (W, j) in enumerate(((Wq, 0), (Wq, 1), (Wk, 0), (Wk, 1))):
                    if b >= 1:
                        pe.wait_ge(lo_done, 4 * (b - 1) + n + 1)
                    for c in range(DC):
                        last = nc.tensor.matmul(ps[:, n], W[:, c, j * P:(j + 1) * P], xT[:, b, c],
                                                start=c == 0, stop=c == DC - 1)
                    last.then_inc(qk_made, 1)
                for t in range(TT):
                    if b >= 1:
                        pe.wait_ge(v_done, TT * (b - 1) + t + 1)
                    for c in range(DC):
                        last = nc.tensor.matmul(ps[:, 4 + t, 0:D], xT[:, b, c, t * P:(t + 1) * P], Wv[:, c],
                                                start=c == 0, stop=c == DC - 1)
                    last.then_inc(v_made, 1)

        @block.scalar
        def _(act):
            act.wait_ge(v_ones, 1)
            for b in range(B):
                u = b % 2
                if b >= 2:
                    act.wait_ge(stored[u], 16 * STORES * (b // 2))
                for n in range(4):
                    act.wait_ge(qk_made, 4 * b + n + 1)
                    nc.scalar.activation(hi[:, u, n], ps[:, n], ACT.Copy).then_inc(hi_done, 1)
                for t in range(TT):
                    act.wait_ge(v_made, TT * b + t + 1)
                    nc.scalar.activation(V[:, u, t, :, 0:DH],
                                         ps[:, 4 + t, 0:D].rearrange("p (h e) -> p h e", h=HEADS),
                                         ACT.Copy).then_inc(v_done, 1)

        @block.vector
        def _(dve):
            for b in range(B):
                u = b % 2
                if b >= 2:
                    dve.wait_ge(stored[u], 16 * STORES * (b // 2))
                for n in range(4):
                    dve.wait_ge(hi_done, 4 * b + n + 1)
                    nc.vector.tensor_tensor(lo[:, u, n], ps[:, n], hi[:, u, n].bitcast(F32),
                                            ALU.subtract).then_inc(lo_done, 1)


class At:

    def __init__(self, i, k, ring):
        self.i, self.k, self.ring = i, k, ring
        self.n = i * ring + k
        self.slot = k % ring
        self.fixed = isinstance(i, int)

    def back(self, by):
        return At(self.i, self.k - by, self.ring)

    def uses(self):
        return self.i + (self.k // self.ring + 1)

    def within(self, count):
        return not self.fixed or 0 <= self.n < count

    def first(self, count=1):
        return self.fixed and self.n < count


def run_steps(eng, step, ring, first, rounds, last):
    for n in range(first):
        step(At(0, n, ring))
    with eng.Fori(0, rounds) as i:
        for k in range(first, first + ring):
            step(At(i, k, ring))
    for n in range(first + rounds * ring, last):
        step(At(0, n, ring))


def attend(nc, sel, kaux, qd, kd, vd, od, fill, pool, pool_filled):
    RING = 4
    KP = 4 * DH
    KR = 96
    NE = 8
    TILE_PAIRS = TT * HG // 2
    with ExitStack() as ctx:
        sb = lambda n, s, d=F32: ctx.enter_context(nc.sbuf_tensor(n, s, d))
        sem = lambda n: ctx.enter_context(nc.semaphore(n))
        Q, K = sb("a_q", [P, RING, HG, S], F32R), sb("a_k", [P, RING, HG, S], F32R)
        V = sb("a_v", [P, RING, TT, HG * 2 * DH])
        aux, zero = sb("a_aux", [KR - KP, HG, S]), sb("a_zero", [HG, HG, S])
        mrow = sb("a_mrow", [HG, RING, S])
        mx = sb("a_mx", [P, RING, TT, HG])
        ident, Sel = sb("a_ident", [P, P]), sb("a_sel", [P, P])
        E = sb("a_e", [P, NE, S])
        O, On, inv = sb("a_o", [P, S]), sb("a_on", [P, S]), sb("a_inv", [P, S])
        psS = ctx.enter_context(nc.psum_tensor("a_psS", [P, 2, 2, S], F32))
        psT = ctx.enter_context(nc.psum_tensor("a_psT", [P, 2, S], F32))
        psO = ctx.enter_context(nc.psum_tensor("a_psO", [P, S], F32))
        psM = ctx.enter_context(nc.psum_tensor("a_psM", [P, S], F32))
        const_in, aux_zero, aux_set = sem("a_const_in"), sem("a_aux_zero"), sem("a_aux_set")
        group_in = [sem(f"a_group_in{r}") for r in range(RING)]
        max_in = [sem(f"a_max_in{r}") for r in range(RING)]
        scored, maxed, turned, negated = sem("a_scored"), sem("a_maxed"), sem("a_turned"), sem("a_negated")
        rescored, expd, weighed = sem("a_rescored"), sem("a_expd"), sem("a_weighed")
        o_copied, summed, divided, stored = sem("a_o_copied"), sem("a_summed"), sem("a_divided"), sem("a_stored")
        inverted = sem("a_inverted")
        LOADS = 7
        run = lambda eng, step: run_steps(eng, step, RING, 3, (STEPS - RING) // RING, STEPS + 3)
        block = ctx.enter_context(nc.Block())

        @block.sync
        def _(sp):
            sp.dma_start(aux[:], kaux).then_inc(const_in, 16)
            sp.dma_start(Sel[:], sel[0]).then_inc(const_in, 16)
            sp.dma_start(ident[:], sel[1]).then_inc(const_in, 16)
            sp.wait_ge(aux_zero, 2)

            def load(at):
                if not at.first(RING):
                    sp.wait_ge(weighed, TT * (at.n - (RING - 1)))
                rows = lambda a, s0, s1: a[bass.ds(at.n, 1), s0:s1].rearrange("a s e h q -> (a s e) h q")
                Qf, Kf, here = Q[:, at.slot].bitcast(F32), K[:, at.slot].bitcast(F32), group_in[at.slot]
                sp.dma_start(Qf[0:2 * DH], rows(qd, 0, 2)).then_inc(here, 16)
                sp.dma_start(Qf[2 * DH:3 * DH], rows(qd, 1, 2)).then_inc(here, 16)
                sp.dma_start(Qf[3 * DH:KP], rows(qd, 0, 1)).then_inc(here, 16)
                sp.dma_start(Kf[0:2 * DH], rows(kd, 0, 2)).then_inc(here, 16)
                sp.dma_start(Kf[2 * DH:KP], rows(kd, 0, 2)).then_inc(here, 16)
                sp.dma_start(Qf[KP:KP + HG], zero[:]).then_inc(here, 16)
                sp.dma_start(V[:, at.slot], vd[bass.ds(at.n, 1)].rearrange("a p t e -> (a p) t e")).then_inc(here, 16)

            load(At(0, 0, RING))

            def step(at):
                if at.back(-1).within(STEPS):
                    load(at.back(-1))
                if at.within(STEPS):
                    for i in range(FILLS // STEPS):
                        row = (at.n * (FILLS // STEPS) + i) * (FILL_PAGES * P)
                        sp.dma_start(pool[bass.ds(row, FILL_PAGES * P)].rearrange("(k p) r -> p k r", p=P),
                                     repeated(fill[:], 1, FILL_PAGES)).then_inc(pool_filled, 16)
                if at.back(1).within(STEPS):
                    sp.wait_ge(negated, at.n)
                    slot = at.back(1).slot
                    sp.dma_start(Q[KP:KP + HG, slot].bitcast(F32),
                                 repeated(mrow[:, slot], 1, HG)).then_inc(max_in[slot], 16)
                if at.back(3).within(STEPS):
                    sp.wait_ge(divided, at.n - 2)
                    sp.dma_start(od[bass.ds(at.n - 3, 1)].rearrange("a p q -> (a p) q"), On[:]).then_inc(stored, 16)
            run(sp, step)
            sp.wait_ge(stored, 16 * STEPS)

        @block.gpsimd
        def _(pool):
            nc.gpsimd.memset(Q[KP:KR].bitcast(F32), 0.0).then_inc(aux_zero, 1)
            nc.gpsimd.memset(zero[:], 0.0).then_inc(aux_zero, 1)

        @block.tensor
        def _(pe):
            pe.wait_ge(const_in, 48)
            pe.wait_ge(aux_set, RING)
            pe.wait_ge(aux_zero, 2)

            def score_tile(at, qt):
                for pair in range(2):
                    i = 2 * qt + pair
                    if not (at.first() and i < 2):
                        pe.wait_ge(maxed, at.n * TILE_PAIRS + (i - 1))
                    for h in range(2):
                        hh = 2 * pair + h
                        last = nc.tensor.matmul(psS[:, pair, h], Q[0:KR, at.slot, hh, qt * P:(qt + 1) * P],
                                                K[0:KR, at.slot, hh], start=True, stop=True)
                    last.then_inc(scored, 1)

            def turn_maxima(at):
                pe.wait_ge(maxed, TILE_PAIRS * (at.n + 1))
                if not at.first(2):
                    pe.wait_ge(divided, at.n - 1)
                for qt in range(TT):
                    last = nc.tensor.transpose(psM[0:HG, qt * P:(qt + 1) * P], mx[:, at.slot, qt], ident[:])
                last.then_inc(turned, 1)

            def rescore(at, kt):
                for hh in range(HG):
                    i = kt * HG + hh
                    if not (at.first() and i < 2):
                        pe.wait_ge(expd, at.n * (TT * HG) + (i - 1))
                    nc.tensor.matmul(psT[:, i % 2], K[0:KR, at.slot, hh, kt * P:(kt + 1) * P],
                                     Q[0:KR, at.slot, hh], start=True, stop=True).then_inc(rescored, 1)

            def weigh(at, kt):
                pe.wait_ge(expd, at.n * (TT * HG) + HG * (kt + 1))
                if kt == 0 and not at.first():
                    pe.wait_ge(o_copied, at.n)
                for hh in range(HG):
                    rows = slice(2 * DH * hh, 2 * DH * (hh + 1))
                    last = nc.tensor.matmul(psO[rows], V[:, at.slot, kt, rows], E[:, (kt * HG + hh) % NE],
                                            start=kt == 0, stop=kt == TT - 1)
                last.then_inc(weighed, 1)

            def step(at):
                scoring, f = at.within(STEPS), at.back(2)
                finishing = f.within(STEPS)
                if scoring:
                    pe.wait_ge(group_in[at.slot], 16 * LOADS * at.uses())
                if finishing:
                    pe.wait_ge(max_in[f.slot], 16 * f.uses())
                    rescore(f, 0)
                for kt in range(TT):
                    if scoring:
                        score_tile(at, kt)
                    if finishing:
                        if kt + 1 < TT:
                            rescore(f, kt + 1)
                        weigh(f, kt)
                    if kt == 0 and at.back(1).within(STEPS):
                        turn_maxima(at.back(1))
                if finishing:
                    pe.wait_ge(o_copied, at.n - 1)
                    if at.back(1).within(STEPS):
                        pe.wait_ge(negated, at.n)
                    nc.tensor.matmul(psM[:], Sel[:], O[:], start=True, stop=True).then_inc(summed, 1)
            run(pe, step)

        @block.scalar
        def _(act):
            act.wait_ge(const_in, 48)
            for r in range(RING):
                nc.scalar.activation(K[KP:KR, r], aux[:], ACT.Copy).then_inc(aux_set, 1)

            def negate(at):
                act.wait_ge(turned, at.n + 1)
                nc.scalar.activation(mrow[:, at.slot], psM[0:HG], ACT.Copy, scale=-1.0).then_inc(negated, 1)

            def step(at):
                turning, f = at.back(1).within(STEPS), at.back(2)
                finishing = f.within(STEPS)
                if turning and not finishing:
                    negate(at.back(1))
                if finishing:
                    for i in range(TT * HG):
                        act.wait_ge(rescored, f.n * (TT * HG) + (i + 1))
                        if not (f.first() and i < NE):
                            act.wait_ge(weighed, f.n * TT + ((i - NE) // HG + 1))
                        nc.scalar.activation(E[:, i % NE], psT[:, i % 2], ACT.Exp, scale=DH ** -0.5).then_inc(expd, 1)
                        if turning and i == NE:
                            negate(at.back(1))
                    act.wait_ge(weighed, TT * (at.n - 1))
                    if not f.first():
                        act.wait_ge(divided, f.n)
                    nc.scalar.activation(O[:], psO[:], ACT.Copy).then_inc(o_copied, 1)
            run(act, step)

        @block.vector
        def _(dve):
            def step(at):
                if at.within(STEPS):
                    for i in range(TILE_PAIRS):
                        qt, pair = divmod(i, 2)
                        dve.wait_ge(scored, at.n * TILE_PAIRS + (i + 1))
                        nc.vector.tensor_reduce(mx[:, at.slot, qt, 2 * pair:2 * pair + 2], psS[:, pair], AX,
                                                ALU.max).then_inc(maxed, 1)
                f = at.back(2)
                if f.within(STEPS):
                    dve.wait_ge(summed, at.n - 1)
                    if not f.first():
                        dve.wait_ge(stored, 16 * f.n)
                    nc.vector.reciprocal(inv[:], psM[:]).then_inc(inverted, 1)
                    dve.wait_ge(inverted, at.n - 1)
                    nc.vector.tensor_tensor(On[:], O[:], inv[:], ALU.mult).then_inc(divided, 1)
            run(dve, step)


class Order:

    def __init__(self, eng, sem, base, per):
        self.eng, self.sem, self.base, self.per, self.n = eng, sem, base, per, 0

    def do(self, ins):
        self.n += 1
        ins.then_inc(self.sem, 1)

    def sync(self, but=0):
        self.eng.wait_ge(self.sem, self.base + (self.n - but))

    def hold(self):
        self.sync()
        self.n += 1
        self.eng.sem_inc(self.sem, 1)

    def close(self):
        assert self.n == self.per, f"{self.n} instructions in order, not {self.per}"


LN_ORDERED = 2 * TT + 1 + 4 + 3 * 3 + TT
MAGIC = float(0x5F3759DF)


def layernorm(nc, o, h, out, st, mv, v, y, t, tiles=TT):
    for i in range(tiles):
        o.do(nc.vector.bn_stats(st[:, i], h[:, i]))
    o.hold()
    for i in range(tiles):
        o.do(nc.vector.bn_aggr(mv[:, i], st[:, i]))
    o.sync()
    o.do(nc.vector.tensor_scalar(v[:, 0], mv[:, :, 1], LN_EPS, None, ALU.add))
    o.sync()
    o.do(nc.vector.tensor_scalar(y.bitcast(I32), v[:, 0].bitcast(I32), 1, None, ALU.arith_shift_right))
    o.do(nc.vector.tensor_scalar(v[:, 1], v[:, 0], -0.5, None, ALU.mult))
    o.sync()
    o.do(nc.vector.tensor_scalar(y.bitcast(I32), y.bitcast(I32), -1.0, MAGIC, ALU.mult, ALU.add))
    o.sync()
    for _ in range(3):
        o.do(nc.vector.tensor_tensor(t, y, y, ALU.mult))
        o.sync()
        o.do(nc.vector.tensor_tensor(t, t, v[:, 1], ALU.mult))
        o.sync()
        o.do(nc.vector.scalar_tensor_tensor(y, t, 1.5, y, ALU.add, ALU.mult))
        o.sync()
    for i in range(tiles):
        o.do(nc.vector.tensor_scalar(out[:, i], h[:, i], mv[:, i, 0:1], y[:, i:i + 1], ALU.subtract, ALU.mult))


CONSTS = {"ident": P, "below": P, "expert": EXPERTS, "page": 3, "page_expert": 3, "slot": SLOTS * TT}
COL = {}
MIX_ORDERED = 167
for _name, _n in CONSTS.items():
    COL[_name] = slice(sum(CONSTS[k] for k in COL), sum(CONSTS[k] for k in COL) + _n)
N_CONST = sum(CONSTS.values())


def mix(nc, consts, wo, wqv, wr, cols, rowsb, x, ctx_t, ctx_r, od, pool, pool_filled, x2d, pages_d):
    with ExitStack() as ctx:
        sb = lambda n, s, d=F32: ctx.enter_context(nc.sbuf_tensor(n, s, d))
        sem = lambda n: ctx.enter_context(nc.semaphore(n))
        C = sb("m_c", [P, N_CONST])
        Wo, Wqv, Wr = sb("m_wo", [P, NG, D]), sb("m_wqv", [P, 4 * DC, D]), sb("m_wr", [P, DC, EXPERTS])
        Cols = sb("m_cols", [P, DC * 2 + 1])
        Rb = sb("m_rowsb", [P, 2 * D + EXPERTS])
        ones, below = sb("m_ones", [P, P], BF16), sb("m_below", [P, P], BF16)
        ones32, ones_row = sb("m_ones32", [P, P]), sb("m_ones640", [P, TT * EXPERTS])
        O, X = sb("m_o", [P, NG, S]), sb("m_x", [P, TT, D])
        CT, CR = sb("m_ct", [P, DC, S]), sb("m_cr", [P, TT, D])
        H, X1, X1b, X2 = (sb(f"m_{n}", [P, TT, D]) for n in ("h", "x1", "x1b", "x2"))
        X1T, ET, HQ, PR, X2T = (sb(f"m_{n}", [P, DC, S]) for n in ("x1t", "et", "hq", "pr", "x2t"))
        A, AT = sb("m_a", [P, TT, S]), sb("m_at", [P, TT, S])
        W1 = sb("m_w1", [P, DC, D])
        st, mv, v = sb("m_st", [P, TT, 6]), sb("m_mv", [P, TT, 2]), sb("m_v", [P, 2, TT])
        y, t4 = sb("m_y", [P, TT]), sb("m_t4", [P, TT])
        dots, nmax, rsum, rinv = (sb(f"m_{n}", [P, TT]) for n in ("dots", "nmax", "rsum", "rinv"))
        u, um, g, ng, eb = sb("m_u", [P, TT]), sb("m_um", [P, 1]), sb("m_g", [1, 1]), sb("m_ng", [P, 1]), sb("m_eb", [P, TT])
        esum, einv, hc = sb("m_esum", [P, 1]), sb("m_einv", [P, 1]), sb("m_hc", [P, DC])
        junk = sb("m_junk", [P, TT, EXPERTS])
        rt = lambda n, d=F32: sb(f"m_{n}", [P, TT, EXPERTS], d)
        lg, pr, rep, need, q, keep, nq, late, key = (rt(n) for n in ("lg", "prob", "rep", "need", "q", "keep", "nq", "late", "key"))
        mask, ri, ni = rt("mask", BF16), rt("ri", I32), rt("ni", I32)
        top, k8, w8 = (sb(f"m_{n}", [P, TT, TOP_K]) for n in ("top", "k8", "w8"))
        tsum = sb("m_tsum", [P, TT])
        place = sb("m_place", [P, TT, TOP_K], U32)
        count, total = sb("m_count", [P, EXPERTS]), sb("m_total", [P, 1])
        npages, cur = sb("m_npages", [P, TT + 1, EXPERTS], I32), sb("m_cur", [P, TT + 1, EXPERTS])
        slots = sb("m_slots", [P, TT, SLOTS])
        et, ptab, ptab_i = sb("m_page_expert", [P, 3]), sb("m_ptab", [P, 3]), sb("m_ptab_i", [P, 3], I32)
        rows = sb("m_rows", [P, TT, SLOTS, ROW])
        ps = ctx.enter_context(nc.psum_tensor("m_ps", [P, 8, S], F32))
        two = lambda n: ps[:, n:n + 2].rearrange("p a (t c) -> p (a t) c", t=2)
        ident = C[:, COL["ident"]]

        const_in = sem("m_const_in")
        o_in, x_in, ct_in, cr_in = sem("m_o_in"), sem("m_x_in"), sem("m_ct_in"), sem("m_cr_in")
        projected, normed, x1_turned, x1t_done, enc_done = (sem(f"m_{n}") for n in ("projected", "normed", "x1_turned", "x1t_done", "enc_done"))
        similar, row_maxed, row_expd, row_scaled, row_turned, at_done = (sem(f"m_{n}") for n in ("similar", "row_maxed", "row_expd", "row_scaled", "row_turned", "at_done"))
        um_done, um_turned, g_done, g_spread, ng_done, eb_done, hc_summed, w1_done = (sem(f"m_{n}") for n in ("um_done", "um_turned", "g_done", "g_spread", "ng_done", "eb_done", "hc_summed", "w1_done"))
        hq_made, hq_done, pr_done, mixed, normed2, x2_turned, x2t_done = (sem(f"m_{n}") for n in ("hq_made", "hq_done", "pr_done", "mixed", "normed2", "x2_turned", "x2t_done"))
        routed, lg_done, lg_expd, mask_done, ranked = (sem(f"m_{n}") for n in ("routed", "lg_done", "lg_expd", "mask_done", "ranked"))
        rows_copied, rows_done, sent, x2_stored, table_done = (sem(f"m_{n}") for n in ("rows_copied", "rows_done", "sent", "x2_stored", "table_done"))
        ordered, all_sent, all_stored, table_out = sem("m_ordered"), sem("m_all_sent"), sem("m_all_stored"), sem("m_table_out")
        dispatching = sem("m_dispatching")
        ones_set, below_set, state_set = sem("m_ones_set"), sem("m_below_set"), sem("m_state_set")
        block = ctx.enter_context(nc.Block())

        @block.sync
        def _(sp):
            sp.dma_start(O[:], od[0:NG].rearrange("g p q -> p g q")).then_inc(o_in, 16)
            sp.dma_start(Wo[:], wo).then_inc(const_in, 16)
            sp.dma_start(X[:], x[0]).then_inc(x_in, 16)
            for dst, src in ((C, consts), (Cols, cols), (Rb, rowsb)):
                sp.dma_start(dst[:], src).then_inc(const_in, 16)
            sp.dma_start(CT[:], ctx_t[0]).then_inc(ct_in, 16)
            sp.dma_start(CR[:], ctx_r[0]).then_inc(cr_in, 16)
            for dst, src in ((Wqv, wqv), (Wr, wr)):
                sp.dma_start(dst[:], src).then_inc(const_in, 16)

            def load(b):
                sp.wait_ge(projected, TT * b)
                sp.dma_start(O[:], od[bass.ds(b * NG, NG)].rearrange("g p q -> p g q")).then_inc(o_in, 16)
                sp.wait_ge(normed, b)
                sp.dma_start(X[:], x[bass.ds(b, 1)].rearrange("a p t d -> (a p) t d")).then_inc(x_in, 16)
                sp.wait_ge(similar, TT * b)
                sp.dma_start(CT[:], ctx_t[bass.ds(b, 1)].rearrange("a p c q -> (a p) c q")).then_inc(ct_in, 16)
                sp.wait_ge(hq_made, DC * b)
                sp.dma_start(CR[:], ctx_r[bass.ds(b, 1)].rearrange("a p t d -> (a p) t d")).then_inc(cr_in, 16)

            def store(b):
                sp.wait_ge(normed2, b + 1)
                sp.dma_start(x2d[bass.ds(b, 1)].rearrange("a p t d -> (a p) t d"), X2[:]).then_inc(x2_stored, 16)
                sp.wait_ge(rows_done, b + 1)
                for t in range(TT):
                    page = b * TT + (POOL_PAGES + t)
                    sp.dma_start(pool[bass.ds(page * P, P)], rows[:, t, TOP_K]).then_inc(x2_stored, 16)
                sp.wait_ge(x2_stored, (b + 1) * (16 * (TT + 1)))
                sp.sem_inc(all_stored, 1)

            sp.sem_inc(all_stored, 1)

            with sp.Fori(0, B - 1) as b:
                load(b + 1)
                store(b)
            store(B - 1)
            sp.wait_ge(table_done, 1)
            sp.dma_start(pages_d.rearrange("c p -> p c"), ptab_i[:], allow_slow_non_contiguous=True).then_inc(table_out, 16)
            sp.wait_ge(table_out, 16)

        @block.gpsimd
        def _(pool_eng):
            for tile, value in ((rows, 0.0), (ones, 1.0), (ones32, 1.0), (ones_row, 1.0)):
                nc.gpsimd.memset(tile[:], value).then_inc(ones_set, 1)
            pool_eng.sem_inc(all_sent, 1)
            pool_eng.wait_ge(pool_filled, FILLS * 16)
            with pool_eng.Fori(0, B) as b:
                pool_eng.wait_ge(rows_done, b + 1)
                pool_eng.sem_inc(dispatching, 1)
                for t in range(TT):
                    for k in range(TOP_K):
                        nc.gpsimd.indirect_dma_start(
                            out=pool, out_offset=bass.IndirectOffsetOnAxis(ap=place[:, t, k:k + 1], axis=0),
                            in_=rows[:, t, k], in_offset=None, bounds_check=POOL_PAGES * P - 1,
                            oob_is_err=False).then_inc(sent, 16)
                pool_eng.wait_ge(sent, (b + 1) * (16 * TT * TOP_K))
                pool_eng.sem_inc(all_sent, 1)

        @block.tensor
        def _(pe):
            pe.wait_ge(const_in, 16 * 6)
            pe.wait_ge(ones_set, 4)
            pe.wait_ge(below_set, 1)

            def turn(src, bank, ready, ready_at, done):
                pe.wait_ge(ready, ready_at)
                for t in range(TT):
                    for c in range(DC):
                        last = nc.tensor.transpose(ps[:, bank + c, t * P:(t + 1) * P],
                                                   src[:, t, c * P:(c + 1) * P], ident)
                last.then_inc(done, 1)

            with pe.Fori(0, B) as b:
                tile = lambda t: b * TT + (t + 1)
                pe.wait_ge(o_in, b * 16 + 16)
                pe.wait_ge(lg_done, b + 1)
                h = two(0)
                for t in range(TT):
                    for n in range(NG):
                        last = nc.tensor.matmul(h[:, t], O[:, n, t * P:(t + 1) * P], Wo[:, n],
                                                start=n == 0, stop=n == NG - 1)
                    last.then_inc(projected, 1)
                turn(X1, 2, normed, b + 1, x1_turned)
                pe.wait_ge(enc_done, b + 1)
                pe.wait_ge(ct_in, b * 16 + 16)

                def similarity(i):
                    if i >= 2:
                        pe.wait_ge(row_expd, tile(i - 2))
                    for c in range(DC):
                        last = nc.tensor.matmul(ps[:, 4 + i % 2], ET[:, c, i * P:(i + 1) * P], CT[:, c],
                                                start=c == 0, stop=c == DC - 1)
                    last.then_inc(similar, 1)

                def turn_row(i):
                    pe.wait_ge(row_scaled, tile(i))
                    if i >= 2:
                        pe.wait_ge(at_done, tile(i - 2))
                    for j in range(TT):
                        last = nc.tensor.transpose(ps[:, 6 + i % 2, j * P:(j + 1) * P],
                                                   A[:, i, j * P:(j + 1) * P], ident)
                    last.then_inc(row_turned, 1)

                similarity(0)
                similarity(1)
                for i in range(2, TT):
                    similarity(i)
                    turn_row(i - 2)
                pe.wait_ge(um_done, b + 1)
                pe.wait_ge(x1t_done, b + 1)
                nc.tensor.transpose(ps[0:1, 2, 0:P], um[:], ident).then_inc(um_turned, 1)
                turn_row(TT - 2)
                pe.wait_ge(g_done, b + 1)
                nc.tensor.matmul(ps[:, 2, P:P + 1], ones32[0:1, :], g[:], start=True, stop=True).then_inc(g_spread, 1)
                turn_row(TT - 1)
                pe.wait_ge(eb_done, b + 1)
                nc.tensor.matmul(ps[:, 2, 2 * P:2 * P + TT], ones32[:], eb[:], start=True, stop=True)
                for c in range(DC):
                    for t in range(TT):
                        last = nc.tensor.matmul(ps[:, 3, c:c + 1], X1[:, t, c * P:(c + 1) * P], eb[:, t:t + 1],
                                                start=t == 0, stop=t == TT - 1)
                last.then_inc(hc_summed, 1)
                pe.wait_ge(at_done, tile(TT - 1))
                pe.wait_ge(cr_in, b * 16 + 16)
                for c in range(DC):
                    for j in range(TT):
                        last = nc.tensor.matmul(ps[:, c], CR[:, j, c * P:(c + 1) * P], AT[:, j],
                                                start=j == 0, stop=j == TT - 1)
                    last.then_inc(hq_made, 1)
                pe.wait_ge(w1_done, b + 1)
                pe.wait_ge(pr_done, b + 1)
                pe.wait_ge(hq_done, DC * b + DC)
                parts = [(X1T, W1, 0, c) for c in range(DC)] + [(HQ, Wqv, DC, c) for c in range(DC)] + \
                    [(PR, Wqv, 2 * DC, c) for c in range(DC)]
                h = two(4)
                for t in range(TT):
                    for n, (src, W, at, c) in enumerate(parts):
                        last = nc.tensor.matmul(h[:, t], src[:, c, t * P:(t + 1) * P], W[:, at + c],
                                                start=n == 0, stop=n == len(parts) - 1)
                    last.then_inc(mixed, 1)
                turn(X2, 6, normed2, b + 1, x2_turned)
                pe.wait_ge(x2t_done, b + 1)
                lgs = two(0)
                for t in range(TT):
                    for c in range(DC):
                        last = nc.tensor.matmul(lgs[:, t, 0:EXPERTS], X2T[:, c, t * P:(t + 1) * P], Wr[:, c],
                                                start=c == 0, stop=c == DC - 1)
                last.then_inc(routed, 1)
                pe.wait_ge(mask_done, b + 1)
                before, upto = two(2), two(4)
                for t in range(TT):
                    for s in range(t):
                        nc.tensor.matmul(before[:, t, 0:EXPERTS], ones[:], mask[:, s], start=s == 0, stop=False)
                        nc.tensor.matmul(upto[:, t, 0:EXPERTS], ones[:], mask[:, s], start=s == 0, stop=False)
                    nc.tensor.matmul(before[:, t, 0:EXPERTS], below[:], mask[:, t], start=t == 0, stop=True)
                    last = nc.tensor.matmul(upto[:, t, 0:EXPERTS], ones[:], mask[:, t], start=t == 0, stop=True)
                last.then_inc(ranked, 1)

        @block.scalar
        def _(act):
            act.wait_ge(const_in, 16 * 6)
            nc.scalar.activation(below[:], C[:, COL["below"]], ACT.Copy).then_inc(below_set, 1)
            with act.Fori(0, B) as b:
                tile = lambda t: b * TT + (t + 1)
                act.wait_ge(x1_turned, b + 1)
                for c in range(DC):
                    last = nc.scalar.activation(X1T[:, c], ps[:, 2 + c], ACT.Copy)
                last.then_inc(x1t_done, 1)
                for i in range(TT):
                    act.wait_ge(row_maxed, tile(i))
                    nc.scalar.activation(A[:, i], ps[:, 4 + i % 2], ACT.Exp, bias=nmax[:, i:i + 1],
                                         accum_out=rsum[:, i:i + 1]).then_inc(row_expd, 1)
                    if i >= 1:
                        act.wait_ge(row_turned, tile(i - 1))
                        nc.scalar.activation(AT[:, :, (i - 1) * P:i * P],
                                             ps[:, 6 + (i - 1) % 2].rearrange("p (j q) -> p j q", j=TT),
                                             ACT.Copy).then_inc(at_done, 1)
                act.wait_ge(ng_done, b + 1)
                nc.scalar.activation(eb[:], u[:], ACT.Exp, bias=ng[:]).then_inc(eb_done, 1)
                act.wait_ge(row_turned, tile(TT - 1))
                nc.scalar.activation(AT[:, :, (TT - 1) * P:], ps[:, 6 + (TT - 1) % 2].rearrange("p (j q) -> p j q", j=TT),
                                     ACT.Copy).then_inc(at_done, 1)
                for c in range(DC):
                    act.wait_ge(hq_made, DC * b + (c + 1))
                    nc.scalar.activation(HQ[:, c], ps[:, c], ACT.Copy).then_inc(hq_done, 1)
                act.wait_ge(x2_turned, b + 1)
                for c in range(DC):
                    last = nc.scalar.activation(X2T[:, c], ps[:, 6 + c], ACT.Copy)
                last.then_inc(x2t_done, 1)
                act.wait_ge(all_sent, b + 1)
                act.wait_ge(all_stored, b + 1)
                for t in range(TT):
                    last = nc.scalar.activation(rows[:, t, :, 0:D], repeated(X2[:, t], 1, SLOTS), ACT.Copy)
                    if t == 0:
                        act.wait_ge(lg_done, b + 2)
                        nc.scalar.activation(lg[:], lg[:], ACT.Exp, scale=-1.0).then_inc(lg_expd, 1)
                last.then_inc(rows_copied, 1)

        @block.vector
        def _(dve):
            dve.wait_ge(const_in, 16 * 6)
            dve.wait_ge(ones_set, 4)
            nc.vector.tensor_copy(ptab[:], C[:, COL["page_expert"]]).then_inc(state_set, 1)
            nc.vector.tensor_copy(slots[:], C[:, COL["slot"]].rearrange("p (t k) -> p t k", t=TT)).then_inc(state_set, 1)
            for state in (count[:], total[:], cur[:, 0]):
                nc.vector.memset(state, 0.0).then_inc(state_set, 1)
            nc.vector.memset(npages[:, 0], 0).then_inc(state_set, 1)
            nc.vector.memset(rows[:, :, TOP_K, W_COL:W_COL + 1], 1.0).then_inc(state_set, 1)
            dve.wait_ge(state_set, 7)
            dve.sem_inc(lg_done, 1)
            w1b, bqv, ebias = Rb[:, 0:D], Rb[:, D:2 * D], Rb[:, 2 * D:]
            w2, w3, bsim = Cols[:, 0:DC], Cols[:, DC:2 * DC], Cols[:, 2 * DC:2 * DC + 1]
            flat = lambda a: a.rearrange("p t e -> p (t e)")
            with dve.Fori(0, B) as b:
                tile = lambda t: b * TT + (t + 1)
                o = Order(dve, ordered, b * MIX_ORDERED, MIX_ORDERED)
                do, sync = o.do, o.sync
                dve.wait_ge(x_in, b * 16 + 16)
                for t in range(TT):
                    dve.wait_ge(projected, tile(t | 1))
                    do(nc.vector.tensor_tensor(H[:, t], two(0)[:, t], X[:, t], ALU.add))
                sync()
                layernorm(nc, o, H, X1, st, mv, v, y[:], t4[:])
                sync()
                nc.vector.tensor_tensor(X1b[:], X1[:], repeated(bqv, 1, TT), ALU.add).then_inc(normed, 1)
                for t in range(TT):
                    do(nc.vector.tensor_tensor_reduce(out=junk[:].rearrange("p t e -> p (t e)")[:, 0:D], in0=X1[:, t], in1=w1b, scale=1.0, scalar=0.0,
                                                      op0=ALU.mult, op1=ALU.add, accum_out=dots[:, t:t + 1]))
                    sync()
                dve.wait_ge(x1t_done, b + 1)
                for c in range(DC):
                    last = nc.vector.tensor_scalar(ET[:, c], X1T[:, c], w3[:, c:c + 1], w2[:, c:c + 1],
                                                   ALU.mult, ALU.add)
                last.then_inc(enc_done, 1)

                def scale_row(i):
                    dve.wait_ge(row_expd, tile(i))
                    do(nc.vector.reciprocal(rinv[:, i:i + 1], rsum[:, i:i + 1]))
                    sync()
                    nc.vector.tensor_scalar(A[:, i], A[:, i], rinv[:, i:i + 1], None, ALU.mult).then_inc(row_scaled, 1)

                for i in range(TT):
                    dve.wait_ge(similar, tile(i))
                    nc.vector.tensor_reduce(nmax[:, i:i + 1], ps[:, 4 + i % 2], AX, ALU.max, negate=True).then_inc(row_maxed, 1)
                    if i >= 1:
                        scale_row(i - 1)
                dve.wait_ge(row_maxed, tile(TT - 1))
                do(nc.vector.scalar_tensor_tensor(u[:], nmax[:], -1.0, dots[:], ALU.mult, ALU.add))
                sync()
                do(nc.vector.tensor_scalar(u[:], u[:], bsim, None, ALU.add))
                sync()
                nc.vector.tensor_reduce(um[:], u[:], AX, ALU.max).then_inc(um_done, 1)
                scale_row(TT - 1)
                dve.wait_ge(um_turned, b + 1)
                nc.vector.tensor_reduce(g[:], ps[0:1, 2, 0:P], AX, ALU.max).then_inc(g_done, 1)
                dve.wait_ge(g_spread, b + 1)
                nc.vector.tensor_scalar(ng[:], ps[:, 2, P:P + 1], -1.0, None, ALU.mult).then_inc(ng_done, 1)
                dve.wait_ge(hc_summed, b + 1)
                do(nc.vector.tensor_reduce(esum[:], ps[:, 2, 2 * P:2 * P + TT], AX, ALU.add))
                sync()
                do(nc.vector.reciprocal(einv[:], esum[:]))
                sync()
                do(nc.vector.tensor_scalar(hc[:], ps[:, 3, 0:DC], einv[:], None, ALU.mult))
                sync()
                for c in range(DC):
                    last = nc.vector.scalar_tensor_tensor(W1[:, c], Wqv[:, 3 * DC + c], hc[:, c:c + 1], Wqv[:, c],
                                                          ALU.mult, ALU.add)
                last.then_inc(w1_done, 1)
                for c in range(DC):
                    dve.wait_ge(hq_done, DC * b + (c + 1))
                    last = nc.vector.tensor_tensor(PR[:, c], HQ[:, c], X1T[:, c], ALU.mult)
                last.then_inc(pr_done, 1)
                dve.wait_ge(all_stored, b + 1)
                for t in range(TT):
                    dve.wait_ge(mixed, tile(t | 1))
                    do(nc.vector.tensor_tensor(H[:, t], two(4)[:, t], X1b[:, t], ALU.add))
                sync()
                layernorm(nc, o, H, X2, st, mv, v, y[:], t4[:])
                sync()
                dve.sem_inc(normed2, 1)
                dve.wait_ge(routed, b + 1)
                for t in range(0, TT, 2):
                    last = nc.vector.tensor_tensor(lg[:, t:t + 2], two(0)[:, t:t + 2, 0:EXPERTS],
                                                   repeated(ebias, 1, 2), ALU.add)
                last.then_inc(lg_done, 1)
                dve.wait_ge(lg_expd, b + 1)
                do(nc.vector.tensor_scalar(lg[:], lg[:], 1.0, None, ALU.add))
                sync()
                do(nc.vector.reciprocal(pr[:], lg[:]))
                o.hold()
                for t in range(TT):
                    do(nc.vector.max(top[:, t], pr[:, t]))
                o.hold()
                for t in range(TT):
                    do(nc.vector.match_replace(rep[:, t], top[:, t], pr[:, t], -1.0))
                do(nc.vector.tensor_reduce(tsum[:], top[:], AX, ALU.add))
                sync()
                nc.vector.tensor_tensor(mask[:], pr[:], rep[:], ALU.not_equal).then_inc(mask_done, 1)
                do(nc.vector.tensor_scalar(tsum[:], tsum[:], 1e-9, None, ALU.add))
                sync()
                do(nc.vector.reciprocal(rinv[:], tsum[:]))
                dve.wait_ge(ranked, b + 1)
                do(nc.vector.tensor_tensor(ri[:, 0:2], two(2)[:, 0:2, 0:EXPERTS], repeated(count[:], 1, 2), ALU.add))
                do(nc.vector.tensor_tensor(ri[:, 2:4], two(2)[:, 2:4, 0:EXPERTS], repeated(count[:], 1, 2), ALU.add))
                do(nc.vector.scalar_tensor_tensor(ni[:, 0:2], two(4)[:, 0:2, 0:EXPERTS], float(P - 1), repeated(count[:], 1, 2), ALU.add, ALU.add))
                do(nc.vector.scalar_tensor_tensor(ni[:, 2:4], two(4)[:, 2:4, 0:EXPERTS], float(P - 1), repeated(count[:], 1, 2), ALU.add, ALU.add))
                sync()
                do(nc.vector.tensor_tensor(count[:], two(4)[:, TT - 1, 0:EXPERTS], count[:], ALU.add))
                do(nc.vector.tensor_scalar(npages[:, 1:], ni[:], 7, None, ALU.arith_shift_right))
                sync()
                do(nc.vector.tensor_tensor(need[:], npages[:, 1:], npages[:, 0:TT], ALU.subtract))
                do(nc.vector.scalar_tensor_tensor(late[:], npages[:, 0:TT], float(P), ri[:], ALU.mult, ALU.is_le))
                do(nc.vector.tensor_scalar(ri[:], ri[:], P - 1, None, ALU.bitwise_and))
                sync()
                do(nc.vector.tensor_tensor_scan(flat(q[:]), ones_row[:], flat(need[:]), total[:], ALU.mult, ALU.add))
                do(nc.vector.tensor_scalar(keep[:], need[:], -1.0, 1.0, ALU.mult, ALU.add))
                sync()
                do(nc.vector.tensor_scalar(total[:], flat(q[:])[:, TT * EXPERTS - 1:], 1.0, None, ALU.mult))
                do(nc.vector.tensor_copy(npages[:, 0], npages[:, TT]))
                sync()
                do(nc.vector.tensor_tensor(q[:], q[:], need[:], ALU.subtract))
                sync()
                do(nc.vector.tensor_tensor(nq[:], q[:], need[:], ALU.mult))
                sync()
                for t in range(TT):
                    do(nc.vector.tensor_tensor(cur[:, t + 1], cur[:, t], keep[:, t], ALU.mult))
                    sync()
                    do(nc.vector.tensor_tensor(cur[:, t + 1], cur[:, t + 1], nq[:, t], ALU.add))
                    sync()
                do(nc.vector.tensor_tensor(q[:], q[:], cur[:, 0:TT], ALU.subtract))
                do(nc.vector.tensor_tensor(nq[:], nq[:], keep[:], ALU.subtract))
                sync()
                do(nc.vector.tensor_tensor(q[:], q[:], late[:], ALU.mult))
                for c in range(3):
                    do(nc.vector.scalar_tensor_tensor(junk[:], nq[:], C[:, COL["page"]][:, c:c + 1],
                                                      repeated(C[:, COL["expert"]], 1, TT), ALU.is_equal, ALU.mult,
                                                      accum_out=et[:, c:c + 1]))
                    sync()
                do(nc.vector.tensor_tensor(q[:], q[:], cur[:, 0:TT], ALU.add))
                do(nc.vector.tensor_tensor(ptab[:], ptab[:], et[:], ALU.add))
                sync()
                do(nc.vector.tensor_copy(cur[:, 0], cur[:, TT]))
                do(nc.vector.scalar_tensor_tensor(q[:], q[:], float(P), ri[:], ALU.mult, ALU.add))
                sync()
                do(nc.vector.tensor_scalar(key[:], q[:], -1.0, FAR, ALU.mult, ALU.add))
                sync()
                do(nc.vector.tensor_tensor(key[:], key[:], mask[:], ALU.mult))
                o.hold()
                for t in range(TT):
                    do(nc.vector.max(k8[:, t], key[:, t]))
                sync()
                for t in range(TT):
                    for k in range(TOP_K):
                        sync(but=TT - 1)
                        do(nc.vector.scalar_tensor_tensor(junk[:, k % TT], key[:, t], k8[:, t, k:k + 1], pr[:, t],
                                                          ALU.is_equal, ALU.mult, accum_out=w8[:, t, k:k + 1]))
                sync()
                dve.wait_ge(rows_copied, b + 1)
                do(nc.vector.tensor_scalar(place[:], k8[:], -1.0, FAR, ALU.mult, ALU.add))
                do(nc.vector.tensor_copy(rows[:, :, :, DST_COL].bitcast(U32), slots[:]))
                for t in range(TT):
                    do(nc.vector.tensor_scalar(rows[:, t, 0:TOP_K, W_COL], w8[:, t], rinv[:, t:t + 1], ROUTED_SCALE,
                                               ALU.mult, ALU.mult))
                sync()
                dve.sem_inc(rows_done, 1)
                do(nc.vector.tensor_scalar(slots[:], slots[:], float(S * SLOTS), None, ALU.add))
                sync()
                o.close()
            nc.vector.tensor_copy(ptab_i[:], ptab[:]).then_inc(table_done, 1)


def experts(nc, ident_d, w, pages_d, pool, contrib):
    RING = 8
    with ExitStack() as ctx:
        sb = lambda n, s, d=F32: ctx.enter_context(nc.sbuf_tensor(n, s, d))
        sem = lambda n: ctx.enter_context(nc.semaphore(n))
        table, ident = sb("e_table", [1, 3 * P], I32), sb("e_ident", [P, P])
        W, X, Y = sb("e_w", [P, RING, DC * INTER + D]), sb("e_x", [P, RING, ROW]), sb("e_y", [P, RING, D])
        XT, G = sb("e_xt", [P, 2, DC, P]), sb("e_g", [P, 2, P])
        psX, psG, psY = (ctx.enter_context(nc.psum_tensor(f"e_ps{n}", [P, 2, S], F32)) for n in "xgy")
        table_in, ident_in = sem("e_table_in"), sem("e_ident_in")
        w_in = [sem(f"e_w_in{r}") for r in range(RING)]
        x_in = [sem(f"e_x_in{r}") for r in range(RING)]
        sent = [sem(f"e_sent{r}") for r in range(RING)]
        turned, xt_done, gated, silu_done, downed, y_done = (
            sem(f"e_{n}") for n in ("turned", "xt_done", "gated", "silu_done", "downed", "y_done"))
        sending = sem("e_sending")
        run = lambda eng, step: run_steps(eng, step, RING, RING, (STEPS_E - RING) // RING, STEPS_E + 2)
        block = ctx.enter_context(nc.Block())

        @block.sync
        def _(sp):
            sp.dma_start(table[:], pages_d.rearrange("(a c) p -> a (c p)", a=1)).then_inc(table_in, 16)
            sp.dma_start(ident[:], ident_d).then_inc(ident_in, 16)
            sp.wait_ge(table_in, 16)

            def step(at):
                if not at.within(STEPS_E):
                    return
                if not at.first(RING):
                    sp.wait_ge(sent[at.slot], 16 * (at.uses() - 1))
                row = at.n * P
                sp.dma_start(X[:, at.slot], pool[bass.ds(row, P)]).then_inc(x_in[at.slot], 16)
                e = sp.value_load(table[0:1, bass.ds(at.n, 1)], min_val=0, max_val=EXPERTS)
                sp.dma_start(W[:, at.slot], w[bass.ds(e, 1)].rearrange("a p n -> (a p) n")).then_inc(w_in[at.slot], 16)
            run(sp, step)

        @block.tensor
        def _(pe):
            pe.wait_ge(ident_in, 16)

            def step(at):
                if at.within(STEPS_E):
                    pe.wait_ge(x_in[at.slot], 16 * at.uses())
                    if not at.first(2):
                        pe.wait_ge(xt_done, at.n - 1)
                    for c in range(DC):
                        last = nc.tensor.transpose(psX[:, at.k % 2, c * P:(c + 1) * P],
                                                   X[:, at.slot, c * P:(c + 1) * P], ident[:])
                    last.then_inc(turned, 1)
                f = at.back(1)
                if f.within(STEPS_E):
                    pe.wait_ge(w_in[f.slot], 16 * f.uses())
                    pe.wait_ge(xt_done, at.n)
                    if not f.first(2):
                        pe.wait_ge(silu_done, at.n - 2)
                    for c in range(DC):
                        last = nc.tensor.matmul(psG[:, f.k % 2, 0:P], W[:, f.slot, c * INTER:(c + 1) * INTER],
                                                XT[:, f.k % 2, c], start=c == 0, stop=c == DC - 1)
                    last.then_inc(gated, 1)
                f = at.back(2)
                if f.within(STEPS_E):
                    pe.wait_ge(silu_done, at.n - 1)
                    if not f.first(2):
                        pe.wait_ge(y_done, at.n - 3)
                    nc.tensor.matmul(psY[:, f.k % 2, 0:D], G[:, f.k % 2], W[:, f.slot, DC * INTER:],
                                     start=True, stop=True).then_inc(downed, 1)
            run(pe, step)

        @block.vector
        def _(dve):
            def step(at):
                if at.within(STEPS_E):
                    dve.wait_ge(turned, at.n + 1)
                    if not at.first(2):
                        dve.wait_ge(gated, at.n - 1)
                    nc.vector.tensor_copy(XT[:, at.k % 2], psX[:, at.k % 2, 0:D].rearrange("p (c q) -> p c q", c=DC)
                                          ).then_inc(xt_done, 1)
            run(dve, step)

        @block.scalar
        def _(act):
            act.wait_ge(ident_in, 16)

            def step(at):
                f = at.back(1)
                if f.within(STEPS_E):
                    act.wait_ge(gated, at.n)
                    if not f.first(2):
                        act.wait_ge(downed, at.n - 2)
                    nc.scalar.activation(G[:, f.k % 2], psG[:, f.k % 2, 0:P], ACT.Silu).then_inc(silu_done, 1)
                f = at.back(2)
                if f.within(STEPS_E):
                    act.wait_ge(downed, at.n - 1)
                    nc.scalar.activation(Y[:, f.slot], psY[:, f.k % 2, 0:D], ACT.Copy,
                                         scale=X[:, f.slot, W_COL:W_COL + 1]).then_inc(y_done, 1)
            run(act, step)

        @block.gpsimd
        def _(pool_eng):
            def step(at):
                f = at.back(2)
                if f.within(STEPS_E):
                    pool_eng.wait_ge(y_done, at.n - 1)
                    pool_eng.sem_inc(sending, 1)
                    nc.gpsimd.indirect_dma_start(
                        out=contrib, out_offset=bass.IndirectOffsetOnAxis(
                            ap=X[:, f.slot, DST_COL:DST_COL + 1].bitcast(U32), axis=0),
                        in_=Y[:, f.slot], in_offset=None, bounds_check=TOKENS * SLOTS - 1,
                        oob_is_err=False).then_inc(sent[f.slot], 16)
            run(pool_eng, step)
            for r in range(RING):
                pool_eng.wait_ge(sent[r], 16 * (STEPS_E // RING))


def combine(nc, x2d, contrib, out):
    with ExitStack() as ctx:
        sb = lambda n, s, d=F32: ctx.enter_context(nc.sbuf_tensor(n, s, d))
        sem = lambda n: ctx.enter_context(nc.semaphore(n))
        Cn, X, H, Y = sb("c_c", [P, TT, SLOTS, D]), sb("c_x", [P, TT, D]), sb("c_h", [P, TT, D]), sb("c_y", [P, TT, D])
        st, mv, v = sb("c_st", [P, TT, 6]), sb("c_mv", [P, TT, 2]), sb("c_v", [P, 2, TT])
        y, t4 = sb("c_y4", [P, TT]), sb("c_t4", [P, TT])
        c_in = [sem(f"c_c_in{t}") for t in range(TT)]
        x_in, ordered, reduced, added, normed, stored, out_free = (
            sem(f"c_{n}") for n in ("x_in", "ordered", "reduced", "added", "normed", "stored", "out_free"))
        block = ctx.enter_context(nc.Block())

        @block.sync
        def _(sp):
            def load(b, again):
                for t in range(TT):
                    if again:
                        sp.wait_ge(reduced, b * TT - (TT - 1 - t))
                    src = contrib[bass.ds(b * (S * SLOTS) + t * P * SLOTS, P * SLOTS)]
                    sp.dma_start(Cn[:, t], src.rearrange("(p k) d -> p k d", k=SLOTS)).then_inc(c_in[t], 16)
                if again:
                    sp.wait_ge(added, b)
                sp.dma_start(X[:], x2d[bass.ds(b, 1)].rearrange("a p t d -> (a p) t d")).then_inc(x_in, 16)
            load(0, False)
            with sp.Fori(0, B - 1) as b:
                load(b + 1, True)

        @block.scalar
        def _(act):
            act.sem_inc(out_free, 1)
            with act.Fori(0, B) as b:
                act.wait_ge(normed, b + 1)
                act.dma_start(out[bass.ds(b, 1)].rearrange("a (t p) d -> (a p) t d", p=P), Y[:]).then_inc(stored, 16)
                act.wait_ge(stored, b * 16 + 16)
                act.sem_inc(out_free, 1)

        @block.vector
        def _(dve):
            with dve.Fori(0, B) as b:
                o = Order(dve, ordered, b * (LN_ORDERED + TT), LN_ORDERED + TT)
                for t in range(TT):
                    dve.wait_ge(c_in[t], b * 16 + 16)
                    nc.vector.tensor_reduce(H[:, t], Cn[:, t].rearrange("p k d -> p d k"), AX, ALU.add).then_inc(reduced, 1)
                dve.wait_ge(x_in, b * 16 + 16)
                dve.wait_ge(reduced, b * TT + TT)
                for t in range(TT):
                    o.do(nc.vector.tensor_tensor(H[:, t], H[:, t], X[:, t], ALU.add))
                o.sync()
                dve.sem_inc(added, 1)
                dve.wait_ge(out_free, b + 1)
                layernorm(nc, o, H, Y, st, mv, v, y[:], t4[:])
                o.sync()
                dve.sem_inc(normed, 1)
                o.close()


def decoder_layer(nc, xt, x, ctx_t, ctx_r, wq, wk, wv, wo, wqv, wr, cols, rowsb, w, sel, kaux, consts, out):
    dram = lambda n, s, d=F32: nc.dram_tensor(n, s, d, kind="Internal").ap()
    qd, kd = (dram(n, [STEPS, 2, DH, HG, S]) for n in ("q_parts", "k_parts"))
    vd, od = dram("v_heads", [STEPS, P, TT, HG * 2 * DH]), dram("o_heads", [STEPS, P, S])
    pool = dram("row_pool", [STEPS_E * P, ROW])
    x2d, contrib = dram("tokens", [B, P, TT, D]), dram("contributions", [TOKENS * SLOTS, D])
    pages_d = dram("page_table", [3, P], I32)
    with ExitStack() as ctx:
        fill = ctx.enter_context(nc.sbuf_tensor("fill", [P, ROW], F32))
        pool_filled = ctx.enter_context(nc.semaphore("pool_filled"))
        project(nc, xt, wq, wk, wv, fill, qd, kd, vd)
        attend(nc, sel, kaux, qd, kd, vd, od, fill, pool, pool_filled)
        mix(nc, consts, wo, wqv, wr, cols, rowsb, x, ctx_t, ctx_r, od, pool, pool_filled, x2d, pages_d)
        experts(nc, consts[:, COL["ident"]], w, pages_d, pool, contrib)
        combine(nc, x2d, contrib, out)


def constants(np):
    sel = np.zeros((2, P, P), np.float32)
    for h in range(HG):
        sel[0, 2 * DH * h + DH, 2 * DH * h:2 * DH * (h + 1)] = 1
    sel[1] = np.eye(P)
    kaux = np.zeros((32, HG, S), np.float32)
    for h in range(HG):
        kaux[h, h] = 1
    c = np.zeros((P, N_CONST), np.float32)
    p = np.arange(P)
    c[:, COL["ident"]] = np.eye(P)
    c[:, COL["below"]] = np.triu(np.ones((P, P)), 1)
    c[:, COL["expert"]] = np.arange(EXPERTS)
    page = p[:, None] + P * np.arange(3)
    c[:, COL["page"]] = page
    c[:, COL["page_expert"]] = np.where((page >= POOL_PAGES) & (page < STEPS_E), EXPERTS, 0)
    t, k = np.arange(TT), np.arange(SLOTS)
    c[:, COL["slot"]] = ((p[:, None, None] + P * t[:, None]) * SLOTS + k).reshape(P, -1)
    return {"sel": sel, "kaux": kaux, "consts": c}


def kernel(**inputs):
    import numpy as np
    import concourse.bacc as bacc
    from concourse.bass_utils import run_bass_kernel_spmd

    I = {k: np.asarray(v) for k, v in inputs.items()}
    turned = lambda a: a.reshape(B, S, DC, P).transpose(0, 3, 2, 1)
    tiled = lambda a: a.reshape(B, TT, P, D).transpose(0, 2, 1, 3)
    chunked = lambda a: a.reshape(-1, P, a.shape[-1]).transpose(1, 0, 2)
    by_step = lambda a: chunked(a.T.reshape(D, DC, 2, HG, DH).transpose(0, 1, 2, 4, 3).reshape(D, D))
    g = lambda n: I["L0_" + n]
    wo = np.zeros((NG, HG, 2 * DH, D), np.float32)
    wo[:, :, 0:DH] = g("attn_w_o").T.reshape(NG, HG, DH, D)
    w_sim = g("xattn_w_sim")
    same = lambda a: np.broadcast_to(a, (P, a.size))
    gate = np.concatenate([g("ffn_w_gate"), g("ffn_w_gate_shared")[None]])
    down = np.concatenate([g("ffn_w_down"), g("ffn_w_down_shared")[None]])
    arrays = {
        "xt": turned(I["x"]), "x": tiled(I["x"]),
        "ctx_t": turned(I["ctx_1024"]), "ctx_r": tiled(I["ctx_1024"]),
        "wq": by_step(g("attn_w_q")), "wk": by_step(g("attn_w_k")), "wv": chunked(g("attn_w_v").T),
        "wo": wo.reshape(NG, P, D).transpose(1, 0, 2), "wqv": chunked(g("xattn_W_qv")),
        "wr": chunked(g("ffn_router_w").T),
        "cols": np.concatenate([w_sim[D:2 * D].reshape(DC, P).T, w_sim[2 * D:].reshape(DC, P).T,
                                np.broadcast_to(g("xattn_b_sim"), (P, 1))], axis=1),
        "rowsb": np.concatenate([same(w_sim[:D]), same(g("xattn_b_qv")), same(g("ffn_expert_bias"))], axis=1),
        "w": np.concatenate([gate.reshape(-1, INTER, DC, P).transpose(0, 3, 2, 1).reshape(-1, P, DC * INTER),
                             down.transpose(0, 2, 1)], axis=2),
        **constants(np),
    }
    arrays = {k: np.ascontiguousarray(v) for k, v in arrays.items()}
    nc = bacc.Bacc("TRN2", target_bir_lowering=False, num_devices=1)
    args = [nc.dram_tensor(k, v.shape, mybir.dt.from_np(v.dtype), kind="ExternalInput").ap() for k, v in arrays.items()]
    out = nc.dram_tensor("out", (B, S, D), F32, kind="ExternalOutput").ap()
    decoder_layer(nc, *args[:13], *args[13:], out)
    return run_bass_kernel_spmd(nc, [arrays], core_ids=[0]).results[0]["out"]
```

```python
from contextlib import ExitStack

import concourse.bass as bass
from concourse import mybir

F32 = mybir.dt.float32
F32R = mybir.dt.float32r
BF16 = mybir.dt.bfloat16
I32 = mybir.dt.int32
U32 = mybir.dt.uint32
ALU = mybir.AluOpType
ACT = mybir.ActivationFunctionType
AX = mybir.AxisListType.X

P = 128
B, S, D = 4, 512, 256
DC = D // P
TT = S // P
HEADS, DH = 16, 16
HG = 4
NG = HEADS // HG
STEPS = B * NG
EXPERTS, TOP_K, INTER = 160, 8, 128
TOKENS = B * S
TILES = TOKENS // P
ROUTED_SCALE = 2.5
PAGES = (TOKENS * TOP_K + EXPERTS * (P - 1)) // P
ROUND = 8
POOL_PAGES = -(-PAGES // ROUND) * ROUND
MORE_AT = 3 * P
W_COL, DST_COL = D, D + 1
ROW = D + 4
FILL_PAGES = 6
FILLS = POOL_PAGES // FILL_PAGES
NOWHERE = 1 << 20
FAR = float(1 << 17)
LN_EPS = 1e-5


def repeated(ap, at, count):
    shape = list(ap.shape)
    return ap.unsqueeze(at).broadcast_to(shape[:at] + [count] + shape[at:])


def project(nc, xt, wq, wk, wv, fill, qd, kd, vd):
    with ExitStack() as ctx:
        sb = lambda n, s, d=F32: ctx.enter_context(nc.sbuf_tensor(n, s, d))
        sem = lambda n: ctx.enter_context(nc.semaphore(n))
        xT = sb("p_xT", [P, B, DC, S])
        Wq, Wk, Wv = sb("p_wq", [P, DC, D]), sb("p_wk", [P, DC, D]), sb("p_wv", [P, DC, D])
        hi, lo = sb("p_hi", [P, 2, 4, S], F32R), sb("p_lo", [P, 2, 4, S], F32R)
        V = sb("p_v", [P, 2, TT, HEADS, 2 * DH])
        ps = ctx.enter_context(nc.psum_tensor("p_ps", [P, 8, S], F32))
        x_in = [sem(f"p_x_in{b}") for b in range(B)]
        w_in, v_ones, fill_zero = sem("p_w_in"), sem("p_v_ones"), sem("p_fill_zero")
        qk_made, v_made = sem("p_qk_made"), sem("p_v_made")
        hi_done, lo_done, v_done = sem("p_hi_done"), sem("p_lo_done"), sem("p_v_done")
        stored = [sem(f"p_stored{u}") for u in range(2)]
        STORES = 8 + 1
        block = ctx.enter_context(nc.Block())

        @block.sync
        def _(sp):
            sp.dma_start(Wq[:], wq).then_inc(w_in, 16)
            sp.dma_start(xT[:, 0], xt[0]).then_inc(x_in[0], 16)
            sp.dma_start(Wk[:], wk).then_inc(w_in, 16)
            sp.dma_start(Wv[:], wv).then_inc(w_in, 16)
            for b in range(1, B):
                sp.dma_start(xT[:, b], xt[b]).then_inc(x_in[b], 16)
            for b in range(B):
                u = b % 2
                sp.wait_ge(lo_done, 4 * (b + 1))
                for part, src in enumerate((hi, lo)):
                    for half in range(2):
                        for w, dst in enumerate((qd, kd)):
                            to = dst[:, part].rearrange("(b j g) e h q -> b g (e h) j q", b=B, g=2)[b, half]
                            rows = slice(P // 2 * half, P // 2 * (half + 1))
                            sp.dma_start(to, src[rows, u, 2 * w:2 * w + 2].bitcast(F32)).then_inc(stored[u], 16)
                sp.wait_ge(v_done, TT * (b + 1))
                sp.dma_start(vd.rearrange("(b g) p t e -> b p t g e", b=B)[b],
                             V[:, u].rearrange("p t (g h) e -> p t g (h e)", g=NG)).then_inc(stored[u], 16)
            for u in range(2):
                sp.wait_ge(stored[u], 16 * STORES * (B // 2))

        @block.gpsimd
        def _(pool_eng):
            nc.gpsimd.memset(V[:], 1.0).then_inc(v_ones, 1)
            nc.gpsimd.memset(fill[:], 0.0).then_inc(fill_zero, 1)
            pool_eng.wait_ge(fill_zero, 1)
            nc.gpsimd.memset(fill[:, DST_COL:DST_COL + 1].bitcast(I32), NOWHERE).then_inc(fill_zero, 1)
            pool_eng.wait_ge(fill_zero, 2)

        @block.tensor
        def _(pe):
            for b in range(B):
                pe.wait_ge(x_in[b], 16)
                if b == 0:
                    pe.wait_ge(w_in, 48)
                for n, (W, j) in enumerate(((Wq, 0), (Wq, 1), (Wk, 0), (Wk, 1))):
                    if b >= 1:
                        pe.wait_ge(lo_done, 4 * (b - 1) + n + 1)
                    for c in range(DC):
                        last = nc.tensor.matmul(ps[:, n], W[:, c, j * P:(j + 1) * P], xT[:, b, c],
                                                start=c == 0, stop=c == DC - 1)
                    last.then_inc(qk_made, 1)
                for t in range(TT):
                    if b >= 1:
                        pe.wait_ge(v_done, TT * (b - 1) + t + 1)
                    for c in range(DC):
                        last = nc.tensor.matmul(ps[:, 4 + t, 0:D], xT[:, b, c, t * P:(t + 1) * P], Wv[:, c],
                                                start=c == 0, stop=c == DC - 1)
                    last.then_inc(v_made, 1)

        @block.scalar
        def _(act):
            act.wait_ge(v_ones, 1)
            for b in range(B):
                u = b % 2
                if b >= 2:
                    act.wait_ge(stored[u], 16 * STORES * (b // 2))
                for n in range(4):
                    act.wait_ge(qk_made, 4 * b + n + 1)
                    nc.scalar.activation(hi[:, u, n], ps[:, n], ACT.Copy).then_inc(hi_done, 1)
                for t in range(TT):
                    act.wait_ge(v_made, TT * b + t + 1)
                    nc.scalar.activation(V[:, u, t, :, 0:DH],
                                         ps[:, 4 + t, 0:D].rearrange("p (h e) -> p h e", h=HEADS),
                                         ACT.Copy).then_inc(v_done, 1)

        @block.vector
        def _(dve):
            for b in range(B):
                u = b % 2
                if b >= 2:
                    dve.wait_ge(stored[u], 16 * STORES * (b // 2))
                for n in range(4):
                    dve.wait_ge(hi_done, 4 * b + n + 1)
                    nc.vector.tensor_tensor(lo[:, u, n], ps[:, n], hi[:, u, n].bitcast(F32),
                                            ALU.subtract).then_inc(lo_done, 1)


class At:

    def __init__(self, i, k, ring):
        self.i, self.k, self.ring = i, k, ring
        self.n = i * ring + k
        self.slot = k % ring
        self.fixed = isinstance(i, int)

    def back(self, by):
        return At(self.i, self.k - by, self.ring)

    def group(self, count):
        return self.i * (self.ring // count) + self.k // count

    def uses(self):
        return self.i + (self.k // self.ring + 1)

    def within(self, count):
        return not self.fixed or 0 <= self.n < count

    def first(self, count=1):
        return self.fixed and self.n < count


class Past(At):

    def __init__(self, i, k, ring):
        super().__init__(i, k, ring)
        self.fixed = False

    def within(self, count):
        return self.k < self.ring

    def back(self, by):
        return Past(self.i, self.k - by, self.ring)


def run_steps(eng, step, ring, first, rounds, last):
    for n in range(first):
        step(At(0, n, ring))
    with eng.Fori(0, rounds) as i:
        for k in range(first, first + ring):
            step(At(i, k, ring))
    for n in range(first + rounds * ring, last):
        step(At(0, n, ring))


def attend(nc, ident_d, kaux, qd, kd, vd, od, fill, pool, pool_filled):
    RING = 4
    KP = 4 * DH
    KR = 96
    NE = TT * HG
    NT = 3
    TILE_PAIRS = TT * HG // 2
    with ExitStack() as ctx:
        sb = lambda n, s, d=F32: ctx.enter_context(nc.sbuf_tensor(n, s, d))
        sem = lambda n: ctx.enter_context(nc.semaphore(n))
        Q, K = sb("a_q", [P, RING, HG, S], F32R), sb("a_k", [P, RING, HG, S], F32R)
        V = sb("a_v", [P, RING, TT, HG * 2 * DH])
        aux, zero = sb("a_aux", [KR - KP, HG, S]), sb("a_zero", [HG, HG, S])
        mrow = sb("a_mrow", [HG, RING, S])
        mx = sb("a_mx", [P, RING, TT, HG])
        ident = sb("a_ident", [P, P])
        E = sb("a_e", [P, NE, S])
        O, On, inv = sb("a_o", [P, S]), sb("a_on", [P, TT, HG, DH]), sb("a_inv", [P, TT, HG])
        psS = ctx.enter_context(nc.psum_tensor("a_psS", [P, 2, 2, S], F32))
        psT = ctx.enter_context(nc.psum_tensor("a_psT", [P, NT, S], F32))
        psO = ctx.enter_context(nc.psum_tensor("a_psO", [P, S], F32))
        const_in, aux_zero, aux_set = sem("a_const_in"), sem("a_aux_zero"), sem("a_aux_set")
        group_in = [sem(f"a_group_in{r}") for r in range(RING)]
        max_in = [sem(f"a_max_in{r}") for r in range(RING)]
        scored, maxed, turned, negated = sem("a_scored"), sem("a_maxed"), sem("a_turned"), sem("a_negated")
        rescored, expd, weighed = sem("a_rescored"), sem("a_expd"), sem("a_weighed")
        o_copied, o_turned, divided, stored = sem("a_o_copied"), sem("a_o_turned"), sem("a_divided"), sem("a_stored")
        inverted = sem("a_inverted")
        LOADS = 7
        run = lambda eng, step: run_steps(eng, step, RING, RING, (STEPS - RING) // RING - 1, STEPS + 3)
        block = ctx.enter_context(nc.Block())

        @block.sync
        def _(sp):
            sp.dma_start(aux[:], kaux).then_inc(const_in, 16)
            sp.dma_start(ident[:], ident_d).then_inc(const_in, 16)
            sp.wait_ge(aux_zero, 2)

            def load(at):
                if not at.first(RING):
                    sp.wait_ge(weighed, TT * (at.n - (RING - 1)))
                rows = lambda a, s0, s1: a[bass.ds(at.n, 1), s0:s1].rearrange("a s e h q -> (a s e) h q")
                Qf, Kf, here = Q[:, at.slot].bitcast(F32), K[:, at.slot].bitcast(F32), group_in[at.slot]
                sp.dma_start(Qf[0:2 * DH], rows(qd, 0, 2)).then_inc(here, 16)
                sp.dma_start(Qf[2 * DH:3 * DH], rows(qd, 1, 2)).then_inc(here, 16)
                sp.dma_start(Qf[3 * DH:KP], rows(qd, 0, 1)).then_inc(here, 16)
                sp.dma_start(Kf[0:2 * DH], rows(kd, 0, 2)).then_inc(here, 16)
                sp.dma_start(Kf[2 * DH:KP], rows(kd, 0, 2)).then_inc(here, 16)
                sp.dma_start(Qf[KP:KP + HG], zero[:]).then_inc(here, 16)
                sp.dma_start(V[:, at.slot], vd[bass.ds(at.n, 1)].rearrange("a p t e -> (a p) t e")).then_inc(here, 16)

            load(At(0, 0, RING))

            def step(at):
                if at.back(-1).within(STEPS):
                    load(at.back(-1))
                if at.within(STEPS):
                    for i in range(FILLS // STEPS):
                        row = (at.n * (FILLS // STEPS) + i) * (FILL_PAGES * P)
                        sp.dma_start(pool[bass.ds(row, FILL_PAGES * P)].rearrange("(k p) r -> p k r", p=P),
                                     repeated(fill[:], 1, FILL_PAGES)).then_inc(pool_filled, 16)
                if at.back(3).within(STEPS):
                    sp.wait_ge(divided, at.n - 2)
                    sp.dma_start(od[bass.ds(at.n - 3, 1)].rearrange("a p t h e -> (a p) t h e"), On[:]).then_inc(stored, 16)
                if at.back(1).within(STEPS):
                    sp.wait_ge(negated, at.n)
                    slot = at.back(1).slot
                    sp.dma_start(Q[KP:KP + HG, slot].bitcast(F32),
                                 repeated(mrow[:, slot], 1, HG)).then_inc(max_in[slot], 16)
            run(sp, step)
            sp.wait_ge(stored, 16 * STEPS)

        @block.gpsimd
        def _(pool):
            nc.gpsimd.memset(Q[KP:KR].bitcast(F32), 0.0).then_inc(aux_zero, 1)
            nc.gpsimd.memset(zero[:], 0.0).then_inc(aux_zero, 1)

        @block.tensor
        def _(pe):
            pe.wait_ge(const_in, 32)
            pe.wait_ge(aux_set, RING)
            pe.wait_ge(aux_zero, 2)

            def score(at, i):
                qt, pair = divmod(i, 2)
                if not (at.first() and i < 2):
                    pe.wait_ge(maxed, at.n * TILE_PAIRS + (i - 1))
                for h in range(2):
                    hh = 2 * pair + h
                    last = nc.tensor.matmul(psS[:, pair, h], Q[0:KR, at.slot, hh, qt * P:(qt + 1) * P],
                                            K[0:KR, at.slot, hh], start=True, stop=True)
                last.then_inc(scored, 1)

            def turn_maxima(at):
                pe.wait_ge(maxed, TILE_PAIRS * (at.n + 1))
                if not at.first():
                    pe.wait_ge(negated, at.n)
                if at.back(2).within(STEPS):
                    pe.wait_ge(divided, at.n - 1)
                for qt in range(TT):
                    last = nc.tensor.transpose(psO[0:HG, qt * P:(qt + 1) * P], mx[:, at.slot, qt], ident[:])
                last.then_inc(turned, 1)

            def rescore(at, kt, half):
                for i in (kt * HG + 2 * half, kt * HG + 2 * half + 1):
                    if i >= NT:
                        pe.wait_ge(expd, at.n * NE + (i - NT + 1))
                    elif i == 0 and not at.first():
                        pe.wait_ge(expd, at.n * NE)
                    nc.tensor.matmul(psT[:, i % NT], K[0:KR, at.slot, i % HG, kt * P:(kt + 1) * P],
                                     Q[0:KR, at.slot, i % HG], start=True, stop=True).then_inc(rescored, 1)

            def weigh(at, kt):
                pe.wait_ge(expd, at.n * NE + HG * (kt + 1))
                if kt == 0:
                    if not at.first():
                        pe.wait_ge(divided, at.n)
                    if at.back(-1).within(STEPS):
                        pe.wait_ge(negated, at.n + 2)
                for hh in range(HG):
                    rows = slice(2 * DH * hh, 2 * DH * (hh + 1))
                    last = nc.tensor.matmul(psO[rows], V[:, at.slot, kt, rows], E[:, kt * HG + hh],
                                            start=kt == 0, stop=kt == TT - 1)
                last.then_inc(weighed, 1)

            def turn_values(at):
                pe.wait_ge(o_copied, at.n + 1)
                for t in range(TT):
                    last = nc.tensor.transpose(psO[:, t * P:(t + 1) * P], O[:, t * P:(t + 1) * P], ident[:])
                last.then_inc(o_turned, 1)

            def step(at):
                m, f, g = at.back(1), at.back(2), at.back(3)
                scoring, turning, finishing, ending = (a.within(STEPS) for a in (at, m, f, g))
                if finishing:
                    pe.wait_ge(max_in[f.slot], 16 * f.uses())
                    rescore(f, 0, 0)
                    rescore(f, 0, 1)
                if ending:
                    weigh(g, TT - 1)
                if scoring:
                    pe.wait_ge(group_in[at.slot], 16 * LOADS * at.uses())
                for i in range(TILE_PAIRS):
                    if finishing and i < TILE_PAIRS - 2:
                        rescore(f, i // 2 + 1, i % 2)
                    if scoring:
                        score(at, i)
                    if ending and i == 1:
                        turn_values(g)
                    if turning and i == 3:
                        turn_maxima(m)
                    if finishing and i >= TILE_PAIRS - TT + 1:
                        weigh(f, i - (TILE_PAIRS - TT + 1))
            run(pe, step)

        @block.scalar
        def _(act):
            act.wait_ge(const_in, 32)
            for r in range(RING):
                nc.scalar.activation(K[KP:KR, r], aux[:], ACT.Copy).then_inc(aux_set, 1)

            def negate(at):
                act.wait_ge(turned, at.n + 1)
                nc.scalar.activation(mrow[:, at.slot], psO[0:HG], ACT.Copy, scale=-1.0).then_inc(negated, 1)

            def copy_values(at):
                act.wait_ge(weighed, TT * (at.n + 1))
                if not at.first():
                    act.wait_ge(o_turned, at.n)
                nc.scalar.activation(O[:], psO[:], ACT.Copy).then_inc(o_copied, 1)

            def step(at):
                m, f, g = at.back(1), at.back(2), at.back(3)
                turning, finishing, ending = (a.within(STEPS) for a in (m, f, g))
                for i in range(NE):
                    if finishing:
                        act.wait_ge(rescored, f.n * NE + (i + 1))
                        if not f.first() and i % HG == 0:
                            act.wait_ge(weighed, f.n * TT - (TT - 1 - i // HG))
                        nc.scalar.activation(E[:, i], psT[:, i % NT], ACT.Exp, scale=DH ** -0.5).then_inc(expd, 1)
                    if ending and i == HG:
                        copy_values(g)
                    if turning and i == NE * 5 // 8:
                        negate(m)
            run(act, step)

        @block.vector
        def _(dve):
            def divide(at):
                dve.wait_ge(o_turned, at.n + 1)
                if not at.first():
                    dve.wait_ge(stored, 16 * at.n)
                o = psO[:].rearrange("p (t h e) -> p t h e", t=TT, h=HG)
                nc.vector.reciprocal(inv[:], o[:, :, :, DH]).then_inc(inverted, 1)
                dve.wait_ge(inverted, at.n + 1)
                nc.vector.tensor_tensor(On[:], o[:, :, :, 0:DH], repeated(inv[:], 3, DH), ALU.mult).then_inc(divided, 1)

            def step(at):
                for i in range(TILE_PAIRS):
                    if at.within(STEPS):
                        qt, pair = divmod(i, 2)
                        dve.wait_ge(scored, at.n * TILE_PAIRS + (i + 1))
                        nc.vector.tensor_reduce(mx[:, at.slot, qt, 2 * pair:2 * pair + 2], psS[:, pair], AX,
                                                ALU.max).then_inc(maxed, 1)
                    if at.back(3).within(STEPS) and i == 1:
                        divide(at.back(3))
            run(dve, step)


class Order:

    def __init__(self, eng, sem, base, per):
        self.eng, self.sem, self.base, self.per, self.n = eng, sem, base, per, 0

    def do(self, ins):
        self.n += 1
        ins.then_inc(self.sem, 1)

    def sync(self, but=0):
        self.eng.wait_ge(self.sem, self.base + (self.n - but))

    def hold(self):
        self.sync()
        self.n += 1
        self.eng.sem_inc(self.sem, 1)

    def close(self):
        assert self.n == self.per, f"{self.n} instructions in order, not {self.per}"


LN_ORDERED = 2 * TT + 1 + 4 + 3 * 3 + TT
MAGIC = float(0x5F3759DF)


def layernorm(nc, o, h, out, st, mv, v, y, t, tiles=TT):
    for i in range(tiles):
        o.do(nc.vector.bn_stats(st[:, i], h[:, i]))
    o.hold()
    for i in range(tiles):
        o.do(nc.vector.bn_aggr(mv[:, i], st[:, i]))
    o.sync()
    o.do(nc.vector.tensor_scalar(v[:, 0], mv[:, :, 1], LN_EPS, None, ALU.add))
    o.sync()
    o.do(nc.vector.tensor_scalar(y.bitcast(I32), v[:, 0].bitcast(I32), 1, None, ALU.arith_shift_right))
    o.do(nc.vector.tensor_scalar(v[:, 1], v[:, 0], -0.5, None, ALU.mult))
    o.sync()
    o.do(nc.vector.tensor_scalar(y.bitcast(I32), y.bitcast(I32), -1.0, MAGIC, ALU.mult, ALU.add))
    o.sync()
    for _ in range(3):
        o.do(nc.vector.tensor_tensor(t, y, y, ALU.mult))
        o.sync()
        o.do(nc.vector.tensor_tensor(t, t, v[:, 1], ALU.mult))
        o.sync()
        o.do(nc.vector.scalar_tensor_tensor(y, t, 1.5, y, ALU.add, ALU.mult))
        o.sync()
    for i in range(tiles):
        o.do(nc.vector.tensor_scalar(out[:, i], h[:, i], mv[:, i, 0:1], y[:, i:i + 1], ALU.subtract, ALU.mult))


CONSTS = {"ident": P, "below": P, "expert": EXPERTS, "page": 3, "slot": TOP_K * TT}
COL = {}
MIX_ORDERED = 164
for _name, _n in CONSTS.items():
    COL[_name] = slice(sum(CONSTS[k] for k in COL), sum(CONSTS[k] for k in COL) + _n)
N_CONST = sum(CONSTS.values())


def mix(nc, consts, wo, wqv, wr, w, cols, rowsb, x, ctx_t, ctx_r, od, pool, pool_filled, x2d, pages_d):
    with ExitStack() as ctx:
        sb = lambda n, s, d=F32: ctx.enter_context(nc.sbuf_tensor(n, s, d))
        sem = lambda n: ctx.enter_context(nc.semaphore(n))
        C = sb("m_c", [P, N_CONST])
        Wo, Wqv, Wr = sb("m_wo", [P, DC, D]), sb("m_wqv", [P, 4 * DC, D]), sb("m_wr", [P, DC, EXPERTS])
        Ws = sb("m_ws", [P, DC * INTER + D])
        Cols = sb("m_cols", [P, DC * 2 + 1])
        Rb = sb("m_rowsb", [P, 2 * D + EXPERTS])
        ones, below = sb("m_ones", [P, P], BF16), sb("m_below", [P, P], BF16)
        ones32, ones_row = sb("m_ones32", [P, P]), sb("m_ones640", [P, TT * EXPERTS])
        O, X = sb("m_o", [P, TT, D]), sb("m_x", [P, TT, D])
        OT = sb("m_ot", [P, DC, S])
        CT, CR = sb("m_ct", [P, DC, S]), sb("m_cr", [P, TT, D])
        H, X1, X1b, X2 = (sb(f"m_{n}", [P, TT, D]) for n in ("h", "x1", "x1b", "x2"))
        X1T, ET, HQ, PR, X2T = (sb(f"m_{n}", [P, DC, S]) for n in ("x1t", "et", "hq", "pr", "x2t"))
        GS, XS = sb("m_gs", [P, S]), sb("m_xs", [P, TT, D])
        A, AT = sb("m_a", [P, TT, S]), sb("m_at", [P, TT, S])
        W1 = sb("m_w1", [P, DC, D])
        st, mv, v = sb("m_st", [P, TT, 6]), sb("m_mv", [P, TT, 2]), sb("m_v", [P, 2, TT])
        y, t4 = sb("m_y", [P, TT]), sb("m_t4", [P, TT])
        dots, nmax, rsum, rinv = (sb(f"m_{n}", [P, TT]) for n in ("dots", "nmax", "rsum", "rinv"))
        u, um, g, ng, eb = sb("m_u", [P, TT]), sb("m_um", [P, 1]), sb("m_g", [1, 1]), sb("m_ng", [P, 1]), sb("m_eb", [P, TT])
        esum, einv, hc = sb("m_esum", [P, 1]), sb("m_einv", [P, 1]), sb("m_hc", [P, DC])
        junk = sb("m_junk", [P, TT, EXPERTS])
        rt = lambda n, d=F32: sb(f"m_{n}", [P, TT, EXPERTS], d)
        lg, pr, rep, need, q, keep, nq, late, key = (rt(n) for n in ("lg", "prob", "rep", "need", "q", "keep", "nq", "late", "key"))
        mask, ri, ni = rt("mask", BF16), rt("ri", I32), rt("ni", I32)
        top, k8, w8 = (sb(f"m_{n}", [P, TT, TOP_K]) for n in ("top", "k8", "w8"))
        tsum = sb("m_tsum", [P, TT])
        place = sb("m_place", [P, TT, TOP_K], U32)
        count, total = sb("m_count", [P, EXPERTS]), sb("m_total", [P, 1])
        npages, cur = sb("m_npages", [P, TT + 1, EXPERTS], I32), sb("m_cur", [P, TT + 1, EXPERTS])
        slots = sb("m_slots", [P, TT, TOP_K])
        et, ptab, ptab_i = sb("m_page_expert", [P, 3]), sb("m_ptab", [P, 3]), sb("m_ptab_i", [P, 4], I32)
        last_page = sb("m_last_page", [P, 1], I32)
        rows = sb("m_rows", [P, TT, TOP_K, ROW])
        ps = ctx.enter_context(nc.psum_tensor("m_ps", [P, 8, S], F32))
        two = lambda n: ps[:, n:n + 2].rearrange("p a (t c) -> p (a t) c", t=2)
        ident = C[:, COL["ident"]]

        const_in = sem("m_const_in")
        o_in, x_in, ct_in, cr_in = sem("m_o_in"), sem("m_x_in"), sem("m_ct_in"), sem("m_cr_in")
        o_turned, ot_done = sem("m_o_turned"), sem("m_ot_done")
        projected, normed, x1_turned, x1t_done, enc_done = (sem(f"m_{n}") for n in ("projected", "normed", "x1_turned", "x1t_done", "enc_done"))
        similar, row_maxed, row_expd, row_scaled, row_turned, at_done = (sem(f"m_{n}") for n in ("similar", "row_maxed", "row_expd", "row_scaled", "row_turned", "at_done"))
        um_done, um_turned, g_done, g_spread, ng_done, eb_done, hc_summed, w1_done = (sem(f"m_{n}") for n in ("um_done", "um_turned", "g_done", "g_spread", "ng_done", "eb_done", "hc_summed", "w1_done"))
        hq_made, hq_done, pr_done, mixed, normed2, x2_turned, x2t_done = (sem(f"m_{n}") for n in ("hq_made", "hq_done", "pr_done", "mixed", "normed2", "x2_turned", "x2t_done"))
        routed, lg_done, pr_made, mask_done, ranked = (sem(f"m_{n}") for n in ("routed", "lg_done", "pr_made", "mask_done", "ranked"))
        rows_copied, rows_done, sent, x2_stored, table_done = (sem(f"m_{n}") for n in ("rows_copied", "rows_done", "sent", "x2_stored", "table_done"))
        shared_gated, shared_silu, shared_made, shared_added = (sem(f"m_shared_{n}") for n in ("gated", "silu", "made", "added"))
        ordered, all_sent, all_stored, table_out = sem("m_ordered"), sem("m_all_sent"), sem("m_all_stored"), sem("m_table_out")
        dispatching, probs_seen = sem("m_dispatching"), sem("m_probs_seen")
        ones_set, below_set, state_set = sem("m_ones_set"), sem("m_below_set"), sem("m_state_set")
        block = ctx.enter_context(nc.Block())

        @block.sync
        def _(sp):
            def load_o(b):
                src = od[bass.ds(b * NG, NG)].rearrange("g p t h e -> p t g (h e)")
                sp.dma_start(O[:].rearrange("p t (g e) -> p t g e", g=NG), src).then_inc(o_in, 16)

            load_o(0)
            sp.dma_start(Wo[:], wo).then_inc(const_in, 16)
            sp.dma_start(X[:], x[0]).then_inc(x_in, 16)
            for dst, src in ((C, consts), (Cols, cols), (Rb, rowsb)):
                sp.dma_start(dst[:], src).then_inc(const_in, 16)
            sp.dma_start(CT[:], ctx_t[0]).then_inc(ct_in, 16)
            sp.dma_start(CR[:], ctx_r[0]).then_inc(cr_in, 16)
            for dst, src in ((Wqv, wqv), (Wr, wr), (Ws, w[EXPERTS])):
                sp.dma_start(dst[:], src).then_inc(const_in, 16)

            def load(b):
                sp.wait_ge(o_turned, b)
                load_o(b)
                sp.wait_ge(normed, b)
                sp.dma_start(X[:], x[bass.ds(b, 1)].rearrange("a p t d -> (a p) t d")).then_inc(x_in, 16)
                sp.wait_ge(similar, TT * b)
                sp.dma_start(CT[:], ctx_t[bass.ds(b, 1)].rearrange("a p c q -> (a p) c q")).then_inc(ct_in, 16)
                sp.wait_ge(hq_made, DC * b)
                sp.dma_start(CR[:], ctx_r[bass.ds(b, 1)].rearrange("a p t d -> (a p) t d")).then_inc(cr_in, 16)

            def store(b):
                sp.wait_ge(shared_added, b + 2)
                sp.dma_start(x2d[bass.ds(b, 1)].rearrange("a p t d -> (a p) t d"), XS[:]).then_inc(x2_stored, 16)
                sp.wait_ge(x2_stored, b * 16 + 16)
                sp.sem_inc(all_stored, 1)

            sp.sem_inc(all_stored, 1)

            with sp.Fori(0, B - 1) as b:
                load(b + 1)
                store(b)
            store(B - 1)
            sp.wait_ge(table_done, 3)
            sp.dma_start(pages_d.rearrange("c p -> p c"), ptab_i[:], allow_slow_non_contiguous=True).then_inc(table_out, 16)
            sp.wait_ge(table_out, 16)

        @block.gpsimd
        def _(pool_eng):
            for tile, value in ((rows, 0.0), (ones, 1.0), (ones32, 1.0), (ones_row, 1.0)):
                nc.gpsimd.memset(tile[:], value).then_inc(ones_set, 1)
            pool_eng.sem_inc(all_sent, 1)
            pool_eng.wait_ge(pool_filled, FILLS * 16)
            with pool_eng.Fori(0, B) as b:
                pool_eng.wait_ge(rows_done, b + 1)
                pool_eng.sem_inc(dispatching, 1)
                for t in range(TT):
                    for k in range(TOP_K):
                        nc.gpsimd.indirect_dma_start(
                            out=pool, out_offset=bass.IndirectOffsetOnAxis(ap=place[:, t, k:k + 1], axis=0),
                            in_=rows[:, t, k], in_offset=None, bounds_check=POOL_PAGES * P - 1,
                            oob_is_err=False).then_inc(sent, 16)
                pool_eng.wait_ge(sent, (b + 1) * (16 * TT * TOP_K))
                pool_eng.sem_inc(all_sent, 1)

        @block.tensor
        def _(pe):
            pe.wait_ge(const_in, 16 * 7)
            pe.wait_ge(ones_set, 4)
            pe.wait_ge(below_set, 1)

            def turn(src, bank, ready, ready_at, done):
                pe.wait_ge(ready, ready_at)
                for t in range(TT):
                    for c in range(DC):
                        last = nc.tensor.transpose(ps[:, bank + c, t * P:(t + 1) * P],
                                                   src[:, t, c * P:(c + 1) * P], ident)
                last.then_inc(done, 1)

            with pe.Fori(0, B) as b:
                tile = lambda t: b * TT + (t + 1)
                pe.wait_ge(shared_added, b + 1)
                turn(O, 6, o_in, b * 16 + 16, o_turned)
                pe.wait_ge(lg_done, b + 1)
                pe.wait_ge(ot_done, b + 1)
                h = two(0)
                for t in range(TT):
                    for c in range(DC):
                        last = nc.tensor.matmul(h[:, t], OT[:, c, t * P:(t + 1) * P], Wo[:, c],
                                                start=c == 0, stop=c == DC - 1)
                    last.then_inc(projected, 1)
                turn(X1, 2, normed, b + 1, x1_turned)
                pe.wait_ge(enc_done, b + 1)
                pe.wait_ge(ct_in, b * 16 + 16)

                def similarity(i):
                    if i >= 2:
                        pe.wait_ge(row_expd, tile(i - 2))
                    for c in range(DC):
                        last = nc.tensor.matmul(ps[:, 4 + i % 2], ET[:, c, i * P:(i + 1) * P], CT[:, c],
                                                start=c == 0, stop=c == DC - 1)
                    last.then_inc(similar, 1)

                def turn_row(i):
                    pe.wait_ge(row_scaled, tile(i))
                    if i >= 2:
                        pe.wait_ge(at_done, tile(i - 2))
                    for j in range(TT):
                        last = nc.tensor.transpose(ps[:, 6 + i % 2, j * P:(j + 1) * P],
                                                   A[:, i, j * P:(j + 1) * P], ident)
                    last.then_inc(row_turned, 1)

                similarity(0)
                similarity(1)
                for i in range(2, TT):
                    similarity(i)
                    turn_row(i - 2)
                pe.wait_ge(um_done, b + 1)
                pe.wait_ge(x1t_done, b + 1)
                nc.tensor.transpose(ps[0:1, 2, 0:P], um[:], ident).then_inc(um_turned, 1)
                turn_row(TT - 2)
                pe.wait_ge(g_done, b + 1)
                nc.tensor.matmul(ps[:, 2, P:P + 1], ones32[0:1, :], g[:], start=True, stop=True).then_inc(g_spread, 1)
                turn_row(TT - 1)
                pe.wait_ge(eb_done, b + 1)
                nc.tensor.matmul(ps[:, 2, 2 * P:2 * P + TT], ones32[:], eb[:], start=True, stop=True)
                for c in range(DC):
                    for t in range(TT):
                        last = nc.tensor.matmul(ps[:, 3, c:c + 1], X1[:, t, c * P:(c + 1) * P], eb[:, t:t + 1],
                                                start=t == 0, stop=t == TT - 1)
                last.then_inc(hc_summed, 1)
                pe.wait_ge(at_done, tile(TT - 1))
                pe.wait_ge(cr_in, b * 16 + 16)
                for c in range(DC):
                    for j in range(TT):
                        last = nc.tensor.matmul(ps[:, c], CR[:, j, c * P:(c + 1) * P], AT[:, j],
                                                start=j == 0, stop=j == TT - 1)
                    last.then_inc(hq_made, 1)
                pe.wait_ge(w1_done, b + 1)
                pe.wait_ge(pr_done, b + 1)
                pe.wait_ge(hq_done, DC * b + DC)
                parts = [(X1T, W1, 0, c) for c in range(DC)] + [(HQ, Wqv, DC, c) for c in range(DC)] + \
                    [(PR, Wqv, 2 * DC, c) for c in range(DC)]
                h = two(4)
                for t in range(TT):
                    for n, (src, W, at, c) in enumerate(parts):
                        last = nc.tensor.matmul(h[:, t], src[:, c, t * P:(t + 1) * P], W[:, at + c],
                                                start=n == 0, stop=n == len(parts) - 1)
                    last.then_inc(mixed, 1)
                turn(X2, 6, normed2, b + 1, x2_turned)
                pe.wait_ge(x2t_done, b + 1)
                lgs = two(0)
                for t in range(TT):
                    for c in range(DC):
                        last = nc.tensor.matmul(lgs[:, t, 0:EXPERTS], X2T[:, c, t * P:(t + 1) * P], Wr[:, c],
                                                start=c == 0, stop=c == DC - 1)
                last.then_inc(routed, 1)
                for c in range(DC):
                    last = nc.tensor.matmul(ps[:, 6], Ws[:, c * INTER:(c + 1) * INTER], X2T[:, c],
                                            start=c == 0, stop=c == DC - 1)
                last.then_inc(shared_gated, 1)
                pe.wait_ge(shared_silu, b + 1)
                out = two(6)
                for t in range(TT):
                    last = nc.tensor.matmul(out[:, t], GS[:, t * P:(t + 1) * P], Ws[:, DC * INTER:], start=True, stop=True)
                last.then_inc(shared_made, 1)
                pe.wait_ge(mask_done, b + 1)
                before, upto = two(2), two(4)
                for t in range(TT):
                    for s in range(t):
                        nc.tensor.matmul(before[:, t, 0:EXPERTS], ones[:], mask[:, s], start=s == 0, stop=False)
                        nc.tensor.matmul(upto[:, t, 0:EXPERTS], ones[:], mask[:, s], start=s == 0, stop=False)
                    nc.tensor.matmul(before[:, t, 0:EXPERTS], below[:], mask[:, t], start=t == 0, stop=True)
                    last = nc.tensor.matmul(upto[:, t, 0:EXPERTS], ones[:], mask[:, t], start=t == 0, stop=True)
                last.then_inc(ranked, 1)

        @block.scalar
        def _(act):
            act.wait_ge(const_in, 16 * 7)
            act.sem_inc(rows_copied, 1)
            nc.scalar.activation(below[:], C[:, COL["below"]], ACT.Copy).then_inc(below_set, 1)
            with act.Fori(0, B) as b:
                tile = lambda t: b * TT + (t + 1)
                act.wait_ge(o_turned, b + 1)
                for c in range(DC):
                    last = nc.scalar.activation(OT[:, c], ps[:, 6 + c], ACT.Copy)
                last.then_inc(ot_done, 1)
                act.wait_ge(x1_turned, b + 1)
                for c in range(DC):
                    last = nc.scalar.activation(X1T[:, c], ps[:, 2 + c], ACT.Copy)
                last.then_inc(x1t_done, 1)
                for i in range(TT):
                    act.wait_ge(row_maxed, tile(i))
                    nc.scalar.activation(A[:, i], ps[:, 4 + i % 2], ACT.Exp, bias=nmax[:, i:i + 1],
                                         accum_out=rsum[:, i:i + 1]).then_inc(row_expd, 1)
                    if i >= 1:
                        act.wait_ge(row_turned, tile(i - 1))
                        nc.scalar.activation(AT[:, :, (i - 1) * P:i * P],
                                             ps[:, 6 + (i - 1) % 2].rearrange("p (j q) -> p j q", j=TT),
                                             ACT.Copy).then_inc(at_done, 1)
                act.wait_ge(ng_done, b + 1)
                nc.scalar.activation(eb[:], u[:], ACT.Exp, bias=ng[:]).then_inc(eb_done, 1)
                act.wait_ge(row_turned, tile(TT - 1))
                nc.scalar.activation(AT[:, :, (TT - 1) * P:], ps[:, 6 + (TT - 1) % 2].rearrange("p (j q) -> p j q", j=TT),
                                     ACT.Copy).then_inc(at_done, 1)
                for c in range(DC):
                    act.wait_ge(hq_made, DC * b + (c + 1))
                    nc.scalar.activation(HQ[:, c], ps[:, c], ACT.Copy).then_inc(hq_done, 1)
                act.wait_ge(x2_turned, b + 1)
                for c in range(DC):
                    last = nc.scalar.activation(X2T[:, c], ps[:, 6 + c], ACT.Copy)
                last.then_inc(x2t_done, 1)
                act.wait_ge(lg_done, b + 2)
                nc.scalar.activation(pr[:], lg[:], ACT.Sigmoid).then_inc(pr_made, 1)
                act.wait_ge(shared_gated, b + 1)
                nc.scalar.activation(GS[:], ps[:, 6], ACT.Silu).then_inc(shared_silu, 1)
                act.wait_ge(all_sent, b + 1)
                for t in range(TT):
                    last = nc.scalar.activation(rows[:, t, :, 0:D], repeated(X2[:, t], 1, TOP_K), ACT.Copy)
                last.then_inc(rows_copied, 1)

        @block.vector
        def _(dve):
            dve.wait_ge(const_in, 16 * 7)
            dve.wait_ge(ones_set, 4)
            nc.vector.tensor_copy(slots[:], C[:, COL["slot"]].rearrange("p (t k) -> p t k", t=TT)).then_inc(state_set, 1)
            for state in (ptab[:], count[:], total[:], cur[:, 0]):
                nc.vector.memset(state, 0.0).then_inc(state_set, 1)
            nc.vector.memset(npages[:, 0], 0).then_inc(state_set, 1)
            dve.wait_ge(state_set, 6)
            dve.sem_inc(lg_done, 1)
            dve.sem_inc(shared_added, 1)
            w1b, bqv, ebias = Rb[:, 0:D], Rb[:, D:2 * D], Rb[:, 2 * D:]
            w2, w3, bsim = Cols[:, 0:DC], Cols[:, DC:2 * DC], Cols[:, 2 * DC:2 * DC + 1]
            flat = lambda a: a.rearrange("p t e -> p (t e)")
            with dve.Fori(0, B) as b:
                tile = lambda t: b * TT + (t + 1)
                o = Order(dve, ordered, b * MIX_ORDERED, MIX_ORDERED)
                do, sync = o.do, o.sync
                dve.wait_ge(x_in, b * 16 + 16)
                for t in range(TT):
                    dve.wait_ge(projected, tile(t | 1))
                    do(nc.vector.tensor_tensor(H[:, t], two(0)[:, t], X[:, t], ALU.add))
                sync()
                layernorm(nc, o, H, X1, st, mv, v, y[:], t4[:])
                sync()
                nc.vector.tensor_tensor(X1b[:], X1[:], repeated(bqv, 1, TT), ALU.add).then_inc(normed, 1)
                for t in range(TT):
                    do(nc.vector.tensor_tensor_reduce(out=junk[:].rearrange("p t e -> p (t e)")[:, 0:D], in0=X1[:, t], in1=w1b, scale=1.0, scalar=0.0,
                                                      op0=ALU.mult, op1=ALU.add, accum_out=dots[:, t:t + 1]))
                    sync()
                dve.wait_ge(x1t_done, b + 1)
                for c in range(DC):
                    last = nc.vector.tensor_scalar(ET[:, c], X1T[:, c], w3[:, c:c + 1], w2[:, c:c + 1],
                                                   ALU.mult, ALU.add)
                last.then_inc(enc_done, 1)

                def scale_row(i):
                    dve.wait_ge(row_expd, tile(i))
                    do(nc.vector.reciprocal(rinv[:, i:i + 1], rsum[:, i:i + 1]))
                    sync()
                    nc.vector.tensor_scalar(A[:, i], A[:, i], rinv[:, i:i + 1], None, ALU.mult).then_inc(row_scaled, 1)

                for i in range(TT):
                    dve.wait_ge(similar, tile(i))
                    nc.vector.tensor_reduce(nmax[:, i:i + 1], ps[:, 4 + i % 2], AX, ALU.max, negate=True).then_inc(row_maxed, 1)
                    if i >= 1:
                        scale_row(i - 1)
                dve.wait_ge(row_maxed, tile(TT - 1))
                do(nc.vector.scalar_tensor_tensor(u[:], nmax[:], -1.0, dots[:], ALU.mult, ALU.add))
                sync()
                do(nc.vector.tensor_scalar(u[:], u[:], bsim, None, ALU.add))
                sync()
                nc.vector.tensor_reduce(um[:], u[:], AX, ALU.max).then_inc(um_done, 1)
                scale_row(TT - 1)
                dve.wait_ge(um_turned, b + 1)
                nc.vector.tensor_reduce(g[:], ps[0:1, 2, 0:P], AX, ALU.max).then_inc(g_done, 1)
                dve.wait_ge(g_spread, b + 1)
                nc.vector.tensor_scalar(ng[:], ps[:, 2, P:P + 1], -1.0, None, ALU.mult).then_inc(ng_done, 1)
                dve.wait_ge(hc_summed, b + 1)
                do(nc.vector.tensor_reduce(esum[:], ps[:, 2, 2 * P:2 * P + TT], AX, ALU.add))
                sync()
                do(nc.vector.reciprocal(einv[:], esum[:]))
                sync()
                do(nc.vector.tensor_scalar(hc[:], ps[:, 3, 0:DC], einv[:], None, ALU.mult))
                sync()
                for c in range(DC):
                    last = nc.vector.scalar_tensor_tensor(W1[:, c], Wqv[:, 3 * DC + c], hc[:, c:c + 1], Wqv[:, c],
                                                          ALU.mult, ALU.add)
                last.then_inc(w1_done, 1)
                for c in range(DC):
                    dve.wait_ge(hq_done, DC * b + (c + 1))
                    last = nc.vector.tensor_tensor(PR[:, c], HQ[:, c], X1T[:, c], ALU.mult)
                last.then_inc(pr_done, 1)
                dve.wait_ge(rows_copied, b + 1)
                for t in range(TT):
                    dve.wait_ge(mixed, tile(t | 1))
                    do(nc.vector.tensor_tensor(H[:, t], two(4)[:, t], X1b[:, t], ALU.add))
                sync()
                layernorm(nc, o, H, X2, st, mv, v, y[:], t4[:])
                sync()
                dve.sem_inc(normed2, 1)
                dve.wait_ge(routed, b + 1)
                for t in range(0, TT, 2):
                    last = nc.vector.tensor_tensor(lg[:, t:t + 2], two(0)[:, t:t + 2, 0:EXPERTS],
                                                   repeated(ebias, 1, 2), ALU.add)
                last.then_inc(lg_done, 1)
                dve.wait_ge(pr_made, b + 1)
                dve.sem_inc(probs_seen, 1)
                for t in range(TT):
                    do(nc.vector.max(top[:, t], pr[:, t]))
                o.hold()
                for t in range(TT):
                    do(nc.vector.match_replace(rep[:, t], top[:, t], pr[:, t], -1.0))
                do(nc.vector.tensor_reduce(tsum[:], top[:], AX, ALU.add))
                sync()
                nc.vector.tensor_tensor(mask[:], pr[:], rep[:], ALU.not_equal).then_inc(mask_done, 1)
                do(nc.vector.tensor_scalar(tsum[:], tsum[:], 1e-9, None, ALU.add))
                sync()
                do(nc.vector.reciprocal(rinv[:], tsum[:]))
                dve.wait_ge(all_stored, b + 1)
                dve.wait_ge(shared_made, b + 1)
                for t in range(0, TT, 2):
                    last = nc.vector.tensor_tensor(XS[:, t:t + 2], two(6)[:, t:t + 2], X2[:, t:t + 2], ALU.add)
                last.then_inc(shared_added, 1)
                dve.wait_ge(ranked, b + 1)
                do(nc.vector.tensor_tensor(ri[:, 0:2], two(2)[:, 0:2, 0:EXPERTS], repeated(count[:], 1, 2), ALU.add))
                do(nc.vector.tensor_tensor(ri[:, 2:4], two(2)[:, 2:4, 0:EXPERTS], repeated(count[:], 1, 2), ALU.add))
                do(nc.vector.scalar_tensor_tensor(ni[:, 0:2], two(4)[:, 0:2, 0:EXPERTS], float(P - 1), repeated(count[:], 1, 2), ALU.add, ALU.add))
                do(nc.vector.scalar_tensor_tensor(ni[:, 2:4], two(4)[:, 2:4, 0:EXPERTS], float(P - 1), repeated(count[:], 1, 2), ALU.add, ALU.add))
                sync()
                do(nc.vector.tensor_tensor(count[:], two(4)[:, TT - 1, 0:EXPERTS], count[:], ALU.add))
                do(nc.vector.tensor_scalar(npages[:, 1:], ni[:], 7, None, ALU.arith_shift_right))
                sync()
                do(nc.vector.tensor_tensor(need[:], npages[:, 1:], npages[:, 0:TT], ALU.subtract))
                do(nc.vector.scalar_tensor_tensor(late[:], npages[:, 0:TT], float(P), ri[:], ALU.mult, ALU.is_le))
                do(nc.vector.tensor_scalar(ri[:], ri[:], P - 1, None, ALU.bitwise_and))
                sync()
                do(nc.vector.tensor_tensor_scan(flat(q[:]), ones_row[:], flat(need[:]), total[:], ALU.mult, ALU.add))
                do(nc.vector.tensor_scalar(keep[:], need[:], -1.0, 1.0, ALU.mult, ALU.add))
                sync()
                do(nc.vector.tensor_scalar(total[:], flat(q[:])[:, TT * EXPERTS - 1:], 1.0, None, ALU.mult))
                do(nc.vector.tensor_copy(npages[:, 0], npages[:, TT]))
                sync()
                do(nc.vector.tensor_tensor(q[:], q[:], need[:], ALU.subtract))
                sync()
                do(nc.vector.tensor_tensor(nq[:], q[:], need[:], ALU.mult))
                sync()
                for t in range(TT):
                    do(nc.vector.tensor_tensor(cur[:, t + 1], cur[:, t], keep[:, t], ALU.mult))
                    sync()
                    do(nc.vector.tensor_tensor(cur[:, t + 1], cur[:, t + 1], nq[:, t], ALU.add))
                    sync()
                do(nc.vector.tensor_tensor(q[:], q[:], cur[:, 0:TT], ALU.subtract))
                do(nc.vector.tensor_tensor(nq[:], nq[:], keep[:], ALU.subtract))
                sync()
                do(nc.vector.tensor_tensor(q[:], q[:], late[:], ALU.mult))
                for c in range(3):
                    do(nc.vector.scalar_tensor_tensor(junk[:], nq[:], C[:, COL["page"]][:, c:c + 1],
                                                      repeated(C[:, COL["expert"]], 1, TT), ALU.is_equal, ALU.mult,
                                                      accum_out=et[:, c:c + 1]))
                    sync()
                do(nc.vector.tensor_tensor(q[:], q[:], cur[:, 0:TT], ALU.add))
                do(nc.vector.tensor_tensor(ptab[:], ptab[:], et[:], ALU.add))
                sync()
                do(nc.vector.tensor_copy(cur[:, 0], cur[:, TT]))
                do(nc.vector.scalar_tensor_tensor(q[:], q[:], float(P), ri[:], ALU.mult, ALU.add))
                sync()
                do(nc.vector.tensor_scalar(key[:], q[:], -1.0, FAR, ALU.mult, ALU.add))
                sync()
                do(nc.vector.tensor_tensor(key[:], key[:], mask[:], ALU.mult))
                o.hold()
                for t in range(TT):
                    do(nc.vector.max(k8[:, t], key[:, t]))
                sync()
                for t in range(TT):
                    for k in range(TOP_K):
                        sync(but=TT - 1)
                        do(nc.vector.scalar_tensor_tensor(junk[:, k % TT], key[:, t], k8[:, t, k:k + 1], pr[:, t],
                                                          ALU.is_equal, ALU.mult, accum_out=w8[:, t, k:k + 1]))
                sync()
                dve.wait_ge(rows_copied, b + 2)
                do(nc.vector.tensor_scalar(place[:], k8[:], -1.0, FAR, ALU.mult, ALU.add))
                do(nc.vector.tensor_copy(rows[:, :, :, DST_COL].bitcast(U32), slots[:]))
                for t in range(TT):
                    do(nc.vector.tensor_scalar(rows[:, t, 0:TOP_K, W_COL], w8[:, t], rinv[:, t:t + 1], ROUTED_SCALE,
                                               ALU.mult, ALU.mult))
                sync()
                dve.sem_inc(rows_done, 1)
                do(nc.vector.tensor_scalar(slots[:], slots[:], float(S * TOP_K), None, ALU.add))
                sync()
                o.close()
            nc.vector.tensor_copy(ptab_i[:, 0:3], ptab[:]).then_inc(table_done, 1)
            nc.vector.tensor_scalar(last_page[:], total[:], -1.0, None, ALU.add).then_inc(table_done, 1)
            dve.wait_ge(table_done, 2)
            nc.vector.tensor_scalar(ptab_i[:, 3:4], last_page[:], ROUND.bit_length() - 1, None,
                                    ALU.arith_shift_right).then_inc(table_done, 1)


def experts(nc, ident_d, w, pages_d, pool, contrib):
    RING, XG = ROUND, 4
    with ExitStack() as ctx:
        sb = lambda n, s, d=F32: ctx.enter_context(nc.sbuf_tensor(n, s, d))
        sem = lambda n: ctx.enter_context(nc.semaphore(n))
        table, ident = sb("e_table", [1, 4 * P], I32), sb("e_ident", [P, P])
        W, X, Y = sb("e_w", [P, RING, DC * INTER + D]), sb("e_x", [P, RING, ROW]), sb("e_y", [P, RING, D])
        tail = sb("e_tail", [P, RING, 2])
        XT, G = sb("e_xt", [P, 2, DC, P]), sb("e_g", [P, 2, P])
        psX, psG, psY = (ctx.enter_context(nc.psum_tensor(f"e_ps{n}", [P, 2, S], F32)) for n in "xgy")
        table_in, ident_in = sem("e_table_in"), sem("e_ident_in")
        w_in = [sem(f"e_w_in{r}") for r in range(RING)]
        x_in = [sem(f"e_x_in{r}") for r in range(RING // XG)]
        sent = [sem(f"e_sent{r}") for r in range(RING)]
        tail_done, turned, xt_done, gated, silu_done, downed, y_done = (
            sem(f"e_{n}") for n in ("tail_done", "turned", "xt_done", "gated", "silu_done", "downed", "y_done"))
        sending, w_loading, x_loading = sem("e_sending"), sem("e_w_loading"), sem("e_x_loading")

        def run(eng, step, drain):
            eng.wait_ge(table_in, 16)
            more = eng.value_load(table[0:1, MORE_AT:MORE_AT + 1], min_val=0, max_val=POOL_PAGES // ROUND - 1)
            for k in range(RING):
                step(At(0, k, RING))
            with eng.Fori(0, POOL_PAGES // ROUND - 1) as i:
                with eng.If(i < more):
                    for k in range(RING, 2 * RING):
                        step(At(i, k, RING))
            for k in range(RING, RING + drain):
                step(Past(more, k, RING))
            return more
        block = ctx.enter_context(nc.Block())

        @block.sync
        def _(sp):
            sp.dma_start(table[:], pages_d.rearrange("(a c) p -> a (c p)", a=1)).then_inc(table_in, 16)
            sp.dma_start(ident[:], ident_d).then_inc(ident_in, 16)

            def step(at):
                if at.k % XG == 0:
                    slots = slice(at.slot, at.slot + XG)
                    if not at.first(RING):
                        sp.wait_ge(turned, at.n - (RING - XG))
                        sp.sem_inc(x_loading, 1)
                        sp.wait_ge(tail_done, at.group(XG) - (RING // XG - 1))
                        sp.sem_inc(x_loading, 1)
                    sp.dma_start(X[:, slots], pool[bass.ds(at.n * P, XG * P)].rearrange("(k p) r -> p k r", p=P)
                                 ).then_inc(x_in[at.slot // XG], 16)
                if not at.first(RING):
                    sp.wait_ge(downed, at.n - (RING - 1))
                    sp.sem_inc(w_loading, 1)
                e = sp.value_load(table[0:1, bass.ds(at.n, 1)], min_val=0, max_val=EXPERTS - 1)
                sp.dma_start(W[:, at.slot], w[bass.ds(e, 1)].rearrange("a p n -> (a p) n")).then_inc(w_in[at.slot], 16)
            run(sp, step, 0)

        @block.tensor
        def _(pe):
            pe.wait_ge(ident_in, 16)

            def step(at):
                if at.within(POOL_PAGES):
                    if at.k % XG == 0:
                        pe.wait_ge(x_in[at.slot // XG], 16 * at.uses())
                    if not at.first(2):
                        pe.wait_ge(xt_done, at.n - 1)
                    for c in range(DC):
                        last = nc.tensor.transpose(psX[:, at.k % 2, c * P:(c + 1) * P],
                                                   X[:, at.slot, c * P:(c + 1) * P], ident[:])
                    last.then_inc(turned, 1)
                f = at.back(1)
                if f.within(POOL_PAGES):
                    pe.wait_ge(w_in[f.slot], 16 * f.uses())
                    pe.wait_ge(xt_done, at.n)
                    if not f.first(2):
                        pe.wait_ge(silu_done, at.n - 2)
                    for c in range(DC):
                        last = nc.tensor.matmul(psG[:, f.k % 2, 0:P], W[:, f.slot, c * INTER:(c + 1) * INTER],
                                                XT[:, f.k % 2, c], start=c == 0, stop=c == DC - 1)
                    last.then_inc(gated, 1)
                f = at.back(2)
                if f.within(POOL_PAGES):
                    pe.wait_ge(silu_done, at.n - 1)
                    if not f.first(2):
                        pe.wait_ge(y_done, at.n - 3)
                    nc.tensor.matmul(psY[:, f.k % 2, 0:D], G[:, f.k % 2], W[:, f.slot, DC * INTER:],
                                     start=True, stop=True).then_inc(downed, 1)
            run(pe, step, 2)

        @block.vector
        def _(dve):
            def step(at):
                if at.k % XG == 0:
                    slots = slice(at.slot, at.slot + XG)
                    dve.wait_ge(x_in[at.slot // XG], 16 * at.uses())
                    if not at.first(RING):
                        for r in range(at.slot, at.slot + XG):
                            dve.wait_ge(sent[r], 16 * (at.uses() - 1))
                    nc.vector.tensor_copy(tail[:, slots], X[:, slots, W_COL:W_COL + 2]).then_inc(tail_done, 1)
                dve.wait_ge(turned, at.n + 1)
                if not at.first(2):
                    dve.wait_ge(gated, at.n - 1)
                nc.vector.tensor_copy(XT[:, at.k % 2], psX[:, at.k % 2, 0:D].rearrange("p (c q) -> p c q", c=DC)
                                      ).then_inc(xt_done, 1)
            run(dve, step, 0)

        @block.scalar
        def _(act):
            def step(at):
                f = at.back(1)
                if f.within(POOL_PAGES):
                    act.wait_ge(gated, at.n)
                    if not f.first(2):
                        act.wait_ge(downed, at.n - 2)
                    nc.scalar.activation(G[:, f.k % 2], psG[:, f.k % 2, 0:P], ACT.Silu).then_inc(silu_done, 1)
                f = at.back(2)
                if f.within(POOL_PAGES):
                    act.wait_ge(downed, at.n - 1)
                    if f.k % XG == 0:
                        act.wait_ge(tail_done, f.group(XG) + 1)
                    if not f.first(RING):
                        act.wait_ge(sent[f.slot], 16 * (f.uses() - 1))
                    nc.scalar.activation(Y[:, f.slot], psY[:, f.k % 2, 0:D], ACT.Copy,
                                         scale=tail[:, f.slot, 0:1]).then_inc(y_done, 1)
            run(act, step, 2)

        @block.gpsimd
        def _(pool_eng):
            def step(at):
                f = at.back(2)
                if f.within(POOL_PAGES):
                    if f.k % XG == 0:
                        pool_eng.wait_ge(tail_done, f.group(XG) + 1)
                    pool_eng.wait_ge(y_done, at.n - 1)
                    pool_eng.sem_inc(sending, 1)
                    nc.gpsimd.indirect_dma_start(
                        out=contrib, out_offset=bass.IndirectOffsetOnAxis(
                            ap=tail[:, f.slot, 1:2].bitcast(U32), axis=0),
                        in_=Y[:, f.slot], in_offset=None, bounds_check=TOKENS * TOP_K - 1,
                        oob_is_err=False).then_inc(sent[f.slot], 16)
            more = run(pool_eng, step, 2)
            for r in range(RING):
                pool_eng.wait_ge(sent[r], more * 16 + 16)


def combine(nc, x2d, contrib, out):
    with ExitStack() as ctx:
        sb = lambda n, s, d=F32: ctx.enter_context(nc.sbuf_tensor(n, s, d))
        sem = lambda n: ctx.enter_context(nc.semaphore(n))
        Cn, X, H, Y = sb("c_c", [P, TT, TOP_K, D]), sb("c_x", [P, TT, D]), sb("c_h", [P, TT, D]), sb("c_y", [P, TT, D])
        st, mv, v = sb("c_st", [P, TT, 6]), sb("c_mv", [P, TT, 2]), sb("c_v", [P, 2, TT])
        y, t4 = sb("c_y4", [P, TT]), sb("c_t4", [P, TT])
        c_in = [sem(f"c_c_in{t}") for t in range(TT)]
        x_in, ordered, reduced, added, normed, stored, out_free = (
            sem(f"c_{n}") for n in ("x_in", "ordered", "reduced", "added", "normed", "stored", "out_free"))
        block = ctx.enter_context(nc.Block())

        @block.sync
        def _(sp):
            def load(b, again):
                for t in range(TT):
                    if again:
                        sp.wait_ge(reduced, b * TT - (TT - 1 - t))
                    src = contrib[bass.ds(b * (S * TOP_K) + t * P * TOP_K, P * TOP_K)]
                    sp.dma_start(Cn[:, t], src.rearrange("(p k) d -> p k d", k=TOP_K)).then_inc(c_in[t], 16)
                if again:
                    sp.wait_ge(added, b)
                sp.dma_start(X[:], x2d[bass.ds(b, 1)].rearrange("a p t d -> (a p) t d")).then_inc(x_in, 16)
            load(0, False)
            with sp.Fori(0, B - 1) as b:
                load(b + 1, True)

        @block.scalar
        def _(act):
            act.sem_inc(out_free, 1)
            with act.Fori(0, B) as b:
                act.wait_ge(normed, b + 1)
                act.dma_start(out[bass.ds(b, 1)].rearrange("a (t p) d -> (a p) t d", p=P), Y[:]).then_inc(stored, 16)
                act.wait_ge(stored, b * 16 + 16)
                act.sem_inc(out_free, 1)

        @block.vector
        def _(dve):
            with dve.Fori(0, B) as b:
                o = Order(dve, ordered, b * (LN_ORDERED + TT), LN_ORDERED + TT)
                for t in range(TT):
                    dve.wait_ge(c_in[t], b * 16 + 16)
                    nc.vector.tensor_reduce(H[:, t], Cn[:, t].rearrange("p k d -> p d k"), AX, ALU.add).then_inc(reduced, 1)
                dve.wait_ge(x_in, b * 16 + 16)
                dve.wait_ge(reduced, b * TT + TT)
                for t in range(TT):
                    o.do(nc.vector.tensor_tensor(H[:, t], H[:, t], X[:, t], ALU.add))
                o.sync()
                dve.sem_inc(added, 1)
                dve.wait_ge(out_free, b + 1)
                layernorm(nc, o, H, Y, st, mv, v, y[:], t4[:])
                o.sync()
                dve.sem_inc(normed, 1)
                o.close()


def decoder_layer(nc, xt, x, ctx_t, ctx_r, wq, wk, wv, wo, wqv, wr, cols, rowsb, w, kaux, consts, out):
    dram = lambda n, s, d=F32: nc.dram_tensor(n, s, d, kind="Internal").ap()
    qd, kd = (dram(n, [STEPS, 2, DH, HG, S]) for n in ("q_parts", "k_parts"))
    vd, od = dram("v_heads", [STEPS, P, TT, HG * 2 * DH]), dram("o_heads", [STEPS, P, TT, HG, DH])
    pool = dram("row_pool", [POOL_PAGES * P, ROW])
    x2d, contrib = dram("tokens", [B, P, TT, D]), dram("contributions", [TOKENS * TOP_K, D])
    pages_d = dram("page_table", [4, P], I32)
    with ExitStack() as ctx:
        fill = ctx.enter_context(nc.sbuf_tensor("fill", [P, ROW], F32))
        pool_filled = ctx.enter_context(nc.semaphore("pool_filled"))
        project(nc, xt, wq, wk, wv, fill, qd, kd, vd)
        attend(nc, consts[:, COL["ident"]], kaux, qd, kd, vd, od, fill, pool, pool_filled)
        mix(nc, consts, wo, wqv, wr, w, cols, rowsb, x, ctx_t, ctx_r, od, pool, pool_filled, x2d, pages_d)
        experts(nc, consts[:, COL["ident"]], w, pages_d, pool, contrib)
        combine(nc, x2d, contrib, out)


def constants(np):
    kaux = np.zeros((32, HG, S), np.float32)
    for h in range(HG):
        kaux[h, h] = 1
    c = np.zeros((P, N_CONST), np.float32)
    p = np.arange(P)
    c[:, COL["ident"]] = np.eye(P)
    c[:, COL["below"]] = np.triu(np.ones((P, P)), 1)
    c[:, COL["expert"]] = np.arange(EXPERTS)
    page = p[:, None] + P * np.arange(3)
    c[:, COL["page"]] = page
    t, k = np.arange(TT), np.arange(TOP_K)
    c[:, COL["slot"]] = ((p[:, None, None] + P * t[:, None]) * TOP_K + k).reshape(P, -1)
    return {"kaux": kaux, "consts": c}


def kernel(**inputs):
    import numpy as np
    import concourse.bacc as bacc
    from concourse.bass_utils import run_bass_kernel_spmd

    I = {k: np.asarray(v) for k, v in inputs.items()}
    turned = lambda a: a.reshape(B, S, DC, P).transpose(0, 3, 2, 1)
    tiled = lambda a: a.reshape(B, TT, P, D).transpose(0, 2, 1, 3)
    chunked = lambda a: a.reshape(-1, P, a.shape[-1]).transpose(1, 0, 2)
    by_step = lambda a: chunked(a.T.reshape(D, DC, 2, HG, DH).transpose(0, 1, 2, 4, 3).reshape(D, D))
    g = lambda n: I["L0_" + n]
    w_sim = g("xattn_w_sim")
    same = lambda a: np.broadcast_to(a, (P, a.size))
    gate = np.concatenate([g("ffn_w_gate"), g("ffn_w_gate_shared")[None]])
    down = np.concatenate([g("ffn_w_down"), g("ffn_w_down_shared")[None]])
    arrays = {
        "xt": turned(I["x"]), "x": tiled(I["x"]),
        "ctx_t": turned(I["ctx_1024"]), "ctx_r": tiled(I["ctx_1024"]),
        "wq": by_step(g("attn_w_q")), "wk": by_step(g("attn_w_k")), "wv": chunked(g("attn_w_v").T),
        "wo": chunked(g("attn_w_o").T), "wqv": chunked(g("xattn_W_qv")),
        "wr": chunked(g("ffn_router_w").T),
        "cols": np.concatenate([w_sim[D:2 * D].reshape(DC, P).T, w_sim[2 * D:].reshape(DC, P).T,
                                np.broadcast_to(g("xattn_b_sim"), (P, 1))], axis=1),
        "rowsb": np.concatenate([same(w_sim[:D]), same(g("xattn_b_qv")), same(g("ffn_expert_bias"))], axis=1),
        "w": np.concatenate([gate.reshape(-1, INTER, DC, P).transpose(0, 3, 2, 1).reshape(-1, P, DC * INTER),
                             down.transpose(0, 2, 1)], axis=2),
        **constants(np),
    }
    arrays = {k: np.ascontiguousarray(v) for k, v in arrays.items()}
    nc = bacc.Bacc("TRN2", target_bir_lowering=False, num_devices=1)
    args = [nc.dram_tensor(k, v.shape, mybir.dt.from_np(v.dtype), kind="ExternalInput").ap() for k, v in arrays.items()]
    out = nc.dram_tensor("out", (B, S, D), F32, kind="ExternalOutput").ap()
    decoder_layer(nc, *args, out)
    return run_bass_kernel_spmd(nc, [arrays], core_ids=[0]).results[0]["out"]
```

```python
from contextlib import ExitStack

import concourse.bass as bass
from concourse import mybir

F32 = mybir.dt.float32
F32R = mybir.dt.float32r
BF16 = mybir.dt.bfloat16
I32 = mybir.dt.int32
U32 = mybir.dt.uint32
ALU = mybir.AluOpType
ACT = mybir.ActivationFunctionType
AX = mybir.AxisListType.X

P = 128
B, S, D = 4, 512, 256
DC = D // P
TT = S // P
HEADS, DH = 16, 16
HG = 4
NG = HEADS // HG
STEPS = B * NG
EXPERTS, TOP_K, INTER = 160, 8, 128
TOKENS = B * S
ROUTED_SCALE = 2.5
PAGES = (TOKENS * TOP_K + EXPERTS * (P - 1)) // P
ROUND = 8
POOL_PAGES = -(-PAGES // ROUND) * ROUND
MORE_AT = 3 * P
W_COL, DST_COL = D, D + 1
ROW = D + 2
FILL_PAGES = 6
FILLS = POOL_PAGES // FILL_PAGES
NOWHERE = 1 << 20
FAR = float(1 << 17)
LN_EPS = 1e-5
RING = 4
KP = 4 * DH
KR = 96


def repeated(ap, at, count):
    shape = list(ap.shape)
    return ap.unsqueeze(at).broadcast_to(shape[:at] + [count] + shape[at:])


def project(nc, xt, wq, wk, wv, kaux, Q, K, zero, fill, qd, kd, vd):
    with ExitStack() as ctx:
        sb = lambda n, s, d=F32: ctx.enter_context(nc.sbuf_tensor(n, s, d))
        sem = lambda n: ctx.enter_context(nc.semaphore(n))
        xT = sb("p_xT", [P, B, DC, S])
        Wq, Wk, Wv = sb("p_wq", [P, DC, D]), sb("p_wk", [P, DC, D]), sb("p_wv", [P, DC, D])
        hi, lo = sb("p_hi", [P, 2, 4, S], F32R), sb("p_lo", [P, 2, 4, S], F32R)
        V = sb("p_v", [P, 2, TT, HEADS, 2 * DH])
        ps = ctx.enter_context(nc.psum_tensor("p_ps", [P, 8, S], F32))
        aux = sb("p_aux", [KR - KP, HG, S])
        aux_in, aux_set = sem("p_aux_in"), sem("p_aux_set")
        x_in = [sem(f"p_x_in{b}") for b in range(B)]
        w_in = [sem(f"p_w_in_{n}") for n in "qkv"]
        v_ones, fill_zero = sem("p_v_ones"), sem("p_fill_zero")
        qk_made, v_made = sem("p_qk_made"), sem("p_v_made")
        hi_done, lo_done, v_done = sem("p_hi_done"), sem("p_lo_done"), sem("p_v_done")
        stored = [sem(f"p_stored{u}") for u in range(2)]
        STORES = 8 + 1
        block = ctx.enter_context(nc.Block())

        @block.sync
        def _(sp):
            sp.dma_start(Wq[:], wq).then_inc(w_in[0], 16)
            sp.dma_start(xT[:, 0], xt[0]).then_inc(x_in[0], 16)
            sp.dma_start(Wk[:], wk).then_inc(w_in[1], 16)
            sp.dma_start(Wv[:], wv).then_inc(w_in[2], 16)
            for b in range(1, B):
                sp.dma_start(xT[:, b], xt[b]).then_inc(x_in[b], 16)
            sp.dma_start(aux[:], kaux).then_inc(aux_in, 16)
            for b in range(B):
                u = b % 2
                sp.wait_ge(lo_done, 4 * (b + 1))
                for part, src in enumerate((hi, lo)):
                    for half in range(2):
                        for w, dst in enumerate((qd, kd)):
                            to = dst[:, part].rearrange("(b j g) e h q -> b g (e h) j q", b=B, g=2)[b, half]
                            rows = slice(P // 2 * half, P // 2 * (half + 1))
                            sp.dma_start(to, src[rows, u, 2 * w:2 * w + 2].bitcast(F32)).then_inc(stored[u], 16)
                sp.wait_ge(v_done, TT * (b + 1))
                sp.dma_start(vd.rearrange("(b g) p t e -> b p t g e", b=B)[b],
                             V[:, u].rearrange("p t (g h) e -> p t g (h e)", g=NG)).then_inc(stored[u], 16)
            for u in range(2):
                sp.wait_ge(stored[u], 16 * STORES * (B // 2))

        @block.gpsimd
        def _(pool_eng):
            nc.gpsimd.memset(V[:], 1.0).then_inc(v_ones, 1)
            nc.gpsimd.memset(fill[:], 0.0).then_inc(fill_zero, 1)
            pool_eng.wait_ge(fill_zero, 1)
            nc.gpsimd.memset(fill[:, DST_COL:DST_COL + 1].bitcast(I32), NOWHERE).then_inc(fill_zero, 1)
            pool_eng.wait_ge(fill_zero, 2)
            nc.gpsimd.memset(Q[KP:KR].bitcast(F32), 0.0).then_inc(fill_zero, 1)
            pool_eng.wait_ge(fill_zero, 3)
            nc.gpsimd.memset(zero[:], 0.0).then_inc(fill_zero, 1)
            pool_eng.wait_ge(fill_zero, 4)

        @block.tensor
        def _(pe):
            for b in range(B):
                pe.wait_ge(x_in[b], 16)
                for n, (W, j) in enumerate(((Wq, 0), (Wq, 1), (Wk, 0), (Wk, 1))):
                    pe.wait_ge(w_in[n // 2], 16)
                    if b >= 1:
                        pe.wait_ge(lo_done, 4 * (b - 1) + n + 1)
                    for c in range(DC):
                        last = nc.tensor.matmul(ps[:, n], W[:, c, j * P:(j + 1) * P], xT[:, b, c],
                                                start=c == 0, stop=c == DC - 1)
                    last.then_inc(qk_made, 1)
                pe.wait_ge(w_in[2], 16)
                for t in range(TT):
                    if b >= 1:
                        pe.wait_ge(v_done, TT * (b - 1) + t + 1)
                    for c in range(DC):
                        last = nc.tensor.matmul(ps[:, 4 + t, 0:D], xT[:, b, c, t * P:(t + 1) * P], Wv[:, c],
                                                start=c == 0, stop=c == DC - 1)
                    last.then_inc(v_made, 1)

        @block.scalar
        def _(act):
            act.wait_ge(v_ones, 1)
            for b in range(B):
                u = b % 2
                if b >= 2:
                    act.wait_ge(stored[u], 16 * STORES * (b // 2))
                for n in range(4):
                    act.wait_ge(qk_made, 4 * b + n + 1)
                    nc.scalar.activation(hi[:, u, n], ps[:, n], ACT.Copy).then_inc(hi_done, 1)
                for t in range(TT):
                    act.wait_ge(v_made, TT * b + t + 1)
                    nc.scalar.activation(V[:, u, t, :, 0:DH],
                                         ps[:, 4 + t, 0:D].rearrange("p (h e) -> p h e", h=HEADS),
                                         ACT.Copy).then_inc(v_done, 1)
                if b == 0:
                    act.wait_ge(aux_in, 16)
                nc.scalar.activation(K[KP:KR, b], aux[:], ACT.Copy).then_inc(aux_set, 1)
            act.wait_ge(aux_set, RING)

        @block.vector
        def _(dve):
            for b in range(B):
                u = b % 2
                if b >= 2:
                    dve.wait_ge(stored[u], 16 * STORES * (b // 2))
                for n in range(4):
                    dve.wait_ge(hi_done, 4 * b + n + 1)
                    nc.vector.tensor_tensor(lo[:, u, n], ps[:, n], hi[:, u, n].bitcast(F32),
                                            ALU.subtract).then_inc(lo_done, 1)


class At:

    def __init__(self, i, k, ring):
        self.i, self.k, self.ring = i, k, ring
        self.n = i * ring + k
        self.slot = k % ring
        self.fixed = isinstance(i, int)

    def back(self, by):
        return At(self.i, self.k - by, self.ring)

    def group(self, count):
        return self.i * (self.ring // count) + self.k // count

    def uses(self):
        return self.i + (self.k // self.ring + 1)

    def within(self, count):
        return not self.fixed or 0 <= self.n < count

    def first(self, count=1):
        return self.fixed and self.n < count


class Past(At):

    def __init__(self, i, k, ring):
        super().__init__(i, k, ring)
        self.fixed = False

    def within(self, count):
        return self.k < self.ring

    def back(self, by):
        return Past(self.i, self.k - by, self.ring)


def run_steps(eng, step, ring, first, rounds, last):
    for n in range(first):
        step(At(0, n, ring))
    with eng.Fori(0, rounds) as i:
        for k in range(first, first + ring):
            step(At(i, k, ring))
    for n in range(first + rounds * ring, last):
        step(At(0, n, ring))


def attend(nc, ident_d, Q, K, zero, qd, kd, vd, od, fill, pool, pool_filled, prefetch):
    NE = TT * HG
    NT = 3
    TILE_PAIRS = TT * HG // 2
    with ExitStack() as ctx:
        sb = lambda n, s, d=F32: ctx.enter_context(nc.sbuf_tensor(n, s, d))
        sem = lambda n: ctx.enter_context(nc.semaphore(n))
        V = sb("a_v", [P, RING, TT, HG * 2 * DH])
        mrow = sb("a_mrow", [HG, RING, S])
        mx = sb("a_mx", [P, RING, TT, HG])
        ident = sb("a_ident", [P, P])
        E = sb("a_e", [P, NE, S])
        O, On, inv = sb("a_o", [P, S]), sb("a_on", [P, TT, HG, DH]), sb("a_inv", [P, TT, HG])
        psS = ctx.enter_context(nc.psum_tensor("a_psS", [P, 2, 2, S], F32))
        psT = ctx.enter_context(nc.psum_tensor("a_psT", [P, NT, S], F32))
        psO = ctx.enter_context(nc.psum_tensor("a_psO", [P, S], F32))
        const_in = sem("a_const_in")
        group_in = [sem(f"a_group_in{r}") for r in range(RING)]
        max_in = [sem(f"a_max_in{r}") for r in range(RING)]
        scored, maxed, turned, negated = sem("a_scored"), sem("a_maxed"), sem("a_turned"), sem("a_negated")
        rescored, expd, weighed = sem("a_rescored"), sem("a_expd"), sem("a_weighed")
        o_copied, o_turned, divided, stored = sem("a_o_copied"), sem("a_o_turned"), sem("a_divided"), sem("a_stored")
        inverted = sem("a_inverted")
        LOADS = 7
        run = lambda eng, step: run_steps(eng, step, RING, RING, (STEPS - RING) // RING - 1, STEPS + 3)
        block = ctx.enter_context(nc.Block())

        @block.sync
        def _(sp):
            sp.dma_start(ident[:], ident_d).then_inc(const_in, 16)

            def load(at):
                if not at.first(RING):
                    sp.wait_ge(weighed, TT * (at.n - (RING - 1)))
                rows = lambda a, s0, s1: a[bass.ds(at.n, 1), s0:s1].rearrange("a s e h q -> (a s e) h q")
                Qf, Kf, here = Q[:, at.slot].bitcast(F32), K[:, at.slot].bitcast(F32), group_in[at.slot]
                sp.dma_start(Qf[0:2 * DH], rows(qd, 0, 2)).then_inc(here, 16)
                sp.dma_start(Qf[2 * DH:3 * DH], rows(qd, 1, 2)).then_inc(here, 16)
                sp.dma_start(Qf[3 * DH:KP], rows(qd, 0, 1)).then_inc(here, 16)
                sp.dma_start(Kf[0:2 * DH], rows(kd, 0, 2)).then_inc(here, 16)
                sp.dma_start(Kf[2 * DH:KP], rows(kd, 0, 2)).then_inc(here, 16)
                sp.dma_start(Qf[KP:KP + HG], zero[:]).then_inc(here, 16)
                sp.dma_start(V[:, at.slot], vd[bass.ds(at.n, 1)].rearrange("a p t e -> (a p) t e")).then_inc(here, 16)

            load(At(0, 0, RING))

            def step(at):
                if at.back(-1).within(STEPS):
                    load(at.back(-1))
                if at.back(3).within(STEPS):
                    sp.wait_ge(divided, at.n - 2)
                    g = at.back(3)
                    cols = slice(g.slot * HG * DH, (g.slot + 1) * HG * DH)
                    sp.dma_start(od[bass.ds(g.uses() - 1, 1), :, :, cols].rearrange("a p t e -> (a p) t e"),
                                 On[:].rearrange("p t h e -> p t (h e)")).then_inc(stored, 16)
                if at.back(1).within(STEPS):
                    sp.wait_ge(negated, at.n)
                    slot = at.back(1).slot
                    sp.dma_start(Q[KP:KP + HG, slot].bitcast(F32),
                                 repeated(mrow[:, slot], 1, HG)).then_inc(max_in[slot], 16)
                if at.within(STEPS):
                    for i in range(FILLS // STEPS):
                        row = (at.n * (FILLS // STEPS) + i) * (FILL_PAGES * P)
                        sp.dma_start(pool[bass.ds(row, FILL_PAGES * P)].rearrange("(k p) r -> p k r", p=P),
                                     repeated(fill[:], 1, FILL_PAGES)).then_inc(pool_filled, 16)
                if at.fixed and at.n == STEPS:
                    prefetch(sp)
            run(sp, step)
            sp.wait_ge(stored, 16 * STEPS)

        @block.tensor
        def _(pe):
            pe.wait_ge(const_in, 16)

            def score(at, i):
                qt, pair = divmod(i, 2)
                if not (at.first() and i < 2):
                    pe.wait_ge(maxed, at.n * TILE_PAIRS + (i - 1))
                for h in range(2):
                    hh = 2 * pair + h
                    last = nc.tensor.matmul(psS[:, pair, h], Q[0:KR, at.slot, hh, qt * P:(qt + 1) * P],
                                            K[0:KR, at.slot, hh], start=True, stop=True)
                last.then_inc(scored, 1)

            def turn_maxima(at):
                pe.wait_ge(maxed, TILE_PAIRS * (at.n + 1))
                if not at.first():
                    pe.wait_ge(negated, at.n)
                if at.back(2).within(STEPS):
                    pe.wait_ge(divided, at.n - 1)
                for qt in range(TT):
                    last = nc.tensor.transpose(psO[0:HG, qt * P:(qt + 1) * P], mx[:, at.slot, qt], ident[:])
                last.then_inc(turned, 1)

            def rescore(at, kt, half):
                for i in (kt * HG + 2 * half, kt * HG + 2 * half + 1):
                    if i >= NT:
                        pe.wait_ge(expd, at.n * NE + (i - NT + 1))
                    elif i == 0 and not at.first():
                        pe.wait_ge(expd, at.n * NE)
                    nc.tensor.matmul(psT[:, i % NT], K[0:KR, at.slot, i % HG, kt * P:(kt + 1) * P],
                                     Q[0:KR, at.slot, i % HG], start=True, stop=True).then_inc(rescored, 1)

            def weigh(at, kt):
                pe.wait_ge(expd, at.n * NE + HG * (kt + 1))
                if kt == 0:
                    if not at.first():
                        pe.wait_ge(divided, at.n)
                    if at.back(-1).within(STEPS):
                        pe.wait_ge(negated, at.n + 2)
                for hh in range(HG):
                    rows = slice(2 * DH * hh, 2 * DH * (hh + 1))
                    last = nc.tensor.matmul(psO[rows], V[:, at.slot, kt, rows], E[:, kt * HG + hh],
                                            start=kt == 0, stop=kt == TT - 1)
                last.then_inc(weighed, 1)

            def turn_values(at):
                pe.wait_ge(o_copied, at.n + 1)
                for t in range(TT):
                    last = nc.tensor.transpose(psO[:, t * P:(t + 1) * P], O[:, t * P:(t + 1) * P], ident[:])
                last.then_inc(o_turned, 1)

            def step(at):
                m, f, g = at.back(1), at.back(2), at.back(3)
                scoring, turning, finishing, ending = (a.within(STEPS) for a in (at, m, f, g))
                if finishing:
                    pe.wait_ge(max_in[f.slot], 16 * f.uses())
                    rescore(f, 0, 0)
                    rescore(f, 0, 1)
                if ending:
                    weigh(g, TT - 1)
                if scoring:
                    pe.wait_ge(group_in[at.slot], 16 * LOADS * at.uses())
                for i in range(TILE_PAIRS):
                    if finishing and i < TILE_PAIRS - 2:
                        rescore(f, i // 2 + 1, i % 2)
                    if scoring:
                        score(at, i)
                    if ending and i == 1:
                        turn_values(g)
                    if turning and i == 3:
                        turn_maxima(m)
                    if finishing and i >= TILE_PAIRS - TT + 1:
                        weigh(f, i - (TILE_PAIRS - TT + 1))
            run(pe, step)

        @block.scalar
        def _(act):
            def negate(at):
                act.wait_ge(turned, at.n + 1)
                nc.scalar.activation(mrow[:, at.slot], psO[0:HG], ACT.Copy, scale=-1.0).then_inc(negated, 1)

            def copy_values(at):
                act.wait_ge(weighed, TT * (at.n + 1))
                if not at.first():
                    act.wait_ge(o_turned, at.n)
                nc.scalar.activation(O[:], psO[:], ACT.Copy).then_inc(o_copied, 1)

            def step(at):
                m, f, g = at.back(1), at.back(2), at.back(3)
                turning, finishing, ending = (a.within(STEPS) for a in (m, f, g))
                for i in range(NE):
                    if finishing:
                        act.wait_ge(rescored, f.n * NE + (i + 1))
                        if not f.first() and i % HG == 0:
                            act.wait_ge(weighed, f.n * TT - (TT - 1 - i // HG))
                        nc.scalar.activation(E[:, i], psT[:, i % NT], ACT.Exp, scale=DH ** -0.5).then_inc(expd, 1)
                    if ending and i == HG:
                        copy_values(g)
                    if turning and i == NE * 5 // 8:
                        negate(m)
            run(act, step)

        @block.vector
        def _(dve):
            def divide(at):
                dve.wait_ge(o_turned, at.n + 1)
                if not at.first():
                    dve.wait_ge(stored, 16 * at.n)
                o = psO[:].rearrange("p (t h e) -> p t h e", t=TT, h=HG)
                nc.vector.reciprocal(inv[:], o[:, :, :, DH]).then_inc(inverted, 1)
                dve.wait_ge(inverted, at.n + 1)
                nc.vector.tensor_tensor(On[:], o[:, :, :, 0:DH], repeated(inv[:], 3, DH), ALU.mult).then_inc(divided, 1)

            def step(at):
                for i in range(TILE_PAIRS):
                    if at.within(STEPS):
                        qt, pair = divmod(i, 2)
                        dve.wait_ge(scored, at.n * TILE_PAIRS + (i + 1))
                        nc.vector.tensor_reduce(mx[:, at.slot, qt, 2 * pair:2 * pair + 2], psS[:, pair], AX,
                                                ALU.max).then_inc(maxed, 1)
                    if at.back(3).within(STEPS) and i == 1:
                        divide(at.back(3))
            run(dve, step)


class Order:

    def __init__(self, eng, sem, base, per):
        self.eng, self.sem, self.base, self.per, self.n = eng, sem, base, per, 0

    def do(self, ins):
        self.n += 1
        ins.then_inc(self.sem, 1)

    def sync(self, but=0):
        self.eng.wait_ge(self.sem, self.base + (self.n - but))

    def hold(self):
        self.sync()
        self.n += 1
        self.eng.sem_inc(self.sem, 1)

    def close(self):
        assert self.n == self.per, f"{self.n} instructions in order, not {self.per}"


START_ORDERED, ONE_ORDERED, TWO_ORDERED = 28, 56, 97
LN_ORDERED = 2 * TT + 1 + 4 + 3 * 3 + 1
MAGIC = float(0x5F3759DF)


def statistics(nc, o, h, st, mv, v, y, shift, t, ready):
    y, shift = y[:, 0:TT], shift[:, 0:TT]
    for i in range(TT):
        ready(i)
        o.do(nc.vector.bn_stats(st[:, i], h[:, i]))
    o.hold()
    for i in range(TT):
        o.do(nc.vector.bn_aggr(mv[:, i], st[:, i]))
    o.sync()
    o.do(nc.vector.tensor_scalar(v[:, 0], mv[:, :, 1], LN_EPS, None, ALU.add))
    o.sync()
    o.do(nc.vector.tensor_scalar(y.bitcast(I32), v[:, 0].bitcast(I32), 1, None, ALU.arith_shift_right))
    o.do(nc.vector.tensor_scalar(v[:, 1], v[:, 0], -0.5, None, ALU.mult))
    o.sync()
    o.do(nc.vector.tensor_scalar(y.bitcast(I32), y.bitcast(I32), -1.0, MAGIC, ALU.mult, ALU.add))
    o.sync()
    for _ in range(3):
        o.do(nc.vector.tensor_tensor(t, y, y, ALU.mult))
        o.sync()
        o.do(nc.vector.tensor_tensor(t, t, v[:, 1], ALU.mult))
        o.sync()
        o.do(nc.vector.scalar_tensor_tensor(y, t, 1.5, y, ALU.add, ALU.mult))
        o.sync()
    o.do(nc.vector.scalar_tensor_tensor(shift, mv[:, :, 0], -1.0, y, ALU.mult, ALU.mult))
    o.sync()


def normalize(nc, out, h, y, shift, done):
    for i in range(TT):
        nc.scalar.activation(out[:, i], h[:, i], ACT.Identity, scale=y[:, i:i + 1],
                             bias=shift[:, i:i + 1]).then_inc(done, 1)


CONSTS = {"ident": P, "below": P, "expert": EXPERTS, "page": 3, "slot": TOP_K * TT}
COL = {}
for _name, _n in CONSTS.items():
    COL[_name] = slice(sum(CONSTS[k] for k in COL), sum(CONSTS[k] for k in COL) + _n)
N_CONST = sum(CONSTS.values())


class MixInputs:

    def __init__(self, nc, ctx, consts, wo, wqv, wr, w, cols, rowsb, x, ctx_t, ctx_r):
        sb = lambda n, s: ctx.enter_context(nc.sbuf_tensor(n, s, F32))
        self.C, self.Wo, self.Wqv = sb("m_c", [P, N_CONST]), sb("m_wo", [P, DC, D]), sb("m_wqv", [P, 4 * DC, D])
        self.Wr = sb("m_wr", [P, DC, EXPERTS])
        self.Ws = sb("m_ws", [P, DC * INTER + D])
        self.Cols = sb("m_cols", [P, DC * 2 + 1])
        self.Rb = sb("m_rowsb", [P, 2 * D + EXPERTS])
        self.X, self.CT, self.CR = sb("m_x", [P, TT, D]), sb("m_ct", [P, DC, S]), sb("m_cr", [P, TT, D])
        self.const_in, self.weights_in, self.x_in, self.ct_in, self.cr_in = (
            ctx.enter_context(nc.semaphore(f"m_{n}")) for n in ("const_in", "weights_in", "x_in", "ct_in", "cr_in"))
        self.sources = consts, wo, wqv, wr, w, cols, rowsb, x, ctx_t, ctx_r

    def load(self, sp):
        consts, wo, wqv, wr, w, cols, rowsb, x, ctx_t, ctx_r = self.sources
        for dst, src in ((self.C, consts), (self.Wo, wo), (self.Cols, cols), (self.Rb, rowsb)):
            sp.dma_start(dst[:], src).then_inc(self.const_in, 16)
        sp.dma_start(self.X[:], x[0]).then_inc(self.x_in, 16)
        sp.dma_start(self.CT[:], ctx_t[0]).then_inc(self.ct_in, 16)
        sp.dma_start(self.CR[:], ctx_r[0]).then_inc(self.cr_in, 16)
        for dst, src in ((self.Wqv, wqv), (self.Wr, wr), (self.Ws, w[EXPERTS])):
            sp.dma_start(dst[:], src).then_inc(self.weights_in, 16)


def mix(nc, inputs, x, ctx_t, ctx_r, od, rows, place, dispatch, last_sent, pool_filled, x2d, pages_d):
    with ExitStack() as ctx:
        sb = lambda n, s, d=F32: ctx.enter_context(nc.sbuf_tensor(n, s, d))
        sem = lambda n: ctx.enter_context(nc.semaphore(n))
        C, Wo, Wqv, Wr, Ws, Cols, Rb = (
            inputs.C, inputs.Wo, inputs.Wqv, inputs.Wr, inputs.Ws, inputs.Cols, inputs.Rb)
        X, CT, CR = inputs.X, inputs.CT, inputs.CR
        const_in, weights_in, x_in, ct_in, cr_in = (
            inputs.const_in, inputs.weights_in, inputs.x_in, inputs.ct_in, inputs.cr_in)
        ones, below = sb("m_ones", [P, P], BF16), sb("m_below", [P, P], BF16)
        ones32, ones_row = sb("m_ones32", [P, P]), sb("m_ones640", [P, TT * EXPERTS])
        O = sb("m_o", [P, TT, D])
        OT = sb("m_ot", [P, DC, S])
        X1, X1b, X2 = (sb(f"m_{n}", [P, TT, D]) for n in ("x1", "x1b", "x2"))
        X1T, ET, HQ, PR, X2T = (sb(f"m_{n}", [P, DC, S]) for n in ("x1t", "et", "hq", "pr", "x2t"))
        GS, XS = sb("m_gs", [P, S]), sb("m_xs", [P, TT, D])
        A, AT = sb("m_a", [P, TT, S]), sb("m_at", [P, TT, S])
        W1 = sb("m_w1", [P, DC, D])
        st, mv, v, t4 = sb("m_st", [P, TT, 6]), sb("m_mv", [P, TT, 2]), sb("m_v", [P, 2, TT]), sb("m_t4", [P, TT])
        y, shift = sb("m_y", [P, 2 * TT]), sb("m_shift", [P, 2 * TT])
        dots, nmax, rsum, rinv, winv = (sb(f"m_{n}", [P, TT]) for n in ("dots", "nmax", "rsum", "rinv", "winv"))
        u, um, g, ng, eb = sb("m_u", [P, TT]), sb("m_um", [P, 1]), sb("m_g", [1, 1]), sb("m_ng", [P, 1]), sb("m_eb", [P, TT])
        esum, einv, hc = sb("m_esum", [P, 1]), sb("m_einv", [P, 1]), sb("m_hc", [P, DC])
        junk1, junk = sb("m_junk1", [P, D]), sb("m_junk", [P, TT, EXPERTS])
        rt = lambda n, d=F32: sb(f"m_{n}", [P, TT, EXPERTS], d)
        lg, pr, rep, need, q, keep, nq, late, key = (rt(n) for n in ("lg", "prob", "rep", "need", "q", "keep", "nq", "late", "key"))
        prw = rt("prob_weights")
        mask, ri, ni = rt("mask", BF16), rt("ri", I32), rt("ni", I32)
        top, k8, w8 = (sb(f"m_{n}", [P, TT, TOP_K]) for n in ("top", "k8", "w8"))
        tsum = sb("m_tsum", [P, TT])
        count, total = sb("m_count", [P, EXPERTS]), sb("m_total", [P, 1])
        npages, cur = sb("m_npages", [P, TT + 1, EXPERTS], I32), sb("m_cur", [P, TT + 1, EXPERTS])
        slots = sb("m_slots", [P, TT, TOP_K])
        et, ptab, ptab_i = sb("m_page_expert", [P, 3]), sb("m_ptab", [P, 3]), sb("m_ptab_i", [P, 4], I32)
        last_page = sb("m_last_page", [P, 1], I32)
        ps = ctx.enter_context(nc.psum_tensor("m_ps", [P, 8, S], F32))
        two = lambda n: ps[:, n:n + 2].rearrange("p a (t c) -> p (a t) c", t=2)
        ident = C[:, COL["ident"]]

        o_in = sem("m_o_in")
        o_turned, ot_done = sem("m_o_turned"), sem("m_ot_done")
        projected, measured, normed, x1_turned, x1t_done = (sem(f"m_{n}") for n in ("projected", "measured", "normed", "x1_turned", "x1t_done"))
        similar, row_maxed, row_expd, row_inverted, row_scaled, row_turned, at_done = (sem(f"m_{n}") for n in ("similar", "row_maxed", "row_expd", "row_inverted", "row_scaled", "row_turned", "at_done"))
        um_done, um_turned, g_done, g_spread, ng_done, eb_done, hc_summed, w1_done = (sem(f"m_{n}") for n in ("um_done", "um_turned", "g_done", "g_spread", "ng_done", "eb_done", "hc_summed", "w1_done"))
        hq_made, hq_done, pr_done, mixed, measured2, normed2, x2_turned, x2t_done = (sem(f"m_{n}") for n in ("hq_made", "hq_done", "pr_done", "mixed", "measured2", "normed2", "x2_turned", "x2t_done"))
        routed, lg_done, pr_made, pr_copied, mask_done, ranked, ranks_read = (sem(f"m_{n}") for n in ("routed", "lg_done", "pr_made", "pr_copied", "mask_done", "ranked", "ranks_read"))
        rows_copied, rows_done, sent, x2_stored, table_done = (sem(f"m_{n}") for n in ("rows_copied", "rows_done", "sent", "x2_stored", "table_done"))
        shared_gated, shared_sigmoid, shared_silu, shared_made, shared_added = (
            sem(f"m_shared_{n}") for n in ("gated", "sigmoid", "silu", "made", "added"))
        ordered1, ordered2 = sem("m_ordered1"), sem("m_ordered2")
        all_sent, all_stored, table_out = sem("m_all_sent"), sem("m_all_stored"), sem("m_table_out")
        dispatching, probs_seen = sem("m_dispatching"), sem("m_probs_seen")
        ones_set, below_set, state_set = sem("m_ones_set"), sem("m_below_set"), sem("m_state_set")
        block = ctx.enter_context(nc.Block())

        def run(eng, start, step):
            start(0)
            step(0, True, False, True)
            with eng.Fori(1, B - 1) as n:
                step(n, True, True, True)
            step(B - 1, True, True, False)
            step(B, False, True, False)

        @block.sync
        def _(sp):
            def load_o(b):
                sp.dma_start(O[:], od[bass.ds(b, 1)].rearrange("a p t d -> (a p) t d")).then_inc(o_in, 16)

            load_o(0)

            def load_a(b):
                sp.wait_ge(o_turned, b)
                load_o(b)
                sp.wait_ge(projected, TT * b)
                sp.dma_start(X[:], x[bass.ds(b, 1)].rearrange("a p t d -> (a p) t d")).then_inc(x_in, 16)

            def load_b(b):
                sp.wait_ge(similar, TT * b)
                sp.dma_start(CT[:], ctx_t[bass.ds(b, 1)].rearrange("a p c q -> (a p) c q")).then_inc(ct_in, 16)
                sp.wait_ge(hq_made, DC * b)
                sp.dma_start(CR[:], ctx_r[bass.ds(b, 1)].rearrange("a p t d -> (a p) t d")).then_inc(cr_in, 16)

            def store(b):
                sp.wait_ge(shared_added, b + 1)
                sp.dma_start(x2d[bass.ds(b, 1)].rearrange("a p t d -> (a p) t d"), XS[:]).then_inc(x2_stored, 16)
                sp.wait_ge(x2_stored, b * 16 + 16)
                sp.sem_inc(all_stored, 1)

            sp.sem_inc(all_stored, 1)
            load_a(1)
            with sp.Fori(0, B - 2) as n:
                load_b(n + 1)
                load_a(n + 2)
                store(n)
            load_b(B - 1)
            store(B - 2)
            store(B - 1)
            sp.wait_ge(table_done, 3)
            sp.dma_start(pages_d.rearrange("c p -> p c"), ptab_i[:], allow_slow_non_contiguous=True).then_inc(table_out, 16)
            sp.wait_ge(table_out, 16)

        @block.gpsimd
        def _(pool_eng):
            for tile in (ones, ones32, ones_row):
                nc.gpsimd.memset(tile[:], 1.0).then_inc(ones_set, 1)
            pool_eng.sem_inc(all_sent, 1)
            pool_eng.wait_ge(pool_filled, FILLS * 16)
            with pool_eng.Fori(0, B - 1) as b:
                for t in range(TT):
                    pool_eng.wait_ge(rows_done, b * TT + (t + 1))
                    pool_eng.sem_inc(dispatching, 1)
                    dispatch(t, sent)
                pool_eng.wait_ge(sent, (b + 1) * (16 * TT * TOP_K))
                pool_eng.sem_inc(all_sent, 1)
            pool_eng.wait_ge(rows_done, (B - 1) * TT + 1)
            pool_eng.sem_inc(dispatching, 1)
            dispatch(0, last_sent)

        @block.tensor
        def _(pe):
            pe.wait_ge(const_in, 16 * 4)
            pe.wait_ge(ones_set, 3)
            pe.wait_ge(below_set, 1)

            def turn(src, bank, done, ready=None, at=0):
                for t in range(TT):
                    if ready is not None:
                        pe.wait_ge(ready, at + (t + 1))
                    for c in range(DC):
                        last = nc.tensor.transpose(ps[:, bank + c, t * P:(t + 1) * P],
                                                   src[:, t, c * P:(c + 1) * P], ident)
                last.then_inc(done, 1)

            def turn_heads(b):
                pe.wait_ge(o_in, b * 16 + 16)
                turn(O, 0, o_turned)

            def project_heads(b):
                pe.wait_ge(ot_done, b + 1)
                pe.wait_ge(x_in, b * 16 + 16)
                h = two(2)
                for t in range(TT):
                    nc.tensor.matmul(h[:, t], ident, X[:, t], start=True, stop=False)
                    for c in range(DC):
                        last = nc.tensor.matmul(h[:, t], OT[:, c, t * P:(t + 1) * P], Wo[:, c],
                                                start=False, stop=c == DC - 1)
                    last.then_inc(projected, 1)

            def turn_x1(b):
                turn(X1, 0, x1_turned, normed, b * TT)

            def rank(m_done):
                pe.wait_ge(mask_done, m_done)
                pe.wait_ge(shared_added, m_done)
                before, upto = two(0), two(2)
                for t in range(TT):
                    for s in range(t):
                        nc.tensor.matmul(before[:, t, 0:EXPERTS], ones[:], mask[:, s], start=s == 0, stop=False)
                        nc.tensor.matmul(upto[:, t, 0:EXPERTS], ones[:], mask[:, s], start=s == 0, stop=False)
                    nc.tensor.matmul(before[:, t, 0:EXPERTS], below[:], mask[:, t], start=t == 0, stop=True)
                    last = nc.tensor.matmul(upto[:, t, 0:EXPERTS], ones[:], mask[:, t], start=t == 0, stop=True)
                last.then_inc(ranked, 1)

            def share(m_done):
                pe.wait_ge(shared_silu, m_done)
                out = two(0)
                for t in range(TT):
                    last = nc.tensor.matmul(out[:, t], GS[:, t * P:(t + 1) * P], Ws[:, DC * INTER:], start=True, stop=True)
                last.then_inc(shared_made, 1)

            def start(b):
                turn_heads(b)
                project_heads(b)
                turn_x1(b)

            def step(n, part_b, part_c, part_a):
                tile = lambda t: n * TT + (t + 1)
                if not part_b:
                    share(n)
                    rank(n)
                    return
                pe.wait_ge(x1t_done, n + 1)
                pe.wait_ge(ct_in, n * 16 + 16)
                if part_c:
                    pe.wait_ge(lg_done, n)

                def similarity(i):
                    if i >= 2:
                        pe.wait_ge(row_expd, tile(i - 2))
                    for c in range(DC):
                        last = nc.tensor.matmul(ps[:, 4 + i % 2], ET[:, c, i * P:(i + 1) * P], CT[:, c],
                                                start=c == 0, stop=c == DC - 1)
                    last.then_inc(similar, 1)

                def turn_row(i):
                    pe.wait_ge(row_scaled, tile(i))
                    if i >= 2:
                        pe.wait_ge(at_done, tile(i - 2))
                    for j in range(TT):
                        last = nc.tensor.transpose(ps[:, 6 + i % 2, j * P:(j + 1) * P],
                                                   A[:, i, j * P:(j + 1) * P], ident)
                    last.then_inc(row_turned, 1)

                similarity(0)
                similarity(1)
                if part_c:
                    share(n)
                for i in range(2, TT):
                    similarity(i)
                    turn_row(i - 2)
                if part_c:
                    rank(n)
                pe.wait_ge(um_done, n + 1)
                pe.wait_ge(row_expd, tile(2))
                nc.tensor.transpose(ps[0:1, 4, 0:P], um[:], ident).then_inc(um_turned, 1)
                turn_row(TT - 2)
                pe.wait_ge(g_done, n + 1)
                nc.tensor.matmul(ps[:, 4, P:P + 1], ones32[0:1, :], g[:], start=True, stop=True).then_inc(g_spread, 1)
                turn_row(TT - 1)

                def attended(c):
                    for j in range(TT):
                        last = nc.tensor.matmul(ps[:, c], CR[:, j, c * P:(c + 1) * P], AT[:, j],
                                                start=j == 0, stop=j == TT - 1)
                    last.then_inc(hq_made, 1)

                pe.wait_ge(at_done, tile(TT - 1))
                pe.wait_ge(cr_in, n * 16 + 16)
                if part_c:
                    pe.wait_ge(ranks_read, n)
                attended(0)
                pe.wait_ge(eb_done, n + 1)
                nc.tensor.matmul(ps[:, 4, 2 * P:2 * P + TT], ones32[:], eb[:], start=True, stop=True)
                for c in range(DC):
                    for t in range(TT):
                        last = nc.tensor.matmul(ps[:, 5, c:c + 1], X1[:, t, c * P:(c + 1) * P], eb[:, t:t + 1],
                                                start=t == 0, stop=t == TT - 1)
                last.then_inc(hc_summed, 1)
                attended(1)
                pe.wait_ge(weights_in, 16 * 3)
                pe.wait_ge(w1_done, n + 1)
                parts = [(X1T, W1, 0, c) for c in range(DC)] + [(HQ, Wqv, DC, c) for c in range(DC)] + \
                    [(PR, Wqv, 2 * DC, c) for c in range(DC)]
                h = two(4)
                for t in range(TT):
                    if t == 1 and part_a:
                        turn_heads(n + 1)
                    nc.tensor.matmul(h[:, t], ident, X1b[:, t], start=True, stop=False)
                    for k, (src, W, at, c) in enumerate(parts):
                        if t == 0 and k == DC:
                            pe.wait_ge(hq_done, DC * n + DC)
                        if t == 0 and k == 2 * DC:
                            pe.wait_ge(pr_done, n + 1)
                        last = nc.tensor.matmul(h[:, t], src[:, c, t * P:(t + 1) * P], W[:, at + c],
                                                start=False, stop=k == len(parts) - 1)
                    last.then_inc(mixed, 1)
                if part_a:
                    project_heads(n + 1)
                turn(X2, 6, x2_turned, normed2, n * TT)
                pe.wait_ge(x2t_done, n + 1)
                lgs = two(4)
                for t in range(TT):
                    for c in range(DC):
                        last = nc.tensor.matmul(lgs[:, t, 0:EXPERTS], X2T[:, c, t * P:(t + 1) * P], Wr[:, c],
                                                start=c == 0, stop=c == DC - 1)
                last.then_inc(routed, 1)
                if part_a:
                    turn_x1(n + 1)
                for c in range(DC):
                    last = nc.tensor.matmul(ps[:, 6], Ws[:, c * INTER:(c + 1) * INTER], X2T[:, c],
                                            start=c == 0, stop=c == DC - 1)
                last.then_inc(shared_gated, 1)
            run(pe, start, step)

        @block.scalar
        def _(act):
            act.wait_ge(const_in, 16 * 4)
            nc.scalar.activation(below[:], C[:, COL["below"]], ACT.Copy).then_inc(below_set, 1)
            w2, w3 = Cols[:, 0:DC], Cols[:, DC:2 * DC]

            def copy_heads(b):
                act.wait_ge(o_turned, b + 1)
                for c in range(DC):
                    last = nc.scalar.activation(OT[:, c], ps[:, c], ACT.Copy)
                last.then_inc(ot_done, 1)

            def copy_x1(b):
                act.wait_ge(x1_turned, b + 1)
                for c in range(DC):
                    nc.scalar.activation(ET[:, c], ps[:, c], ACT.Identity, scale=w3[:, c:c + 1], bias=w2[:, c:c + 1])
                    last = nc.scalar.activation(X1T[:, c], ps[:, c], ACT.Copy)
                last.then_inc(x1t_done, 1)

            def start(b):
                copy_heads(b)
                act.wait_ge(measured, b + 1)
                normalize(nc, X1, two(2), y, shift, normed)
                copy_x1(b)

            def step(n, part_b, part_c, part_a):
                tile = lambda t: n * TT + (t + 1)
                if part_b:
                    def exp_row(i):
                        act.wait_ge(row_maxed, tile(i))
                        nc.scalar.activation(A[:, i], ps[:, 4 + i % 2], ACT.Exp, bias=nmax[:, i:i + 1],
                                             accum_out=rsum[:, i:i + 1]).then_inc(row_expd, 1)

                    def scale_row(i):
                        act.wait_ge(row_inverted, tile(i))
                        nc.scalar.activation(A[:, i], A[:, i], ACT.Copy, scale=rinv[:, i:i + 1]).then_inc(row_scaled, 1)

                    def copy_row(i):
                        act.wait_ge(row_turned, tile(i))
                        nc.scalar.activation(AT[:, :, i * P:(i + 1) * P],
                                             ps[:, 6 + i % 2].rearrange("p (j q) -> p j q", j=TT),
                                             ACT.Copy).then_inc(at_done, 1)

                    for i in range(TT):
                        exp_row(i)
                        if i >= 1:
                            scale_row(i - 1)
                        if i >= 2:
                            copy_row(i - 2)
                    scale_row(TT - 1)
                    copy_row(TT - 2)
                    copy_row(TT - 1)
                    act.wait_ge(ng_done, n + 1)
                    nc.scalar.activation(eb[:], u[:], ACT.Exp, bias=ng[:]).then_inc(eb_done, 1)

                def copy_rows(t):
                    if t == 0:
                        act.wait_ge(all_sent, n)
                    ins = nc.scalar.activation(rows[:, t, :, 0:D], repeated(X2[:, t], 1, TOP_K), ACT.Copy)
                    if t == TT - 1:
                        ins.then_inc(rows_copied, 1)

                if part_c:
                    if not part_b:
                        act.wait_ge(rows_done, TT * (n - 1))
                    act.wait_ge(pr_made, n)
                    nc.scalar.activation(prw[:], pr[:], ACT.Copy).then_inc(pr_copied, 1)
                    copy_rows(0)
                    copy_rows(1)
                if part_b:
                    for c in range(DC):
                        act.wait_ge(hq_made, DC * n + (c + 1))
                        nc.scalar.activation(HQ[:, c], ps[:, c], ACT.Copy).then_inc(hq_done, 1)
                if part_c:
                    copy_rows(2)
                    copy_rows(3)
                if not part_b:
                    return
                if part_a:
                    copy_heads(n + 1)
                act.wait_ge(measured2, n + 1)
                normalize(nc, X2, two(4), y[:, TT:], shift[:, TT:], normed2)
                act.wait_ge(x2_turned, n + 1)
                for c in range(DC):
                    last = nc.scalar.activation(X2T[:, c], ps[:, 6 + c], ACT.Copy)
                last.then_inc(x2t_done, 1)
                if part_a:
                    act.wait_ge(measured, n + 2)
                    normalize(nc, X1, two(2), y, shift, normed)
                act.wait_ge(lg_done, n + 1)
                nc.scalar.activation(pr[:], lg[:], ACT.Sigmoid).then_inc(pr_made, 1)
                if part_a:
                    copy_x1(n + 1)
                act.wait_ge(shared_gated, n + 1)
                nc.scalar.activation(GS[:], ps[:, 6], ACT.Sigmoid).then_inc(shared_sigmoid, 1)
            run(act, start, step)

        @block.vector
        def _(dve):
            dve.wait_ge(const_in, 16 * 4)
            dve.wait_ge(ones_set, 3)
            nc.vector.tensor_copy(slots[:], C[:, COL["slot"]].rearrange("p (t k) -> p t k", t=TT)).then_inc(state_set, 1)
            for state in (ptab[:], count[:], total[:], cur[:, 0]):
                nc.vector.memset(state, 0.0).then_inc(state_set, 1)
            nc.vector.memset(npages[:, 0], 0).then_inc(state_set, 1)
            dve.wait_ge(state_set, 6)
            w1b, bqv, ebias = Rb[:, 0:D], Rb[:, D:2 * D], Rb[:, 2 * D:]
            bsim = Cols[:, 2 * DC:2 * DC + 1]
            flat = lambda a: a.rearrange("p t e -> p (t e)")

            def measure_heads(b, o1):
                statistics(nc, o1, two(2), st, mv, v, y, shift, t4[:], lambda t: dve.wait_ge(projected, b * TT + ((t | 1) + 1)))
                dve.sem_inc(measured, 1)

            def use_x1(b, o1):
                dve.wait_ge(normed, TT * (b + 1))
                o1.do(nc.vector.tensor_tensor(X1b[:], X1[:], repeated(bqv, 1, TT), ALU.add))
                for t in range(TT):
                    o1.do(nc.vector.tensor_tensor_reduce(out=junk1[:], in0=X1[:, t], in1=w1b, scale=1.0, scalar=0.0,
                                                         op0=ALU.mult, op1=ALU.add, accum_out=dots[:, t:t + 1]))
                    o1.sync()

            def start(b):
                o1 = Order(dve, ordered1, 0, START_ORDERED)
                measure_heads(b, o1)
                use_x1(b, o1)
                o1.close()

            def step(n, part_b, part_c, part_a):
                tile = lambda t: n * TT + (t + 1)
                o1 = Order(dve, ordered1, n * ONE_ORDERED + START_ORDERED, ONE_ORDERED)
                do1, sync1 = o1.do, o1.sync
                o2 = Order(dve, ordered2, (n - 1) * TWO_ORDERED, TWO_ORDERED)
                do, sync = o2.do, o2.sync
                before, upto = two(0), two(2)

                def logits():
                    dve.wait_ge(routed, n + 1)
                    for t in range(0, TT, 2):
                        last = nc.vector.tensor_tensor(lg[:, t:t + 2], two(4)[:, t:t + 2, 0:EXPERTS],
                                                       repeated(ebias, 1, 2), ALU.add)
                    last.then_inc(lg_done, 1)

                def choose():
                    dve.wait_ge(pr_made, n)
                    dve.sem_inc(probs_seen, 1)
                    for t in range(TT):
                        do(nc.vector.max(top[:, t], pr[:, t]))
                    o2.hold()
                    for t in range(TT):
                        do(nc.vector.match_replace(rep[:, t], top[:, t], pr[:, t], -1.0))
                    do(nc.vector.tensor_reduce(tsum[:], top[:], AX, ALU.add))
                    sync()
                    nc.vector.tensor_tensor(mask[:], pr[:], rep[:], ALU.not_equal).then_inc(mask_done, 1)
                    do(nc.vector.tensor_scalar(tsum[:], tsum[:], 1e-9, None, ALU.add))
                    sync()
                    do(nc.vector.reciprocal(winv[:], tsum[:]))

                def gate_shared():
                    dve.wait_ge(shared_sigmoid, n)
                    nc.vector.tensor_tensor(GS[:], GS[:], ps[:, 6], ALU.mult).then_inc(shared_silu, 1)

                def add_shared():
                    dve.wait_ge(all_stored, n)
                    dve.wait_ge(shared_made, n)
                    for t in range(0, TT, 2):
                        last = nc.vector.tensor_tensor(XS[:, t:t + 2], two(0)[:, t:t + 2], X2[:, t:t + 2], ALU.add)
                    last.then_inc(shared_added, 1)

                def count_rows():
                    dve.wait_ge(ranked, n)
                    for t in range(0, TT, 2):
                        ts = slice(t, t + 2)
                        do(nc.vector.tensor_tensor(ri[:, ts], before[:, ts, 0:EXPERTS], repeated(count[:], 1, 2), ALU.add))
                        do(nc.vector.scalar_tensor_tensor(ni[:, ts], upto[:, ts, 0:EXPERTS], float(P - 1),
                                                          repeated(count[:], 1, 2), ALU.add, ALU.add))
                    sync()
                    do(nc.vector.tensor_tensor(count[:], upto[:, TT - 1, 0:EXPERTS], count[:], ALU.add))
                    do(nc.vector.tensor_scalar(npages[:, 1:], ni[:], 7, None, ALU.arith_shift_right))
                    sync()
                    dve.sem_inc(ranks_read, 1)

                def need_pages():
                    do(nc.vector.tensor_tensor(need[:], npages[:, 1:], npages[:, 0:TT], ALU.subtract))
                    do(nc.vector.scalar_tensor_tensor(late[:], npages[:, 0:TT], float(P), ri[:], ALU.mult, ALU.is_le))
                    do(nc.vector.tensor_scalar(ri[:], ri[:], P - 1, None, ALU.bitwise_and))
                    sync()
                    do(nc.vector.tensor_tensor_scan(flat(q[:]), ones_row[:], flat(need[:]), total[:], ALU.mult, ALU.add))
                    do(nc.vector.tensor_scalar(keep[:], need[:], -1.0, 1.0, ALU.mult, ALU.add))
                    sync()

                def new_pages():
                    do(nc.vector.tensor_scalar(total[:], flat(q[:])[:, TT * EXPERTS - 1:], 1.0, None, ALU.mult))
                    do(nc.vector.tensor_copy(npages[:, 0], npages[:, TT]))
                    sync()
                    do(nc.vector.tensor_tensor(q[:], q[:], need[:], ALU.subtract))
                    sync()
                    do(nc.vector.tensor_tensor(nq[:], q[:], need[:], ALU.mult))
                    sync()

                def current_pages():
                    for t in range(TT):
                        do(nc.vector.tensor_tensor(cur[:, t + 1], cur[:, t], keep[:, t], ALU.mult))
                        sync()
                        do(nc.vector.tensor_tensor(cur[:, t + 1], cur[:, t + 1], nq[:, t], ALU.add))
                        sync()

                def choose_pages():
                    do(nc.vector.tensor_tensor(q[:], q[:], cur[:, 0:TT], ALU.subtract))
                    do(nc.vector.tensor_tensor(nq[:], nq[:], keep[:], ALU.subtract))
                    sync()
                    do(nc.vector.tensor_tensor(q[:], q[:], late[:], ALU.mult))

                def page_experts(c):
                    do(nc.vector.scalar_tensor_tensor(junk[:], nq[:], C[:, COL["page"]][:, c:c + 1],
                                                      repeated(C[:, COL["expert"]], 1, TT), ALU.is_equal, ALU.mult,
                                                      accum_out=et[:, c:c + 1]))
                    sync()
                    if c == 2:
                        do(nc.vector.tensor_tensor(ptab[:], ptab[:], et[:], ALU.add))
                        sync()

                def keys():
                    sync()
                    do(nc.vector.tensor_tensor(q[:], q[:], cur[:, 0:TT], ALU.add))
                    sync()
                    do(nc.vector.tensor_copy(cur[:, 0], cur[:, TT]))
                    do(nc.vector.scalar_tensor_tensor(q[:], q[:], float(P), ri[:], ALU.mult, ALU.add))
                    sync()

                def places():
                    do(nc.vector.tensor_scalar(key[:], q[:], -1.0, FAR, ALU.mult, ALU.add))
                    sync()
                    do(nc.vector.tensor_tensor(key[:], key[:], mask[:], ALU.mult))
                    o2.hold()
                    for t in range(TT):
                        do(nc.vector.max(k8[:, t], key[:, t]))
                    sync()

                def weights(t):
                    if t == 0:
                        dve.wait_ge(pr_copied, n)
                    for k in range(TOP_K):
                        sync(but=TT - 1)
                        do(nc.vector.scalar_tensor_tensor(junk[:, k % TT], key[:, t], k8[:, t, k:k + 1], prw[:, t],
                                                          ALU.is_equal, ALU.mult, accum_out=w8[:, t, k:k + 1]))
                    sync()

                def tails(t):
                    if t == 0:
                        dve.wait_ge(rows_copied, n)
                    do(nc.vector.tensor_scalar(place[:, t], k8[:, t], -1.0, FAR, ALU.mult, ALU.add))
                    do(nc.vector.tensor_copy(rows[:, t, :, DST_COL].bitcast(U32), slots[:, t]))
                    do(nc.vector.tensor_scalar(rows[:, t, :, W_COL], w8[:, t], winv[:, t:t + 1], ROUTED_SCALE,
                                               ALU.mult, ALU.mult))
                    sync()
                    dve.sem_inc(rows_done, 1)

                def row_max(i):
                    dve.wait_ge(similar, tile(i))
                    nc.vector.tensor_reduce(nmax[:, i:i + 1], ps[:, 4 + i % 2], AX, ALU.max, negate=True).then_inc(row_maxed, 1)

                def invert_row(i):
                    dve.wait_ge(row_expd, tile(i))
                    nc.vector.reciprocal(rinv[:, i:i + 1], rsum[:, i:i + 1]).then_inc(row_inverted, 1)

                if part_b:
                    row_max(0)
                if part_c:
                    gate_shared()
                if part_b:
                    row_max(1)
                    invert_row(0)
                if part_c:
                    choose()
                if part_b:
                    row_max(2)
                    invert_row(1)
                if part_c:
                    add_shared()
                if part_b:
                    row_max(3)
                    invert_row(2)
                    dve.wait_ge(row_maxed, tile(TT - 1))
                    do1(nc.vector.scalar_tensor_tensor(u[:], nmax[:], -1.0, dots[:], ALU.mult, ALU.add))
                    sync1()
                    do1(nc.vector.tensor_scalar(u[:], u[:], bsim, None, ALU.add))
                    sync1()
                    nc.vector.tensor_reduce(um[:], u[:], AX, ALU.max).then_inc(um_done, 1)
                    invert_row(3)
                if part_b:
                    dve.wait_ge(um_turned, n + 1)
                    nc.vector.tensor_reduce(g[:], ps[0:1, 4, 0:P], AX, ALU.max).then_inc(g_done, 1)
                if part_c:
                    count_rows()
                if part_b:
                    dve.wait_ge(g_spread, n + 1)
                    nc.vector.tensor_scalar(ng[:], ps[:, 4, P:P + 1], -1.0, None, ALU.mult).then_inc(ng_done, 1)
                if part_c:
                    need_pages()
                    new_pages()
                    current_pages()
                if part_b:
                    dve.wait_ge(hc_summed, n + 1)
                    do1(nc.vector.tensor_reduce(esum[:], ps[:, 4, 2 * P:2 * P + TT], AX, ALU.add))
                    sync1()
                    do1(nc.vector.reciprocal(einv[:], esum[:]))
                    sync1()
                    do1(nc.vector.tensor_scalar(hc[:], ps[:, 5, 0:DC], einv[:], None, ALU.mult))
                    sync1()
                    dve.wait_ge(weights_in, 16 * 3)
                    for c in range(DC):
                        last = nc.vector.scalar_tensor_tensor(W1[:, c], Wqv[:, 3 * DC + c], hc[:, c:c + 1], Wqv[:, c],
                                                              ALU.mult, ALU.add)
                    last.then_inc(w1_done, 1)
                if part_c:
                    choose_pages()
                if part_b:
                    for c in range(DC):
                        dve.wait_ge(hq_done, DC * n + (c + 1))
                        last = nc.vector.tensor_tensor(PR[:, c], HQ[:, c], X1T[:, c], ALU.mult)
                    last.then_inc(pr_done, 1)
                if part_c:
                    keys()
                    places()
                    for t in range(TT - 1):
                        weights(t)
                        tails(t)
                        page_experts(t)
                if part_b:
                    statistics(nc, o1, two(4), st, mv, v, y[:, TT:], shift[:, TT:], t4[:],
                               lambda t: dve.wait_ge(mixed, tile(t | 1)))
                    dve.sem_inc(measured2, 1)
                if part_a:
                    measure_heads(n + 1, o1)
                if part_b:
                    logits()
                if part_c:
                    weights(TT - 1)
                    tails(TT - 1)
                    do(nc.vector.tensor_scalar(slots[:], slots[:], float(S * TOP_K), None, ALU.add))
                    sync()
                    o2.close()
                if part_a:
                    use_x1(n + 1, o1)
                    o1.close()
            run(dve, start, step)
            nc.vector.tensor_copy(ptab_i[:, 0:3], ptab[:]).then_inc(table_done, 1)
            nc.vector.tensor_scalar(last_page[:], total[:], -1.0, None, ALU.add).then_inc(table_done, 1)
            dve.wait_ge(table_done, 2)
            nc.vector.tensor_scalar(ptab_i[:, 3:4], last_page[:], ROUND.bit_length() - 1, None,
                                    ALU.arith_shift_right).then_inc(table_done, 1)


def experts(nc, tokens, dispatch, last_sent, w, pages_d, pool, contrib):
    RING, XG = ROUND, 4
    with ExitStack() as ctx:
        sb = lambda n, s, d=F32: ctx.enter_context(nc.sbuf_tensor(n, s, d))
        sem = lambda n: ctx.enter_context(nc.semaphore(n))
        table, ident, ident_in = sb("e_table", [1, 4 * P], I32), tokens.ident, tokens.ident_in
        W, X, Y = sb("e_w", [P, RING, DC * INTER + D]), sb("e_x", [P, RING, ROW]), sb("e_y", [P, RING, D])
        tail = sb("e_tail", [P, RING, 2])
        XT, G = sb("e_xt", [P, 2, DC, P]), sb("e_g", [P, 2, P])
        psX, psG, psY = (ctx.enter_context(nc.psum_tensor(f"e_ps{n}", [P, 2, S], F32)) for n in "xgy")
        table_in = sem("e_table_in")
        w_in = [sem(f"e_w_in{r}") for r in range(RING)]
        x_in = [sem(f"e_x_in{r}") for r in range(RING // XG)]
        sent = [sem(f"e_sent{r}") for r in range(RING)]
        tail_done, turned, xt_done, gated, silu_done, downed, y_done = (
            sem(f"e_{n}") for n in ("tail_done", "turned", "xt_done", "gated", "silu_done", "downed", "y_done"))
        sending, w_loading, x_loading = sem("e_sending"), sem("e_w_loading"), sem("e_x_loading")

        def run(eng, step, drain):
            eng.wait_ge(table_in, 16)
            more = eng.value_load(table[0:1, MORE_AT:MORE_AT + 1], min_val=0, max_val=POOL_PAGES // ROUND - 1)
            for k in range(RING):
                step(At(0, k, RING))
            with eng.Fori(0, POOL_PAGES // ROUND - 1) as i:
                with eng.If(i < more):
                    for k in range(RING, 2 * RING):
                        step(At(i, k, RING))
            for k in range(RING, RING + drain):
                step(Past(more, k, RING))
            return more
        block = ctx.enter_context(nc.Block())

        @block.sync
        def _(sp):
            sp.dma_start(table[:], pages_d.rearrange("(a c) p -> a (c p)", a=1)).then_inc(table_in, 16)
            sp.dma_start(ident[:], tokens.ident_d).then_inc(ident_in, 16)

            def load_rows(at):
                sp.dma_start(X[:, at.slot:at.slot + XG],
                             pool[bass.ds(at.n * P, XG * P)].rearrange("(k p) r -> p k r", p=P)
                             ).then_inc(x_in[at.slot // XG], 16)

            def step(at):
                if at.k % XG == 0 and not at.first(RING):
                    sp.wait_ge(turned, at.n - (RING - XG))
                    sp.sem_inc(x_loading, 1)
                    sp.wait_ge(tail_done, at.group(XG) - (RING // XG - 1))
                    sp.sem_inc(x_loading, 1)
                    load_rows(at)
                if not at.first(RING):
                    sp.wait_ge(downed, at.n - (RING - 1))
                    sp.sem_inc(w_loading, 1)
                e = sp.value_load(table[0:1, bass.ds(at.n, 1)], min_val=0, max_val=EXPERTS - 1)
                sp.dma_start(W[:, at.slot], w[bass.ds(e, 1)].rearrange("a p n -> (a p) n")).then_inc(w_in[at.slot], 16)
                if at.fixed and at.n == RING - 1:
                    sp.wait_ge(last_sent, 16 * TT * TOP_K)
                    for n in range(0, RING, XG):
                        load_rows(At(0, n, RING))
            run(sp, step, 0)
            tokens.load(sp)

        @block.tensor
        def _(pe):
            pe.wait_ge(ident_in, 16)

            def step(at):
                if at.within(POOL_PAGES):
                    if at.k % XG == 0:
                        pe.wait_ge(x_in[at.slot // XG], 16 * at.uses())
                    if not at.first(2):
                        pe.wait_ge(xt_done, at.n - 1)
                    for c in range(DC):
                        last = nc.tensor.transpose(psX[:, at.k % 2, c * P:(c + 1) * P],
                                                   X[:, at.slot, c * P:(c + 1) * P], ident[:])
                    last.then_inc(turned, 1)
                f = at.back(1)
                if f.within(POOL_PAGES):
                    pe.wait_ge(w_in[f.slot], 16 * f.uses())
                    pe.wait_ge(xt_done, at.n)
                    if not f.first(2):
                        pe.wait_ge(silu_done, at.n - 2)
                    for c in range(DC):
                        last = nc.tensor.matmul(psG[:, f.k % 2, 0:P], W[:, f.slot, c * INTER:(c + 1) * INTER],
                                                XT[:, f.k % 2, c], start=c == 0, stop=c == DC - 1)
                    last.then_inc(gated, 1)
                f = at.back(2)
                if f.within(POOL_PAGES):
                    pe.wait_ge(silu_done, at.n - 1)
                    if not f.first(2):
                        pe.wait_ge(y_done, at.n - 3)
                    nc.tensor.matmul(psY[:, f.k % 2, 0:D], G[:, f.k % 2], W[:, f.slot, DC * INTER:],
                                     start=True, stop=True).then_inc(downed, 1)
            run(pe, step, 2)

        @block.vector
        def _(dve):
            def step(at):
                if at.k % XG == 0:
                    slots = slice(at.slot, at.slot + XG)
                    dve.wait_ge(x_in[at.slot // XG], 16 * at.uses())
                    if not at.first(RING):
                        for r in range(at.slot, at.slot + XG):
                            dve.wait_ge(sent[r], 16 * (at.uses() - 1))
                    nc.vector.tensor_copy(tail[:, slots], X[:, slots, W_COL:W_COL + 2]).then_inc(tail_done, 1)
                dve.wait_ge(turned, at.n + 1)
                if not at.first(2):
                    dve.wait_ge(gated, at.n - 1)
                nc.vector.tensor_copy(XT[:, at.k % 2], psX[:, at.k % 2, 0:D].rearrange("p (c q) -> p c q", c=DC)
                                      ).then_inc(xt_done, 1)
            run(dve, step, 0)

        @block.scalar
        def _(act):
            def step(at):
                f = at.back(1)
                if f.within(POOL_PAGES):
                    act.wait_ge(gated, at.n)
                    if not f.first(2):
                        act.wait_ge(downed, at.n - 2)
                    nc.scalar.activation(G[:, f.k % 2], psG[:, f.k % 2, 0:P], ACT.Silu).then_inc(silu_done, 1)
                f = at.back(2)
                if f.within(POOL_PAGES):
                    act.wait_ge(downed, at.n - 1)
                    if f.k % XG == 0:
                        act.wait_ge(tail_done, f.group(XG) + 1)
                    if not f.first(RING):
                        act.wait_ge(sent[f.slot], 16 * (f.uses() - 1))
                    nc.scalar.activation(Y[:, f.slot], psY[:, f.k % 2, 0:D], ACT.Copy,
                                         scale=tail[:, f.slot, 0:1]).then_inc(y_done, 1)
            run(act, step, 2)

        @block.gpsimd
        def _(pool_eng):
            def step(at):
                f = at.back(2)
                if f.within(POOL_PAGES):
                    if f.k % XG == 0:
                        pool_eng.wait_ge(tail_done, f.group(XG) + 1)
                    pool_eng.wait_ge(y_done, at.n - 1)
                    pool_eng.sem_inc(sending, 1)
                    nc.gpsimd.indirect_dma_start(
                        out=contrib, out_offset=bass.IndirectOffsetOnAxis(
                            ap=tail[:, f.slot, 1:2].bitcast(U32), axis=0),
                        in_=Y[:, f.slot], in_offset=None, bounds_check=TOKENS * TOP_K - 1,
                        oob_is_err=False).then_inc(sent[f.slot], 16)
            for t in range(1, TT):
                dispatch(t, last_sent)
            more = run(pool_eng, step, 2)
            for r in range(RING):
                pool_eng.wait_ge(sent[r], more * 16 + 16)


class Tokens:

    def __init__(self, nc, ctx, ident_d, x2d):
        self.ident = ctx.enter_context(nc.sbuf_tensor("c_ident", [P, P], F32))
        self.X = ctx.enter_context(nc.sbuf_tensor("c_x", [P, B, TT, D], F32))
        self.ident_in = ctx.enter_context(nc.semaphore("c_ident_in"))
        self.x_in = [ctx.enter_context(nc.semaphore(f"c_x_in{b}")) for b in range(B)]
        self.ident_d, self.x2d = ident_d, x2d

    def load(self, sp):
        for b in range(B):
            sp.dma_start(self.X[:, b], self.x2d[b]).then_inc(self.x_in[b], 16)


def combine(nc, tokens, contrib, out):
    RING = 2
    with ExitStack() as ctx:
        sb = lambda n, s, d=F32: ctx.enter_context(nc.sbuf_tensor(n, s, d))
        sem = lambda n: ctx.enter_context(nc.semaphore(n))
        Cn = sb("c_c", [P, RING, TT, TOP_K, D])
        X, ident, ident_in, x_in = tokens.X, tokens.ident, tokens.ident_in, tokens.x_in
        H, Y = sb("c_h", [P, RING, TT, D]), sb("c_y", [P, RING, TT, D])
        st, mv, v = sb("c_st", [P, TT, 6]), sb("c_mv", [P, TT, 2]), sb("c_v", [P, 2, TT])
        y, shift, t4 = sb("c_rstd", [P, RING, TT]), sb("c_shift", [P, RING, TT]), sb("c_t4", [P, TT])
        ps = ctx.enter_context(nc.psum_tensor("c_ps", [P, RING * TT, S], F32))
        summed = sem("c_summed")
        c_in = [sem(f"c_c_in{r}") for r in range(RING * TT)]
        stored = [sem(f"c_stored{r}") for r in range(RING)]
        ordered, reduced, added, measured, normed = (sem(f"c_{n}") for n in ("ordered", "reduced", "added", "measured", "normed"))
        block = ctx.enter_context(nc.Block())

        @block.sync
        def _(sp):
            for b in range(B):
                r = b % RING
                for t in range(TT):
                    if b >= RING:
                        sp.wait_ge(reduced, (b - RING) * TT + t + 1)
                        sp.wait_ge(summed, (b - RING) * TT + t + 1)
                    at = (b * TT + t) * P * TOP_K
                    sp.dma_start(Cn[:, r, t], contrib[at:at + P * TOP_K].rearrange("(p k) d -> p k d", k=TOP_K)
                                 ).then_inc(c_in[r * TT + t], 16)

        @block.tensor
        def _(pe):
            pe.wait_ge(ident_in, 16)
            for b in range(B):
                r = b % RING
                pe.wait_ge(x_in[b], 16)
                for t in range(TT):
                    if b >= RING:
                        pe.wait_ge(added, (b - RING) * TT + t + 1)
                    bank = ps[:, r * TT + t, 0:D]
                    nc.tensor.matmul(bank, ident[:], X[:, b, t], start=True, stop=False)
                    pe.wait_ge(c_in[r * TT + t], 16 * (b // RING + 1))
                    for k in range(TOP_K // 2):
                        last = nc.tensor.matmul(bank, ident[:], Cn[:, r, t, k], start=False, stop=k == TOP_K // 2 - 1)
                    last.then_inc(summed, 1)

        @block.scalar
        def _(act):
            for b in range(B):
                r = b % RING
                act.wait_ge(measured, b + 1)
                if b >= RING:
                    act.wait_ge(stored[r], 16 * (b // RING))
                normalize(nc, Y[:, r], H[:, r], y[:, r], shift[:, r], normed)
                act.wait_ge(normed, TT * (b + 1))
                act.dma_start(out[b].rearrange("(t p) d -> p t d", p=P), Y[:, r]).then_inc(stored[r], 16)
            for r in range(RING):
                act.wait_ge(stored[r], 16 * (B // RING))

        @block.vector
        def _(dve):
            for b in range(B):
                r = b % RING
                o = Order(dve, ordered, b * LN_ORDERED, LN_ORDERED)
                if b >= RING:
                    dve.wait_ge(normed, TT * (b - RING + 1))
                for t in range(TT):
                    dve.wait_ge(c_in[r * TT + t], 16 * (b // RING + 1))
                    nc.vector.tensor_reduce(H[:, r, t], Cn[:, r, t, TOP_K // 2:].rearrange("p k d -> p d k"), AX,
                                            ALU.add).then_inc(reduced, 1)
                    dve.wait_ge(summed, b * TT + t + 1)
                    dve.wait_ge(reduced, b * TT + t + 1)
                    nc.vector.tensor_tensor(H[:, r, t], H[:, r, t], ps[:, r * TT + t, 0:D], ALU.add).then_inc(added, 1)
                statistics(nc, o, H[:, r], st, mv, v, y[:, r], shift[:, r], t4[:],
                           lambda t: dve.wait_ge(added, TT * b + t + 1))
                dve.sem_inc(measured, 1)
                o.close()


def decoder_layer(nc, xt, x, ctx_t, ctx_r, wq, wk, wv, wo, wqv, wr, cols, rowsb, w, kaux, consts, out):
    dram = lambda n, s, d=F32: nc.dram_tensor(n, s, d, kind="Internal").ap()
    qd, kd = (dram(n, [STEPS, 2, DH, HG, S]) for n in ("q_parts", "k_parts"))
    vd, od = dram("v_heads", [STEPS, P, TT, HG * 2 * DH]), dram("o_heads", [B, P, TT, D])
    pool = dram("row_pool", [POOL_PAGES * P, ROW])
    x2d, contrib = dram("tokens", [B, P, TT, D]), dram("contributions", [TOKENS * TOP_K, D])
    pages_d = dram("page_table", [4, P], I32)
    with ExitStack() as ctx:
        fill = ctx.enter_context(nc.sbuf_tensor("fill", [P, ROW], F32))
        pool_filled = ctx.enter_context(nc.semaphore("pool_filled"))
        inputs = MixInputs(nc, ctx, consts, wo, wqv, wr, w, cols, rowsb, x, ctx_t, ctx_r)
        with ExitStack() as heads:
            Q, K = (heads.enter_context(nc.sbuf_tensor(n, [P, RING, HG, S], F32R)) for n in ("a_q", "a_k"))
            zero = heads.enter_context(nc.sbuf_tensor("a_zero", [HG, HG, S], F32))
            project(nc, xt, wq, wk, wv, kaux, Q, K, zero, fill, qd, kd, vd)
            attend(nc, consts[:, COL["ident"]], Q, K, zero, qd, kd, vd, od, fill, pool, pool_filled, inputs.load)
        rows = ctx.enter_context(nc.sbuf_tensor("rows", [P, TT, TOP_K, ROW], F32))
        last_sent = ctx.enter_context(nc.semaphore("last_sent"))
        place = ctx.enter_context(nc.sbuf_tensor("places", [P, TT, TOP_K], U32))

        def dispatch(t, sent):
            for k in range(TOP_K):
                nc.gpsimd.indirect_dma_start(
                    out=pool, out_offset=bass.IndirectOffsetOnAxis(ap=place[:, t, k:k + 1], axis=0),
                    in_=rows[:, t, k], in_offset=None, bounds_check=POOL_PAGES * P - 1,
                    oob_is_err=False).then_inc(sent, 16)

        mix(nc, inputs, x, ctx_t, ctx_r, od, rows, place, dispatch, last_sent, pool_filled, x2d, pages_d)
        tokens = Tokens(nc, ctx, consts[:, COL["ident"]], x2d)
        experts(nc, tokens, dispatch, last_sent, w, pages_d, pool, contrib)
        combine(nc, tokens, contrib, out)


def constants(np):
    kaux = np.zeros((32, HG, S), np.float32)
    for h in range(HG):
        kaux[h, h] = 1
    c = np.zeros((P, N_CONST), np.float32)
    p = np.arange(P)
    c[:, COL["ident"]] = np.eye(P)
    c[:, COL["below"]] = np.triu(np.ones((P, P)), 1)
    c[:, COL["expert"]] = np.arange(EXPERTS)
    page = p[:, None] + P * np.arange(3)
    c[:, COL["page"]] = page
    t, k = np.arange(TT), np.arange(TOP_K)
    c[:, COL["slot"]] = ((p[:, None, None] + P * t[:, None]) * TOP_K + k).reshape(P, -1)
    return {"kaux": kaux, "consts": c}


def kernel(**inputs):
    import numpy as np
    import concourse.bacc as bacc
    from concourse.bass_utils import run_bass_kernel_spmd

    I = {k: np.asarray(v) for k, v in inputs.items()}
    turned = lambda a: a.reshape(B, S, DC, P).transpose(0, 3, 2, 1)
    tiled = lambda a: a.reshape(B, TT, P, D).transpose(0, 2, 1, 3)
    chunked = lambda a: a.reshape(-1, P, a.shape[-1]).transpose(1, 0, 2)
    by_step = lambda a: chunked(a.T.reshape(D, DC, 2, HG, DH).transpose(0, 1, 2, 4, 3).reshape(D, D))
    g = lambda n: I["L0_" + n]
    w_sim = g("xattn_w_sim")
    same = lambda a: np.broadcast_to(a, (P, a.size))
    gate = np.concatenate([g("ffn_w_gate"), g("ffn_w_gate_shared")[None]])
    down = np.concatenate([g("ffn_w_down"), g("ffn_w_down_shared")[None]])
    arrays = {
        "xt": turned(I["x"]), "x": tiled(I["x"]),
        "ctx_t": turned(I["ctx_1024"]), "ctx_r": tiled(I["ctx_1024"]),
        "wq": by_step(g("attn_w_q")), "wk": by_step(g("attn_w_k")), "wv": chunked(g("attn_w_v").T),
        "wo": chunked(g("attn_w_o").T), "wqv": chunked(g("xattn_W_qv")),
        "wr": chunked(g("ffn_router_w").T),
        "cols": np.concatenate([w_sim[D:2 * D].reshape(DC, P).T, w_sim[2 * D:].reshape(DC, P).T,
                                np.broadcast_to(g("xattn_b_sim"), (P, 1))], axis=1),
        "rowsb": np.concatenate([same(w_sim[:D]), same(g("xattn_b_qv")), same(g("ffn_expert_bias"))], axis=1),
        "w": np.concatenate([gate.reshape(-1, INTER, DC, P).transpose(0, 3, 2, 1).reshape(-1, P, DC * INTER),
                             down.transpose(0, 2, 1)], axis=2),
        **constants(np),
    }
    arrays = {k: np.ascontiguousarray(v) for k, v in arrays.items()}
    nc = bacc.Bacc("TRN2", target_bir_lowering=False, num_devices=1)
    args = [nc.dram_tensor(k, v.shape, mybir.dt.from_np(v.dtype), kind="ExternalInput").ap() for k, v in arrays.items()]
    out = nc.dram_tensor("out", (B, S, D), F32, kind="ExternalOutput").ap()
    decoder_layer(nc, *args, out)
    return run_bass_kernel_spmd(nc, [arrays], core_ids=[0]).results[0]["out"]
```
